# Optimizing a Trainium2 kernel written in Bass

```python
import numpy as np
import jax
import jax.numpy as jnp

def _softmax(x, axis=-1):
    return jax.nn.softmax(x, axis=axis)

def _gelu(x):
    return jax.nn.gelu(x, approximate=True)

def _silu(x):
    return jax.nn.silu(x)

def _sigmoid(x):
    return jax.nn.sigmoid(x)

def _layernorm(x, axis=-1, eps=1e-05):
    m = jnp.mean(x, axis=axis, keepdims=True)
    v = jnp.var(x, axis=axis, keepdims=True)
    return (x - m) / jnp.sqrt(v + eps)

def _scatter_add(tgt, idx, src, axis=0):
    return tgt.at[idx].add(src)

def _segment_sum(src, seg, n):
    return jax.ops.segment_sum(src, seg, n)
kernel_name = 'mk_seq_postln_d1_jaxref_r4_817bd3'

def setup_inputs(seed: int=0):
    np.random.seed(seed)
    _w = jnp.asarray

    def _L0_attn_setup():
        import jax, jax.numpy as jnp
        import numpy as np
        from jax import lax
        D_MODEL = 256
        D_STATE = 16
        D_CONV = 4
        EXPAND = 2
        D_INNER = D_MODEL * EXPAND
        DT_RANK = 64
        BATCH = 2
        SEQ = 1024
        DT_MIN, DT_MAX = (0.001, 0.1)
        key = jax.random.key(seed)
        ks = jax.random.split(key, 12)
        xavier = lambda k, shape: jax.random.normal(k, shape, jnp.float32) * np.float32(np.sqrt(2.0 / (shape[0] + shape[1])))
        x = jax.random.normal(ks[0], (BATCH, SEQ, D_MODEL), jnp.float32)
        in_proj_w = xavier(ks[1], (2 * D_INNER, D_MODEL))
        in_proj_b = jnp.zeros((2 * D_INNER,), jnp.float32)
        conv_w = jax.random.normal(ks[2], (D_INNER, D_CONV), jnp.float32) * 0.02
        conv_b = jnp.zeros((D_INNER,), jnp.float32)
        A_log = jnp.log(jnp.tile(jnp.arange(1, D_STATE + 1, dtype=jnp.float32)[:, None], (1, D_INNER)))
        D = jnp.ones((D_INNER,), jnp.float32)
        x_proj_w = xavier(ks[3], (DT_RANK + 2 * D_STATE, D_INNER))
        dt_proj_w = jax.random.normal(ks[4], (D_INNER, DT_RANK), jnp.float32) * np.float32(DT_RANK ** (-0.5))
        dt = jnp.exp(jax.random.uniform(ks[5], (D_INNER,), jnp.float32) * np.float32(np.log(DT_MAX) - np.log(DT_MIN)) + np.float32(np.log(DT_MIN)))
        dt_proj_b = dt + jnp.log(-jnp.expm1(-dt))
        out_proj_w = xavier(ks[6], (D_MODEL, D_INNER))
        out_proj_b = jnp.zeros((D_MODEL,), jnp.float32)
        return {'x': x, 'in_proj_w': in_proj_w, 'in_proj_b': in_proj_b, 'conv_w': conv_w, 'conv_b': conv_b, 'A_log': A_log, 'D': D, 'x_proj_w': x_proj_w, 'dt_proj_w': dt_proj_w, 'dt_proj_b': dt_proj_b, 'out_proj_w': out_proj_w, 'out_proj_b': out_proj_b}
    _L0_attn_in = _L0_attn_setup()

    def _L0_ffn_setup():
        import jax, jax.numpy as jnp
        import numpy as np
        B, S, D = (2, 512, 256)
        I = 128
        E = 16
        TOP_K = 2

        def _mlp(x, wg, wu, wd):
            return jnp.einsum('bsi,id->bsd', jax.nn.silu(x @ wg) * (x @ wu), wd)
        key = jax.random.key(seed)
        ks = jax.random.split(key, 10)
        sc_d = 1.0 / np.sqrt(D)
        sc_i = 1.0 / np.sqrt(I)
        return {'x': jax.random.normal(ks[0], (B, S, D), dtype=jnp.float32), 'gate_w': jax.random.normal(ks[1], (D, E), dtype=jnp.float32) * sc_d, 'gate_b': jnp.zeros((E,), dtype=jnp.float32), 'shared_wg': jax.random.normal(ks[2], (D, I), dtype=jnp.float32) * sc_d, 'shared_wu': jax.random.normal(ks[3], (D, I), dtype=jnp.float32) * sc_d, 'shared_wd': jax.random.normal(ks[4], (I, D), dtype=jnp.float32) * sc_i, 'experts_wg': jax.random.normal(ks[5], (E, D, I), dtype=jnp.float32) * sc_d, 'experts_wu': jax.random.normal(ks[6], (E, D, I), dtype=jnp.float32) * sc_d, 'experts_wd': jax.random.normal(ks[7], (E, I, D), dtype=jnp.float32) * sc_i}
    _L0_ffn_in = _L0_ffn_setup()
    _d = {'L0_attn_x': _L0_attn_in['x'], 'L0_attn_in_proj_w': _L0_attn_in['in_proj_w'], 'L0_attn_in_proj_b': _L0_attn_in['in_proj_b'], 'L0_attn_conv_w': _L0_attn_in['conv_w'], 'L0_attn_conv_b': _L0_attn_in['conv_b'], 'L0_attn_A_log': _L0_attn_in['A_log'], 'L0_attn_D': _L0_attn_in['D'], 'L0_attn_x_proj_w': _L0_attn_in['x_proj_w'], 'L0_attn_dt_proj_w': _L0_attn_in['dt_proj_w'], 'L0_attn_dt_proj_b': _L0_attn_in['dt_proj_b'], 'L0_attn_out_proj_w': _L0_attn_in['out_proj_w'], 'L0_attn_out_proj_b': _L0_attn_in['out_proj_b'], 'L0_ffn_gate_w': _L0_ffn_in['gate_w'], 'L0_ffn_gate_b': _L0_ffn_in['gate_b'], 'L0_ffn_shared_wg': _L0_ffn_in['shared_wg'], 'L0_ffn_shared_wu': _L0_ffn_in['shared_wu'], 'L0_ffn_shared_wd': _L0_ffn_in['shared_wd'], 'L0_ffn_experts_wg': _L0_ffn_in['experts_wg'], 'L0_ffn_experts_wu': _L0_ffn_in['experts_wu'], 'L0_ffn_experts_wd': _L0_ffn_in['experts_wd']}
    _x0 = _d['L0_attn_x']
    _d['L0_attn_x'] = jax.random.normal(jax.random.fold_in(jax.random.key(seed), 1), (4, 2048, 256), dtype=_x0.dtype)
    del _x0
    return _d

def reference(L0_attn_x, L0_attn_in_proj_w, L0_attn_in_proj_b, L0_attn_conv_w, L0_attn_conv_b, L0_attn_A_log, L0_attn_D, L0_attn_x_proj_w, L0_attn_dt_proj_w, L0_attn_dt_proj_b, L0_attn_out_proj_w, L0_attn_out_proj_b, L0_ffn_gate_w, L0_ffn_gate_b, L0_ffn_shared_wg, L0_ffn_shared_wu, L0_ffn_shared_wd, L0_ffn_experts_wg, L0_ffn_experts_wu, L0_ffn_experts_wd):

    def _L0_attn_ref(x, in_proj_w, in_proj_b, conv_w, conv_b, A_log, D, x_proj_w, dt_proj_w, dt_proj_b, out_proj_w, out_proj_b):
        import jax, jax.numpy as jnp
        import numpy as np
        from jax import lax
        D_MODEL = 256
        D_STATE = 16
        D_CONV = 4
        EXPAND = 2
        D_INNER = D_MODEL * EXPAND
        DT_RANK = 64
        BATCH = 2
        SEQ = 1024
        DT_MIN, DT_MAX = (0.001, 0.1)
        b, L, _ = x.shape
        xz = x @ in_proj_w.T + in_proj_b
        x_in, z = jnp.split(xz, 2, axis=-1)
        x_pad = jnp.pad(x_in, ((0, 0), (D_CONV - 1, 0), (0, 0)))
        x_conv = conv_b
        x_conv = sum((x_pad[:, k:k + L, :] * conv_w[None, None, :, k] for k in range(D_CONV))) + conv_b
        x_conv = jax.nn.silu(x_conv)
        x_dbl = x_conv @ x_proj_w.T
        dt_low = x_dbl[..., :DT_RANK]
        Bm = x_dbl[..., DT_RANK:DT_RANK + D_STATE]
        Cm = x_dbl[..., DT_RANK + D_STATE:]
        dt = jax.nn.softplus(dt_low @ dt_proj_w.T + dt_proj_b)
        A = -jnp.exp(A_log).T
        safe_A = jnp.where(jnp.abs(A) < 1e-06, jnp.ones_like(A), A)

        def step(h, inp):
            xt, dtt, Bt, Ct = inp
            A_bar = jnp.exp(dtt[..., None] * A)
            B_bar = (A_bar - 1.0) / safe_A * Bt[:, None, :]
            h = A_bar * h + B_bar * xt[..., None]
            y = jnp.einsum('bds,bs->bd', h, Ct) + D * xt
            return (h, y)
        xs = (jnp.swapaxes(x_conv, 0, 1), jnp.swapaxes(dt, 0, 1), jnp.swapaxes(Bm, 0, 1), jnp.swapaxes(Cm, 0, 1))
        h0 = jnp.zeros((b, D_INNER, D_STATE), x.dtype)
        _, ys = lax.scan(step, h0, xs)
        y = jnp.swapaxes(ys, 0, 1) * jax.nn.silu(z)
        return y @ out_proj_w.T + out_proj_b

    def _L0_ffn_ref(x, gate_w, gate_b, shared_wg, shared_wu, shared_wd, experts_wg, experts_wu, experts_wd):
        import jax, jax.numpy as jnp
        import numpy as np
        B, S, D = (2, 512, 256)
        I = 128
        E = 16
        TOP_K = 2

        def _mlp(x, wg, wu, wd):
            return jnp.einsum('bsi,id->bsd', jax.nn.silu(x @ wg) * (x @ wu), wd)
        router_logits = jax.nn.sigmoid(x @ gate_w + gate_b)
        expert_values, expert_indices = jax.lax.top_k(router_logits, k=TOP_K)
        expert_values = expert_values / jnp.sum(expert_values, axis=-1, keepdims=True)
        hg = jnp.einsum('bsd,edi->bsei', x, experts_wg)
        hu = jnp.einsum('bsd,edi->bsei', x, experts_wu)
        all_outputs = jnp.einsum('bsei,eid->bsed', jax.nn.silu(hg) * hu, experts_wd)
        selected = jnp.take_along_axis(all_outputs, expert_indices[..., None], axis=2)
        expert_weighted = jnp.sum(expert_values[..., None] * selected, axis=2)
        return x + _mlp(x, shared_wg, shared_wu, shared_wd) + expert_weighted
    x = L0_attn_x
    x = _layernorm(x + _L0_attn_ref(x, L0_attn_in_proj_w, L0_attn_in_proj_b, L0_attn_conv_w, L0_attn_conv_b, L0_attn_A_log, L0_attn_D, L0_attn_x_proj_w, L0_attn_dt_proj_w, L0_attn_dt_proj_b, L0_attn_out_proj_w, L0_attn_out_proj_b), axis=-1)
    x = _layernorm(x + _L0_ffn_ref(x, L0_ffn_gate_w, L0_ffn_gate_b, L0_ffn_shared_wg, L0_ffn_shared_wu, L0_ffn_shared_wd, L0_ffn_experts_wg, L0_ffn_experts_wu, L0_ffn_experts_wd), axis=-1)
    return x

_drawn_inputs = setup_inputs


def setup_inputs(seed=0):
    import zlib

    import numpy as np

    out = dict(_drawn_inputs(seed))
    spreads = {'L0_attn_in_proj_b': (0.0, 0.553),
     'L0_attn_conv_b': (0.0, 0.1),
     'L0_attn_D': (1.0, 0.6),
     'L0_attn_out_proj_b': (0.0, 0.1),
     'L0_ffn_gate_b': (0.0, 0.1)}
    factors = {'L0_attn_conv_w': 3.769,
     'L0_attn_A_log': 8.0,
     'L0_attn_x_proj_w': 8.0,
     'L0_attn_dt_proj_w': 8.0,
     'L0_attn_dt_proj_b': 8.0}
    for name, (base, spread) in spreads.items():
        noise = np.random.default_rng([zlib.crc32(name.encode()), seed]).standard_normal(out[name].shape)
        drawn = base * np.exp(spread * noise) if base else spread * noise
        out[name] = jnp.asarray(drawn.astype(out[name].dtype))
    for name, factor in factors.items():
        out[name] = (out[name] * factor).astype(out[name].dtype)
    return out
```

```python
from contextlib import ExitStack

import concourse.bass as bass
from concourse import mybir

F32 = mybir.dt.float32
BF16 = mybir.dt.bfloat16
U32 = mybir.dt.uint32
ALU = mybir.AluOpType
ACT = mybir.ActivationFunctionType

P = 128
T = 512
NB, L, DM = 4, 2048, 256
NW = L // T
UNITS = NB * NW
DI = 512
CH = DI // P
KT = DM // P
NS = 16
TAPS = 4
HALO = TAPS - 1
RANK = 64
TT = T // P
EPS = 1e-5
NE = 16
IF = 128

LOG1P = (0.9999997755, -0.4999712607, 0.332711867, -0.2447046963,
         0.1767549328, -0.106677904, 0.04337084989, -0.008336497544)
HORNER = len(LOG1P) - 1
NORM = 16
POOL_HC = (2, 6, 10, 13)


ITEMS = CH * NS
HS = 8
HCS = 4
LAG = 3
LEAD = 4
EVAC = 2
QUAD = 2

def count(unit, per, add):
    j, k = unit
    return per * k + add if isinstance(j, int) and j == 0 else j * (2 * per) + (per * k + add)


def number(unit):
    return count(unit, 1, 0)


def loads(unit):
    j, k = unit
    return 16 * (k // 2 + 1) if isinstance(j, int) else j * 16 + 16 * (k // 2 + 1)


def later(unit, n=1):
    return (unit[0], unit[1] + n)


def batch(unit):
    j, k = unit
    if isinstance(j, int):
        return k % NB
    half = j % 2
    return half * 2 + k if k < 2 else half * (-2) + k


def wait(eng, sem, value):
    if not isinstance(value, int) or value > 0:
        eng.wait_ge(sem, value)


def mamba(nc, d):
    with ExitStack() as ctx:
        def sb(name, shape, dt=F32):
            return ctx.enter_context(nc.sbuf_tensor(name, shape, dt))

        def psum(name, shape):
            return ctx.enter_context(nc.psum_tensor(name, shape, F32))

        def sem(name):
            return ctx.enter_context(nc.semaphore(name))

        w_in = sb("w_in", [P, KT, 2 * DI])
        w_x = sb("w_x", [P, CH, RANK + P])
        w_dt = sb("w_dt", [RANK, DI])
        w_out = sb("w_out", [P, CH, DM])
        b_out = sb("b_out", [1, DM])
        b_in = sb("b_in", [P, 2 * CH])
        taps = sb("taps", [P, CH, TAPS])
        b_conv = sb("b_conv", [P, CH])
        d_skip = sb("d_skip", [P, CH])
        b_dt = sb("b_dt", [P, CH])
        a_log = sb("a_log", [P, CH, NS])
        a_mat = sb("a_mat", [P, CH, NS])
        a_big = sb("a_big", [P, CH, NS])
        a_inv = sb("a_inv", [P, CH, NS])
        ident = sb("ident", [P, P])
        ones = sb("ones", [1, P])
        zeros = sb("zeros", [P, DM])
        pick = sb("pick", [P, 2 * NS], BF16)
        dg_inv = sb("dg_inv", [P, CH, NS, P])
        dg_tap = sb("dg_tap", [P, CH, TAPS, P])
        dg_skip = sb("dg_skip", [P, CH, P])
        carry = sb("carry", [P, NB, CH, NS])
        halo = sb("halo", [P, NB, CH, HALO])

        x_t = sb("x_t", [P, 2, KT, T])
        x_tok = sb("x_tok", [P, TT, DM])
        x_in = sb("x_in", [P, CH, HALO + T])
        x_conv = sb("x_conv", [P, 2, CH, T])
        dt = sb("dt", [P, 2, CH, T])
        gate = sb("gate", [P, CH, T])
        poly = sb("poly", [P, CH, T])
        rest = poly[:, 0]
        dt_low = poly[0:RANK, 1]
        parts = sb("parts", [P, 2, T], BF16)
        y_gated = sb("y_gated", [P, CH, T])
        stats = sb("stats", [P, TT, 6])
        mean_var = sb("mean_var", [P, TT, 2])
        spread = sb("spread", [P, TT])

        h = sb("h", [P, HS, T])
        hc = sb("hc", [P, HCS, T])
        b_rep = sb("b_rep", [P, NS, T])
        c_rep = sb("c_rep", [P, len(POOL_HC), T])

        y_ps = psum("y_ps", [P, 2, T])
        a_ps = psum("a_ps", [P, 2, T])
        work = psum("work", [P, 2, T])
        c_ps = psum("c_ps", [P, 2, T])

        weights_in = sem("weights_in")
        x_t_in = [sem(f"x_t_in{q}") for q in range(2)]
        x_tok_in = sem("x_tok_in")
        x1_out = sem("x1_out")
        slots_zeroed = sem("slots_zeroed")
        ident_ready = sem("ident_ready")
        pick_ready = sem("pick_ready")
        zeroed = sem("zeroed")
        a_exp = sem("a_exp")
        a_inv_step = sem("a_inv_step")
        diags_ready = sem("diags_ready")
        filled = [sem(f"work_filled{q}") for q in range(2)]
        emptied = [sem(f"work_emptied{q}") for q in range(2)]
        halo_moved = sem("halo_moved")
        x_conv_ready = sem("x_conv_ready")
        gate_ready = sem("gate_ready")
        abs_done = sem("abs_done")
        exp_neg_ready = sem("exp_neg_ready")
        poly_ready = sem("poly_ready")
        softplus_step = sem("softplus_step")
        high_ready = sem("high_ready")
        split_step = sem("split_step")
        dt_ready = sem("dt_ready")
        u_ready = sem("u_ready")
        a_ready = sem("a_ready")
        b_ready = sem("b_ready")
        scanned = sem("scanned")
        summed = sem("summed")
        c_ready = sem("c_ready")
        hc_vector = sem("hc_vector")
        hc_pool = sem("hc_pool")
        carried = sem("carried")
        gated = sem("gated")
        norm_step = sem("norm_step")
        std_ready = sem("std_ready")

        NP, NV = CH * len(POOL_HC), CH * (NS - len(POOL_HC))

        def on_pool(m):
            return m % NS in POOL_HC

        def pool_before(m):
            return sum(on_pool(k) for k in range(m))

        def vector_before(m):
            return m - pool_before(m)

        PLACE = [("x0", 0), ("x1", 2), ("x2", 4), ("z0", 5), ("x3", 6), ("z1", 7), ("c0", 8), ("o0", 10), ("c1", 11),
                 ("o1", 12), ("z2", 13), ("c2", 14), ("z3", 15), ("c3", 17), ("dl", 22), ("bc", 24),
                 ("d0", 27), ("d1", 29), ("d2", 31), ("d3", 33)]
        last_chunk = ITEMS - NS
        PLACE += sorted([(f"B{s}", last_chunk - EVAC + s) for s in range(NS)] +
                        [(f"C{s}", last_chunk + s) for s in POOL_HC], key=lambda t: t[1])
        WHERE = dict(PLACE)

        class Plan:

            def __init__(self, kinds, base):
                self.tiles = [t for t, _ in PLACE if t[0] in kinds or t in kinds]
                self.base = base

            def at(self, m):
                return [t for t in self.tiles if WHERE[t] == m]

            def has(self, tile):
                return tile in self.tiles

            def bank(self, tile):
                return self.tiles.index(tile) % 2

            def before(self, tile, unit):
                n = self.tiles.index(tile) // 2
                b = self.base
                return b(unit) + n if callable(b) else b + n

        PREP = ["x", "c", "dl", "bc", "d", "B", "C"]
        first = Plan(PREP, 0)
        second = Plan(PREP + ["z"], 17)
        inner = Plan(PREP + ["z", "o"], lambda u: count(u, 20, 16))
        last = Plan(["z", "o"], 16 + 20 * (UNITS - 1))
        final = Plan(["o"], 16 + 20 * (UNITS - 1) + 3)

        def emptied_all(eng, plan, unit, tiles):
            most = {}
            for t in tiles:
                most[plan.bank(t)] = t
            for bank, t in most.items():
                eng.wait_ge(emptied[bank], plan.before(t, unit) + 1)

        def hc_wait(eng, unit, m):
            if on_pool(m):
                eng.wait_ge(hc_pool, count(unit, NP, pool_before(m) + 1))
            else:
                eng.wait_ge(hc_vector, count(unit, NV, vector_before(m) + 1))

        def before(unit, m, n):
            return (unit, m - n) if m >= n else (later(unit, -1), m - n + ITEMS)

        def after(unit, m, n):
            return (unit, m + n) if m + n < ITEMS else (later(unit), m + n - ITEMS)

        def row_ready(eng, unit, tile):
            if isinstance(unit[0], int) and unit[1] == 0:
                emptied_all(eng, first, (0, -1), [tile])
            else:
                emptied_all(eng, inner, later(unit, -1), [tile])

        def whole(eng, unit_program):
            unit_program((0, 0), second)
            with eng.Fori(0, (UNITS - 2) // 2) as j:
                unit_program((j, 1), inner)
                unit_program((j, 2), inner)
            unit_program((0, UNITS - 1), last)

        WEIGHTS = ["w_in", "w_x", "w_dt", "w_out", "b_out", "b_in", "taps", "b_conv", "d_skip", "b_dt", "a_log"]
        holders = dict(w_in=w_in, w_x=w_x, w_dt=w_dt, w_out=w_out, b_out=b_out, b_in=b_in, taps=taps,
                       b_conv=b_conv, d_skip=d_skip, b_dt=b_dt, a_log=a_log)
        ALL_WEIGHTS = 16 * len(WEIGHTS)
        ADD_RELU_AT = (52, 54, 56, 58)
        x_arg = x_in[:, :, HALO:]

        block = ctx.enter_context(nc.Block())

        @block.sync
        def _(sp):
            sp.dma_start(x_t[:, 0], d["x_t"][0]).then_inc(x_t_in[0], 16)
            for name in WEIGHTS:
                sp.dma_start(holders[name][:], d[name]).then_inc(weights_in, 16)
            sp.dma_start(x_tok[:], d["x_tok"][0]).then_inc(x_tok_in, 16)

            ZERO = SLOT_TILES // UNITS

            def unit_program(u, plan):
                nq = (u[1] + 1) % 2
                if plan is second:
                    sp.wait_ge(zeroed, 6)
                sp.dma_start(d["x_slots"][:, bass.ds(number(u) * ZERO, ZERO)],
                             zeros[:].unsqueeze(1).to_broadcast([P, ZERO, DM])).then_inc(slots_zeroed, 16)
                if plan is not last:
                    if plan is not second:
                        prev = later(u, -1)
                        sp.wait_ge(emptied[inner.bank("z3")], inner.before("z3", prev) + 1)
                    sp.dma_start(x_t[:, nq], d["x_t"][number(later(u))]).then_inc(x_t_in[nq], 16)
                if plan is not second:
                    sp.wait_ge(norm_step, count(u, NORM, 0))
                    sp.dma_start(d["x1"][number(later(u, -1))], x_tok[:]).then_inc(x1_out, 16)
                    sp.wait_ge(x1_out, count(u, 16, 0))
                    sp.dma_start(x_tok[:], d["x_tok"][number(u)]).then_inc(x_tok_in, 16)

            whole(sp, unit_program)
            sp.wait_ge(norm_step, NORM * UNITS)
            sp.dma_start(d["x1"][UNITS - 1], x_tok[:]).then_inc(x1_out, 16)
            sp.wait_ge(x1_out, 16 * UNITS)
            sp.wait_ge(slots_zeroed, 16 * UNITS)

        @block.gpsimd
        def _(pool):
            nc.gpsimd.memset(ident[:], 0.0).then_inc(zeroed, 1)
            nc.gpsimd.memset(pick[:], 0.0).then_inc(zeroed, 1)
            nc.gpsimd.memset(ones[:], 1.0).then_inc(zeroed, 1)
            nc.gpsimd.memset(carry[:], 0.0).then_inc(zeroed, 1)
            nc.gpsimd.memset(halo[:], 0.0).then_inc(zeroed, 1)
            nc.gpsimd.memset(zeros[:], 0.0).then_inc(zeroed, 1)
            pool.wait_ge(zeroed, 6)
            nc.gpsimd.affine_select(out=ident[:], in_=ident[:], compare_op=ALU.not_equal, fill=1.0, base=0,
                                    pattern=[[-1, P]], channel_multiplier=1).then_inc(ident_ready, 1)
            for n, row in enumerate((0, 64, 96)):
                wait(pool, pick_ready, n)
                nc.gpsimd.affine_select(out=pick[:], in_=pick[:], compare_op=ALU.not_equal, fill=1.0, base=-row,
                                        pattern=[[-1, 2 * NS]], channel_multiplier=1).then_inc(pick_ready, 1)

            def make_u(u, m):
                c, s = divmod(m, NS)
                if m == 0:
                    pool.wait_ge(x_conv_ready, count(u, 1, 1))
                if c == 0:
                    row_ready(pool, u, f"B{s}")
                if u[1] > 0 or m >= HS:
                    ou, om = before(u, m, HS)
                    hc_wait(pool, ou, om)
                    pool.wait_ge(carried, count(ou, ITEMS // QUAD, om // QUAD + 1))
                nc.gpsimd.tensor_tensor(h[:, m % HS], x_conv[:, u[1] % 2, c], b_rep[:, s], ALU.mult).then_inc(u_ready, 1)

            def make_hc(u, m):
                n = POOL_HC.index(m % NS)
                pool.wait_ge(scanned, count(u, ITEMS, m + 1))
                if m < NS:
                    row_ready(pool, u, f"C{m}")
                wait(pool, summed, count(u, ITEMS, m - HCS + 1))
                nc.gpsimd.tensor_tensor(hc[:, m % HCS], h[:, m % HS], c_rep[:, n], ALU.mult).then_inc(hc_pool, 1)

            def add_relu(u, c):
                n, nq = later(u), (u[1] + 1) % 2
                pool.wait_ge(softplus_step, count(n, HORNER, HORNER))
                nc.gpsimd.tensor_tensor(dt[:, nq, c], dt[:, nq, c], poly[:, c], ALU.add).then_inc(dt_ready, 1)

            def unit_program(u, plan):
                for m in range(ITEMS):
                    nu, nm = after(u, m, LEAD)
                    if not (plan is last and m + LEAD >= ITEMS):
                        make_u(nu, nm)
                    pu, pm = before(u, m, 1)
                    if on_pool(pm) and not (plan is second and m == 0):
                        make_hc(pu, pm)
                    if plan is not last and m in ADD_RELU_AT:
                        add_relu(u, ADD_RELU_AT.index(m))

            for c in range(CH):
                add_relu((0, -1), c)
            for m in range(LEAD):
                make_u((0, 0), m)
            whole(pool, unit_program)

        @block.scalar
        def _(act):
            act.wait_ge(weights_in, ALL_WEIGHTS)
            nc.scalar.activation(a_mat[:], a_log[:], ACT.Exp).then_inc(a_exp, 1)

            def make_a(u, m):
                c, s = divmod(m, NS)
                if s == 0:
                    act.wait_ge(dt_ready, count(u, CH, c + 1))
                wait(act, scanned, count(u, ITEMS, m - 1))
                nc.scalar.activation(a_ps[:, m % 2], dt[:, u[1] % 2, c], ACT.Exp,
                                     scale=a_mat[:, c, s:s + 1]).then_inc(a_ready, 1)

            def tile(u, plan, t):
                n, nq = later(u), (u[1] + 1) % 2
                bank = plan.bank(t)
                kind = t[0]
                if t in ("dl", "bc"):
                    act.wait_ge(filled[bank], plan.before(t, u) + 1)
                    if t == "dl":
                        wait(act, dt_ready, count(n, CH, 0))
                        nc.scalar.activation(dt_low, work[0:RANK, bank], ACT.Copy).then_inc(emptied[bank], 1)
                    else:
                        nc.scalar.activation(parts[:, nq], work[:, bank], ACT.Copy).then_inc(high_ready, 1)
                    return
                c = int(t[1:])
                if kind == "B":
                    act.wait_ge(filled[bank], plan.before(t, u) + 1)
                    wait(act, u_ready, count(n, ITEMS, c + 1 - NS))
                    nc.scalar.activation(b_rep[:, c], work[:, bank], ACT.Copy).then_inc(emptied[bank], 1)
                elif kind == "C":
                    k = POOL_HC.index(c)
                    act.wait_ge(filled[bank], plan.before(t, u) + 1)
                    wait(act, hc_pool, count(n, NP, k + 1 - len(POOL_HC)))
                    nc.scalar.activation(c_rep[:, k], work[:, bank], ACT.Copy).then_inc(emptied[bank], 1)
                elif kind == "x":
                    act.wait_ge(filled[bank], plan.before(t, u) + 1)
                    wait(act, softplus_step, count(n, HORNER, 0))
                    nc.scalar.activation(x_in[:, c, HALO:], work[:, bank], ACT.Identity,
                                         bias=b_in[:, c:c + 1]).then_inc(emptied[bank], 1)
                elif kind == "c":
                    act.wait_ge(filled[bank], plan.before(t, u) + 1)
                    if c == 0:
                        wait(act, u_ready, count(u, ITEMS, 0))
                    nc.scalar.activation(x_conv[:, nq, c], work[:, bank], ACT.Identity,
                                         bias=b_conv[:, c:c + 1]).then_inc(emptied[bank], 1)
                elif kind == "z":
                    act.wait_ge(filled[bank], plan.before(t, u) + 1)
                    if c == 0:
                        wait(act, gated, count(u, CH, 0))
                    nc.scalar.activation(gate[:, c], work[:, bank], ACT.Identity,
                                         bias=b_in[:, CH + c:CH + c + 1]).then_inc(emptied[bank], 1)
                elif kind == "d":
                    act.wait_ge(filled[bank], plan.before(t, u) + 1)
                    if c == 0:
                        wait(act, a_ready, count(u, ITEMS, 0))
                        act.wait_ge(halo_moved, count(n, 2, 2))
                    nc.scalar.activation(x_arg[:, c], work[:, bank], ACT.Abs, bias=b_dt[:, c:c + 1]).then_inc(abs_done, 1)
                    nc.scalar.activation(dt[:, nq, c], work[:, bank], ACT.Relu,
                                         bias=b_dt[:, c:c + 1]).then_inc(emptied[bank], 1)

            def root(pu):
                act.wait_ge(norm_step, count(pu, NORM, 11))
                nc.scalar.activation(spread[:], spread[:], ACT.Sqrt).then_inc(std_ready, 1)

            def weave(u, plan, m):
                n, nq = later(u), (u[1] + 1) % 2
                for t in plan.at(m - EVAC):
                    if t[0] != "o":
                        tile(u, plan, t)
                if m == 20:
                    if plan.has("c0"):
                        emptied_all(act, plan, u, [f"c{c}" for c in range(CH)])
                        nc.scalar.activation(x_conv[:, nq], x_conv[:, nq], ACT.Silu).then_inc(x_conv_ready, 1)
                    if plan.has("z0"):
                        emptied_all(act, plan, u, [f"z{c}" for c in range(CH)])
                        nc.scalar.activation(gate[:], gate[:], ACT.Silu).then_inc(gate_ready, 1)
                    if plan.has("o0"):
                        root(later(u, -1))
                if m == 36 and plan.has("d0"):
                    act.wait_ge(abs_done, count(n, CH, CH))
                    nc.scalar.activation(x_arg, x_arg, ACT.Exp, scale=-1.0).then_inc(exp_neg_ready, 1)
                    act.wait_ge(exp_neg_ready, count(n, 1, 1))
                    act.wait_ge(split_step, count(n, 2, 2))
                    nc.scalar.activation(poly[:], x_arg, ACT.Copy, scale=LOG1P[-1]).then_inc(poly_ready, 1)

            def unit_program(u, plan):
                for m in range(ITEMS):
                    nu, nm = after(u, m, 2)
                    if not (plan is last and m + 2 >= ITEMS):
                        make_a(nu, nm)
                    weave(u, plan, m)

            for m in range(ITEMS):
                weave((0, -1), first, m)
            act.wait_ge(a_inv_step, 5)
            for m in range(2):
                make_a((0, 0), m)
            whole(act, unit_program)
            root((0, UNITS - 1))

        @block.tensor
        def _(pe):
            pe.wait_ge(weights_in, ALL_WEIGHTS)
            pe.wait_ge(diags_ready, 1)
            pe.wait_ge(pick_ready, 3)

            def replicate(dst, q, row):
                return nc.tensor.matmul(dst, pick[:, row:row + 1].to_broadcast([P, P]), parts[:, q], start=True, stop=True)

            def make_c(u, m):
                n = vector_before(m)
                if m < NS:
                    pe.wait_ge(split_step, count(u, 2, 2))
                wait(pe, hc_vector, count(u, NV, n - 1))
                replicate(c_ps[:, n % 2], u[1] % 2, NS + m % NS).then_inc(c_ready, 1)

            def add_item(u, m):
                c, s = divmod(m, NS)
                if s == 0:
                    wait(pe, gated, count(u, CH, c - 1))
                    if c == 0:
                        pe.wait_ge(x_conv_ready, count(u, 1, 1))
                    nc.tensor.matmul(y_ps[:, c % 2], dg_skip[:, c], x_conv[:, u[1] % 2, c], start=True, stop=False)
                hc_wait(pe, u, m)
                nc.tensor.matmul(y_ps[:, c % 2], dg_inv[:, c, s], hc[:, m % HCS], start=False,
                                 stop=(s == NS - 1)).then_inc(summed, 1)

            def tile(u, plan, t):
                n, q, nq = later(u), u[1] % 2, (u[1] + 1) % 2
                bank = plan.bank(t)
                wait(pe, emptied[bank], plan.before(t, u))
                out = work[:, bank]
                if t == "x0":
                    pe.wait_ge(x_t_in[nq], loads(n))
                if t[0] in "BC":
                    if t == "B0":
                        pe.wait_ge(split_step, count(n, 2, 2))
                    mm = replicate(out, nq, int(t[1:]) + (NS if t[0] == "C" else 0))
                elif t[0] == "x" or t[0] == "z":
                    m = int(t[1]) + (CH if t[0] == "z" else 0)
                    src = nq if t[0] == "x" else q
                    for k in range(KT):
                        mm = nc.tensor.matmul(out, w_in[:, k, m * P:(m + 1) * P], x_t[:, src, k], start=(k == 0), stop=(k == KT - 1))
                elif t[0] == "c":
                    c = int(t[1])
                    pe.wait_ge(halo_moved, count(n, 2, 1))
                    emptied_all(pe, plan, u, [f"x{c}"])
                    for k in range(TAPS):
                        mm = nc.tensor.matmul(out, dg_tap[:, c, k], x_in[:, c, k:k + T], start=(k == 0), stop=(k == TAPS - 1))
                elif t == "dl":
                    pe.wait_ge(x_conv_ready, count(n, 1, 1))
                    for c in range(CH):
                        mm = nc.tensor.matmul(work[0:RANK, bank], w_x[:, c, 0:RANK], x_conv[:, nq, c], start=(c == 0), stop=(c == CH - 1))
                elif t == "bc":
                    for c in range(CH):
                        mm = nc.tensor.matmul(out, w_x[:, c, RANK:], x_conv[:, nq, c], start=(c == 0), stop=(c == CH - 1))
                elif t[0] == "d":
                    c = int(t[1])
                    emptied_all(pe, plan, u, ["dl"])
                    mm = nc.tensor.matmul(out, w_dt[:, c * P:(c + 1) * P], dt_low, start=True, stop=True)
                elif t[0] == "o":
                    pe.wait_ge(gated, count(u, CH, 0))
                    for tt in range(2):
                        tok = (2 * int(t[1]) + tt) * P
                        o = work[:, bank, tt * DM:(tt + 1) * DM]
                        nc.tensor.matmul(o, ones[:], b_out[:], start=True, stop=False)
                        for c in range(CH):
                            mm = nc.tensor.matmul(o, y_gated[:, c, tok:tok + P], w_out[:, c], start=False, stop=(c == CH - 1))
                mm.then_inc(filled[bank], 1)

            def weave(u, plan, m):
                for t in plan.at(m):
                    tile(u, plan, t)

            def unit_program(u, plan):
                for m in range(ITEMS):
                    nu, nm = after(u, m, 1)
                    if not on_pool(nm) and not (plan is last and m == ITEMS - 1):
                        make_c(nu, nm)
                    pu, pm = before(u, m, LAG)
                    if not (plan is second and m < LAG):
                        add_item(pu, pm)
                    weave(u, plan, m)

            for m in range(ITEMS):
                weave((0, -1), first, m)
            make_c((0, 0), 0)
            whole(pe, unit_program)
            for m in range(ITEMS - LAG, ITEMS):
                add_item((0, UNITS - 1), m)
            for t in ("o0", "o1"):
                tile((0, UNITS), final, t)

        @block.vector
        def _(dve):
            dve.wait_ge(weights_in, ALL_WEIGHTS)
            dve.wait_ge(ident_ready, 1)
            for c in range(CH):
                for k in range(TAPS):
                    nc.vector.tensor_scalar(dg_tap[:, c, k], ident[:], taps[:, c, k:k + 1], None, ALU.mult)
                nc.vector.tensor_scalar(dg_skip[:, c], ident[:], d_skip[:, c:c + 1], None, ALU.mult)
            dve.wait_ge(a_exp, 1)
            nc.vector.tensor_scalar(a_big[:], a_mat[:], 1e-6, None, ALU.is_ge).then_inc(a_inv_step, 1)
            dve.wait_ge(a_inv_step, 1)
            nc.vector.scalar_tensor_tensor(out=a_inv[:], in0=a_mat[:], scalar=-1.0, in1=a_big[:], op0=ALU.mult,
                                           op1=ALU.mult).then_inc(a_inv_step, 1)
            dve.wait_ge(a_inv_step, 2)
            nc.vector.scalar_tensor_tensor(out=a_inv[:], in0=a_inv[:], scalar=1.0, in1=a_big[:], op0=ALU.add,
                                           op1=ALU.subtract).then_inc(a_inv_step, 1)
            dve.wait_ge(a_inv_step, 3)
            nc.vector.reciprocal(a_inv[:], a_inv[:]).then_inc(a_inv_step, 1)
            dve.wait_ge(a_inv_step, 4)
            nc.vector.tensor_scalar(a_mat[:], a_mat[:], -1.0, None, ALU.mult).then_inc(a_inv_step, 1)
            for c in range(CH):
                for s in range(NS):
                    one = nc.vector.tensor_scalar(dg_inv[:, c, s], ident[:], a_inv[:, c, s:s + 1], None, ALU.mult)
            one.then_inc(diags_ready, 1)

            def make_b(u, m):
                dve.wait_ge(a_ready, count(u, ITEMS, m + 1))
                dve.wait_ge(u_ready, count(u, ITEMS, m + 1))
                nc.vector.scalar_tensor_tensor(out=h[:, m % HS], in0=a_ps[:, m % 2], scalar=1.0, in1=h[:, m % HS],
                                               op0=ALU.subtract, op1=ALU.mult).then_inc(b_ready, 1)

            def scan(u, m):
                c, s = divmod(m, NS)
                dve.wait_ge(b_ready, count(u, ITEMS, m + 1))
                nc.vector.tensor_tensor_scan(h[:, m % HS], a_ps[:, m % 2], h[:, m % HS],
                                             carry[:, batch(u), c, s:s + 1], ALU.mult, ALU.add).then_inc(scanned, 1)

            def save_carry(u, g):
                c, s = divmod(g * QUAD, NS)
                slot = g * QUAD % HS
                dve.wait_ge(scanned, count(u, ITEMS, g * QUAD + QUAD))
                nc.vector.tensor_scalar(carry[:, batch(u), c, s:s + QUAD], h[:, slot:slot + QUAD, T - 1], 1.0, None,
                                        ALU.mult).then_inc(carried, 1)

            def make_hc(u, m):
                dve.wait_ge(c_ready, count(u, NV, vector_before(m) + 1))
                dve.wait_ge(scanned, count(u, ITEMS, m + 1))
                wait(dve, summed, count(u, ITEMS, m - HCS + 1))
                nc.vector.tensor_tensor(hc[:, m % HCS], h[:, m % HS], c_ps[:, vector_before(m) % 2], ALU.mult).then_inc(hc_vector, 1)

            def make_gated(u, c):
                dve.wait_ge(summed, count(u, ITEMS, (c + 1) * NS))
                if c == 0:
                    dve.wait_ge(gate_ready, count(u, 1, 1))
                nc.vector.tensor_tensor(y_gated[:, c], y_ps[:, c % 2], gate[:, c], ALU.mult).then_inc(gated, 1)

            def halo_in(n):
                wait(dve, halo_moved, count(n, 2, 0))
                nc.vector.tensor_scalar(x_in[:, :, 0:HALO], halo[:, batch(n)], 1.0, None, ALU.mult).then_inc(halo_moved, 1)

            def halo_out(u, plan):
                emptied_all(dve, plan, u, [f"x{c}" for c in range(CH)])
                dve.wait_ge(halo_moved, count(later(u), 2, 1))
                nc.vector.tensor_scalar(halo[:, batch(later(u))], x_in[:, :, T:], 1.0, None, ALU.mult).then_inc(halo_moved, 1)

            def norm_so_far(pu, n):
                dve.wait_ge(norm_step, count(pu, NORM, n))

            def norm_sums(u, plan, t):
                k, bank, pu = int(t[1]), plan.bank(t), later(u, -1)
                if k == 0:
                    dve.wait_ge(x_tok_in, count(pu, 16, 16))
                dve.wait_ge(filled[bank], plan.before(t, u) + 1)
                two = x_tok[:, 2 * k:2 * k + 2]
                nc.vector.tensor_tensor(two, work[:, bank].rearrange("p (a b) -> p a b", a=2), two,
                                        ALU.add).then_inc(emptied[bank], 1)
                dve.wait_ge(emptied[bank], plan.before(t, u) + 1)
                for tt in (2 * k, 2 * k + 1):
                    nc.vector.bn_stats(stats[:, tt], x_tok[:, tt]).then_inc(norm_step, 1)
                norm_so_far(pu, 5 * k + 2)
                nc.vector.memset(spread[:, 2 * k:2 * k + 2], EPS).then_inc(norm_step, 1)
                for tt in (2 * k, 2 * k + 1):
                    nc.vector.bn_aggr(mean_var[:, tt], stats[:, tt]).then_inc(norm_step, 1)
                if k == 1:
                    norm_so_far(pu, 10)
                    nc.vector.tensor_tensor(spread[:], spread[:], mean_var[:, :, 1], ALU.add).then_inc(norm_step, 1)

            def normalise(pu):
                dve.wait_ge(std_ready, count(pu, 1, 1))
                nc.vector.reciprocal(spread[:], spread[:]).then_inc(norm_step, 1)
                norm_so_far(pu, 12)
                for tt in range(TT):
                    row = x_tok[:, tt]
                    nc.vector.tensor_scalar(row, row, mean_var[:, tt, 0:1], spread[:, tt:tt + 1], ALU.subtract,
                                            ALU.mult).then_inc(norm_step, 1)

            def split(u, plan):
                n, nq, bank = later(u), (u[1] + 1) % 2, plan.bank("bc")
                dve.wait_ge(high_ready, count(n, 1, 1))
                wait(dve, dt_ready, count(n, CH, 0))
                nc.vector.tensor_tensor(rest[64:], work[64:, bank], parts[64:, nq], ALU.subtract).then_inc(emptied[bank], 1)
                dve.wait_ge(emptied[bank], plan.before("bc", u) + 1)
                nc.vector.tensor_copy(parts[64:, nq], rest[64:]).then_inc(split_step, 1)
                dve.wait_ge(split_step, count(n, 2, 1))
                nc.vector.tensor_tensor(parts[96:, nq], rest[96:], parts[96:, nq], ALU.subtract).then_inc(split_step, 1)

            def softplus(u, k):
                n = later(u)
                if k == 0:
                    dve.wait_ge(poly_ready, count(n, 1, 1))
                else:
                    dve.wait_ge(softplus_step, count(n, HORNER, k))
                nc.vector.scalar_tensor_tensor(out=poly[:], in0=poly[:], scalar=LOG1P[-2 - k], in1=x_arg,
                                               op0=ALU.add, op1=ALU.mult).then_inc(softplus_step, 1)

            GATED_AT = {24: 0, 36: 1, 52: 2}
            SOFTPLUS_AT = tuple(range(38, 38 + 2 * HORNER, 2))

            def weave(u, plan, m):
                if plan.has("x0"):
                    if m == 5:
                        halo_in(later(u))
                    if m == 10:
                        halo_out(u, plan)
                    if m == 28:
                        split(u, plan)
                    if m in SOFTPLUS_AT:
                        softplus(u, SOFTPLUS_AT.index(m))
                if m == 4 and plan in (inner, last):
                    make_gated(later(u, -1), CH - 1)
                if m in GATED_AT and plan is not first:
                    make_gated(u, GATED_AT[m])
                if plan.has("o0"):
                    if m in (12, 14):
                        norm_sums(u, plan, f"o{(m - 12) // 2}")
                    if m == 26:
                        normalise(later(u, -1))

            def unit_program(u, plan):
                for m in range(ITEMS):
                    scan(u, m)
                    nu, nm = after(u, m, 1)
                    if not (plan is last and m == ITEMS - 1):
                        make_b(nu, nm)
                    pu, pm = before(u, m, 1)
                    if not on_pool(pm) and not (plan is second and m == 0):
                        make_hc(pu, pm)
                    if m % QUAD == 0 and not (plan is second and m == 0):
                        gu, gm = before(u, m, QUAD)
                        save_carry(gu, gm // QUAD)
                    weave(u, plan, m)

            dve.wait_ge(zeroed, 6)
            for m in range(ITEMS):
                weave((0, -1), first, m)
            make_b((0, 0), 0)
            whole(dve, unit_program)
            make_hc((0, UNITS - 1), ITEMS - 1)
            make_gated((0, UNITS - 1), CH - 1)
            for k in range(2):
                norm_sums((0, UNITS), final, f"o{k}")
            normalise((0, UNITS - 1))


GROUP = 4
ROWS = UNITS * T
TILES = ROWS // P
SLOT_TILES = 2 * TILES + NE
GROUPS = SLOT_TILES // GROUP
SHARED = NE


OWNER_PART = SLOT_TILES // 3
EITHER_AT, SLOTS_AT, OWNER_AT = 12, 34, 42


def moe_layout(g, chunks):
    import numpy as np

    def stack(name):
        return np.concatenate([g[f"L0_ffn_experts_{name}"], g[f"L0_ffn_shared_{name}"][None]])

    up = np.concatenate([stack("wg"), stack("wu")], axis=2)
    return {
        "w_gate": chunks(g["L0_ffn_gate_w"]),
        "b_gate": g["L0_ffn_gate_b"][None],
        "w_up": up.reshape(NE + 1, KT, P, 2 * IF).transpose(2, 0, 1, 3),
        "w_down": stack("wd").transpose(1, 0, 2),
    }


def moe(nc, d):
    with ExitStack() as ctx:
        def sb(name, shape, dt=F32):
            return ctx.enter_context(nc.sbuf_tensor(name, shape, dt))

        def sem(name):
            return ctx.enter_context(nc.semaphore(name))

        w_gate = sb("w_gate", [P, KT, NE])
        b_gate = sb("b_gate", [1, NE])
        w_up = sb("w_up", [P, NE + 1, KT, 2 * IF])
        w_down = sb("w_down", [P, NE + 1, DM])
        ident = sb("moe_ident", [P, P])
        ones = sb("moe_ones", [1, P])
        tri = sb("tri", [P, P], BF16)
        full = sb("full", [P, P], BF16)
        precedence = sb("precedence", [P, NE])
        steps = sb("steps", [P, TILES])
        slots_seq = sb("slots_seq", [1, SLOT_TILES])

        acc = sb("acc", [P, UNITS, TT, DM])
        x1_t = sb("x1_t", [P, UNITS, KT, T])

        score = sb("score", [P, TILES, NE])
        rank = sb("rank", [P, TILES, NE])
        chosen = sb("chosen", [P, 2, TILES, NE])
        either = sb("either", [P, TILES, NE], BF16)
        best = sb("best", [P, 2, TILES])
        first_rank = sb("first_rank", [P, TILES])
        used = sb("used", [P, NE])
        used_end = sb("used_end", [P, NE])
        owner_f = sb("owner_f", [1, SLOT_TILES])
        owner = sb("owner", [1, SLOT_TILES], U32)
        slot_f = sb("slot_f", [P, 2, TILES])
        slot = sb("slot", [P, 2, TILES], U32)
        mean_var = sb("moe_mean_var", [P, 2, TT, 2])
        stats = sb("moe_stats", [P, 2, TT, 6])
        spread = sb("moe_spread", [P, 2, TT])
        silu = chosen[:, 0].rearrange("p a b -> p (a b)").rearrange("p (a b) -> p a b", a=2)
        hidden = chosen[:, 1].rearrange("p a b -> p (a b)").rearrange("p (a b) -> p a b", a=2)

        def room(first, units):
            return x1_t[:, first:first + units].rearrange("p u k t -> p (u k t)")

        x_slots = room(0, 2).rearrange("p (g c f) -> p g c f", g=2, c=GROUP)
        y_slots = room(2, 2).rearrange("p (g c f) -> p g c f", g=2, c=GROUP)
        xt = room(4, 1).rearrange("p (a f) -> p a f", a=4)
        e_silu = room(5, 1).rearrange("p (a f) -> p a f", a=8)[:, 0:2]
        e_hidden = room(5, 1).rearrange("p (a f) -> p a f", a=8)[:, 2:4]
        e_hidden_t = room(5, 1).rearrange("p (a f) -> p a f", a=8)[:, 4:6]
        NG = 4
        gathered = room(6, 2 * NG).rearrange("p (n t r f) -> p n t r f", n=NG, t=TT, r=2)

        banks = ctx.enter_context(nc.psum_tensor("banks", [P, 8, T], F32))
        turn_ps = banks[:, 0:4].rearrange("p (a k) t -> p a k t", a=2)
        logits_ps = banks[:, 4:6].rearrange("p a t -> p (a t)").rearrange("p (a e) -> p a e", a=TILES)
        within_ps = banks[:, 0:2].rearrange("p a t -> p (a t)").rearrange("p (a e) -> p a e", a=TILES)
        totals_ps = banks[:, 2:4].rearrange("p a t -> p (a t)").rearrange("p (a e) -> p a e", a=TILES)
        g_ps, u_ps = banks[:, 0:2], banks[:, 2:4]
        d_ps = banks[:, 4:6].rearrange("p a t -> p (a t)").rearrange("p (a f) -> p a f", a=TT)
        xt_ps = banks[:, 0:2]
        gu_ps = banks[:, 2:4]
        ht_ps = banks[:, 4:5]
        y_ps = banks[:, 5:7]

        w_in_sem = sem("moe_weights_in")
        x1_in = [sem(f"x1_in{q}") for q in range(4)]
        made = sem("moe_constants_made")
        turned = sem("turned")
        x1_t_act = sem("x1_t_act")
        x1_t_dve = sem("x1_t_dve")
        logits_ready = sem("logits_ready")
        score_ready = sem("score_ready")
        step = sem("route_step")
        counted = sem("counted")
        up_ready = sem("up_ready")
        silu_ready = sem("silu_ready")
        hidden_ready = sem("hidden_ready")
        down_ready = sem("down_ready")
        blended = sem("blended")
        scattered = [sem(f"scattered{q}") for q in range(4)]
        x_slots_in = [sem(f"x_slots_in{q}") for q in range(2)]
        xt_made = sem("xt_made")
        xt_ready = sem("xt_ready")
        e_up = sem("e_up")
        e_silu_ready = sem("e_silu_ready")
        e_hidden_ready = sem("e_hidden_ready")
        ht_made = sem("ht_made")
        ht_ready = sem("ht_ready")
        y_made = sem("y_made")
        y_ready = sem("y_ready")
        y_stored = [sem(f"y_stored{q}") for q in range(2)]
        gathered_in = [sem(f"gathered_in{q}") for q in range(NG)]
        mixed = sem("mixed")
        norm = sem("moe_norm_step")
        std = sem("moe_std_ready")
        out_stored = sem("out_stored")

        MOE_NORM = 2 * TT + 3 + TT
        NAMES = ["w_gate", "b_gate", "w_up", "w_down"]
        held = dict(w_gate=w_gate, b_gate=b_gate, w_up=w_up, w_down=w_down)

        BODY = 2 * GROUP
        BODIES = SLOT_TILES // BODY

        def tiles(eng, program):
            for c in range(BODY):
                program(0, c, c)
            with eng.Fori(1, BODIES - 1) as r:
                for c in range(BODY):
                    program(r, c, None)
            for c in range(BODY):
                program(BODIES - 1, c, (BODIES - 1) * BODY + c)

        def tile_no(r, c):
            return r * BODY + c

        block = ctx.enter_context(nc.Block())

        @block.sync
        def _(sp):
            for q in range(4):
                sp.dma_start(acc[:, q], d["x1"][q]).then_inc(x1_in[q], 16)
            for name in NAMES:
                sp.dma_start(held[name][:], d[name]).then_inc(w_in_sem, 16)
            for i in range(4, UNITS):
                sp.wait_ge(x1_in[i % 4], 16 * (i // 4))
                sp.dma_start(acc[:, i], d["x1"][i]).then_inc(x1_in[i % 4], 16)

            for q in range(4):
                sp.wait_ge(scattered[q], UNITS // 4 * 16 * 2 * TT)
            sp.wait_ge(hidden_ready, UNITS)

            def load(r, g):
                sp.dma_start(x_slots[:, g], d["x_slots"][:, r * BODY + g * GROUP:r * BODY + (g + 1) * GROUP] if isinstance(r, int)
                             else d["x_slots"][:, bass.ds(r * BODY + g * GROUP, GROUP)]).then_inc(x_slots_in[g], 16)

            def store(r, g):
                sp.wait_ge(y_ready, r * BODY + (g + 1) * GROUP)
                sp.dma_start(d["y_slots"][:, r * BODY + g * GROUP:r * BODY + (g + 1) * GROUP] if isinstance(r, int)
                             else d["y_slots"][:, bass.ds(r * BODY + g * GROUP, GROUP)], y_slots[:, g]).then_inc(y_stored[g], 16)

            load(0, 0)
            load(0, 1)

            def body(r, more):
                for g in range(2):
                    if more:
                        sp.wait_ge(xt_made, r * BODY + (g + 1) * GROUP)
                        load(r + 1, g)
                    store(r, g)

            body(0, True)
            with sp.Fori(1, BODIES - 1) as r:
                body(r, True)
            body(BODIES - 1, False)

            for i in range(UNITS):
                sp.wait_ge(norm, (i + 1) * MOE_NORM)
                sp.dma_start(d["out"][i], acc[:, i]).then_inc(out_stored, 16)
            sp.wait_ge(out_stored, 16 * UNITS)

        @block.gpsimd
        def _(pool):
            nc.gpsimd.memset(ident[:], 0.0).then_inc(made, 1)
            nc.gpsimd.memset(ones[:], 1.0).then_inc(made, 1)
            nc.gpsimd.memset(tri[:], 0.0).then_inc(made, 1)
            nc.gpsimd.memset(full[:], 1.0).then_inc(made, 1)
            pool.wait_ge(made, 4)
            nc.gpsimd.affine_select(out=ident[:], in_=ident[:], compare_op=ALU.not_equal, fill=1.0, base=0,
                                    pattern=[[-1, P]], channel_multiplier=1).then_inc(made, 1)
            nc.gpsimd.affine_select(out=tri[:], in_=tri[:], compare_op=ALU.is_ge, fill=1.0, base=0,
                                    pattern=[[-1, P]], channel_multiplier=1).then_inc(made, 1)
            nc.gpsimd.iota(precedence[:], pattern=[[-1, NE]], base=NE, channel_multiplier=0,
                           allow_small_or_imprecise_dtypes=True).then_inc(made, 1)
            nc.gpsimd.iota(steps[:], pattern=[[P, TILES]], base=0, channel_multiplier=0,
                           allow_small_or_imprecise_dtypes=True).then_inc(made, 1)
            nc.gpsimd.iota(slots_seq[:], pattern=[[1, SLOT_TILES]], base=0, channel_multiplier=0,
                           allow_small_or_imprecise_dtypes=True).then_inc(made, 1)

            pool.wait_ge(step, SLOTS_AT)
            for t in range(TILES):
                i, tt = divmod(t, TT)
                if tt == 0:
                    wait(pool, scattered[i % 4], 16 * 2 * TT * (i // 4))
                for r in range(2):
                    nc.gpsimd.indirect_dma_start(
                        d["x_rows"], bass.IndirectOffsetOnAxis(slot[:, r, t:t + 1], 0),
                        acc[:, i, tt], None).then_inc(scattered[i % 4], 16)

            for q in range(2):
                pool.wait_ge(y_stored[q], 16 * BODIES)
            for t in range(TILES):
                i, tt = divmod(t, TT)
                if tt == 0 and i >= NG:
                    pool.wait_ge(mixed, (i - NG + 1) * 2 * TT)
                for r in range(2):
                    nc.gpsimd.indirect_dma_start(
                        gathered[:, i % NG, tt, r], None, d["y_rows"],
                        bass.IndirectOffsetOnAxis(slot[:, r, t:t + 1], 0)).then_inc(gathered_in[i % NG], 16)

        MADE = 9

        @block.scalar
        def _(act):
            for i in range(UNITS):
                act.wait_ge(turned, i + 1)
                nc.scalar.copy(x1_t[:, i, 0], turn_ps[:, i % 2, 0]).then_inc(x1_t_act, 1)
            act.wait_ge(logits_ready, UNITS)
            nc.scalar.activation(score[:], logits_ps, ACT.Sigmoid).then_inc(score_ready, 1)
            for i in range(UNITS):
                act.wait_ge(up_ready, i + 1)
                act.wait_ge(step, SLOTS_AT)
                wait(act, hidden_ready, i - 1)
                nc.scalar.activation(silu[:, i % 2], g_ps[:, i % 2], ACT.Silu).then_inc(silu_ready, 1)

            def hidden_t(r, c, k):
                act.wait_ge(ht_made, tile_no(r, c) + 1)
                if k is None or k >= 2:
                    act.wait_ge(y_made, tile_no(r, c) - 1)
                nc.scalar.copy(e_hidden_t[:, c % 2], ht_ps[:, 0, 0:P]).then_inc(ht_ready, 1)

            def program(r, c, k):
                if k is None or k >= 2:
                    hidden_t(r, c - 2, None if k is None else k - 2)
                act.wait_ge(e_up, tile_no(r, c) + 1)
                if k is None or k >= 2:
                    act.wait_ge(e_hidden_ready, tile_no(r, c) - 1)
                nc.scalar.activation(e_silu[:, c % 2], gu_ps[:, c % 2, 0:IF], ACT.Silu).then_inc(e_silu_ready, 1)

            tiles(act, program)
            for k in (SLOT_TILES - 2, SLOT_TILES - 1):
                hidden_t(BODIES - 1, k - (BODIES - 1) * BODY, k)

            for i in range(UNITS):
                act.wait_ge(norm, i * MOE_NORM + 2 * TT + 2)
                nc.scalar.activation(spread[:, i % 2], spread[:, i % 2], ACT.Sqrt).then_inc(std, 1)

        @block.tensor
        def _(pe):
            pe.wait_ge(made, MADE)
            pe.wait_ge(w_in_sem, 16 * len(NAMES))

            def turn(i):
                pe.wait_ge(x1_in[i % 4], 16 * (i // 4 + 1))
                wait(pe, x1_t_act, i - 1)
                wait(pe, x1_t_dve, i - 1)
                for k in range(KT):
                    for tt in range(TT):
                        one = nc.tensor.transpose(turn_ps[:, i % 2, k, tt * P:(tt + 1) * P],
                                                  acc[:, i, tt, k * P:(k + 1) * P], ident[:])
                one.then_inc(turned, 1)

            def logits(i):
                pe.wait_ge(x1_t_act, i + 1)
                pe.wait_ge(x1_t_dve, i + 1)
                for tt in range(TT):
                    o = logits_ps[:, i * TT + tt]
                    nc.tensor.matmul(o, ones[:], b_gate[:], start=True, stop=False)
                    for k in range(KT):
                        one = nc.tensor.matmul(o, x1_t[:, i, k, tt * P:(tt + 1) * P], w_gate[:, k], start=False, stop=(k == KT - 1))
                one.then_inc(logits_ready, 1)

            for i in range(UNITS):
                turn(i)
                if i > 0:
                    logits(i - 1)
            logits(UNITS - 1)

            pe.wait_ge(step, EITHER_AT)
            half = TILES // 2
            for a in range(2):
                nc.tensor.matmul(within_ps[:, a * half:(a + 1) * half], tri[:], either[:, a * half:(a + 1) * half], start=True, stop=True)
            for a in range(2):
                one = nc.tensor.matmul(totals_ps[:, a * half:(a + 1) * half], full[:], either[:, a * half:(a + 1) * half], start=True, stop=True)
            one.then_inc(counted, 1)

            pe.wait_ge(step, SLOTS_AT)

            def down(i):
                pe.wait_ge(hidden_ready, i + 1)
                wait(pe, blended, i)
                for tt in range(TT):
                    one = nc.tensor.matmul(d_ps[:, tt], hidden[:, i % 2, tt * P:(tt + 1) * P], w_down[:, SHARED], start=True, stop=True)
                one.then_inc(down_ready, 1)

            for i in range(UNITS):
                wait(pe, hidden_ready, i - 1)
                for o, at in ((g_ps, 0), (u_ps, IF)):
                    for k in range(KT):
                        one = nc.tensor.matmul(o[:, i % 2], w_up[:, SHARED, k, at:at + IF], x1_t[:, i, k], start=(k == 0), stop=(k == KT - 1))
                one.then_inc(up_ready, 1)
                if i > 0:
                    down(i - 1)
            down(UNITS - 1)

            pe.wait_ge(step, OWNER_AT)
            pe.wait_ge(hidden_ready, UNITS)
            pe.wait_ge(blended, UNITS)

            def turn_slots(r, c, k):
                group = c // GROUP
                if c % GROUP == 0:
                    pe.wait_ge(x_slots_in[group], (r + 1) * 16)
                if k is None or k >= 2:
                    pe.wait_ge(xt_ready, tile_no(r, c) - 1)
                for h in range(KT):
                    one = nc.tensor.transpose(xt_ps[:, c % 2, h * P:(h + 1) * P],
                                              x_slots[:, group, c % GROUP, h * P:(h + 1) * P], ident[:])
                one.then_inc(xt_made, 1)

            def up_slots(r, c, k, e):
                pe.wait_ge(xt_ready, tile_no(r, c) + 1)
                if k is None or k >= 2:
                    pe.wait_ge(e_hidden_ready, tile_no(r, c) - 1)
                for h in range(KT):
                    one = nc.tensor.matmul(gu_ps[:, c % 2, 0:2 * IF], xt[:, c % 4, h * P:(h + 1) * P], w_up[:, e, h], start=(h == 0), stop=(h == KT - 1))
                one.then_inc(e_up, 1)

            def turn_hidden(r, c, k):
                pe.wait_ge(e_hidden_ready, tile_no(r, c) + 1)
                if k is None or k >= 1:
                    pe.wait_ge(ht_ready, tile_no(r, c))
                nc.tensor.transpose(ht_ps[:, 0, 0:P], e_hidden[:, c % 2], ident[:]).then_inc(ht_made, 1)

            def down_slots(r, c, k, e):
                pe.wait_ge(ht_ready, tile_no(r, c) + 1)
                if k is None or k >= 2:
                    pe.wait_ge(y_ready, tile_no(r, c) - 1)
                nc.tensor.matmul(y_ps[:, c % 2, 0:DM], e_hidden_t[:, c % 2], w_down[:, e], start=True, stop=True).then_inc(y_made, 1)

            def expert(r, c):
                return pe.value_load(owner[0:1, bass.ds(tile_no(r, c), 1)] if not isinstance(r, int)
                                     else owner[0:1, tile_no(r, c):tile_no(r, c) + 1], min_val=0, max_val=NE - 1)

            def body(r, k0):
                owners = {c: expert(r, c) for c in range(-2 if k0 != 0 else 0, BODY)}
                for c in range(BODY):
                    k = None if k0 is None else k0 + c
                    old = None if k0 is None else k - 2
                    if old is None or old >= 0:
                        turn_hidden(r, c - 2, old)
                    if k is None or k + 1 < SLOT_TILES:
                        if c + 1 < BODY:
                            turn_slots(r, c + 1, None if k is None else k + 1)
                        else:
                            turn_slots(r + 1, 0, None if k is None else k + 1)
                    up_slots(r, c, k, owners[c])
                    if old is None or old >= 0:
                        down_slots(r, c - 2, old, owners[c - 2])

            turn_slots(0, 0, 0)
            body(0, 0)
            with pe.Fori(1, BODIES - 1) as r:
                body(r, None)
            body(BODIES - 1, (BODIES - 1) * BODY)
            for k in (SLOT_TILES - 2, SLOT_TILES - 1):
                c = k - (BODIES - 1) * BODY
                turn_hidden(BODIES - 1, c, k)
                down_slots(BODIES - 1, c, k, expert(BODIES - 1, c))

        @block.vector
        def _(dve):
            AX = mybir.AxisListType.X
            V = nc.vector
            dve.wait_ge(made, MADE)
            for i in range(UNITS):
                dve.wait_ge(turned, i + 1)
                V.tensor_copy(x1_t[:, i, 1], turn_ps[:, i % 2, 1]).then_inc(x1_t_dve, 1)

            done_steps = [0]

            def done(one):
                one.then_inc(step, 1)
                done_steps[0] += 1
                dve.wait_ge(step, done_steps[0])

            def over_experts(v):
                return v.unsqueeze(2).to_broadcast([P, TILES, NE])

            def over_tiles(v):
                return v.unsqueeze(1).to_broadcast([P, TILES, NE])

            dve.wait_ge(score_ready, 1)
            for r in range(2):
                done(V.tensor_reduce(best[:, r], score[:], AX, ALU.max))
                done(V.tensor_tensor(rank[:], score[:], over_experts(best[:, r]), ALU.is_equal))
                done(V.tensor_tensor(rank[:], rank[:], over_tiles(precedence[:]), ALU.mult))
                done(V.tensor_reduce(first_rank[:], rank[:], AX, ALU.max))
                done(V.tensor_tensor(chosen[:, r], rank[:], over_experts(first_rank[:]), ALU.is_equal))
                if r == 0:
                    done(V.scalar_tensor_tensor(out=score[:], in0=chosen[:, 0], scalar=-2.0, in1=score[:],
                                                op0=ALU.mult, op1=ALU.add))
            done(V.tensor_tensor(either[:], chosen[:, 0], chosen[:, 1], ALU.add))
            assert done_steps[0] == EITHER_AT
            done(V.tensor_tensor(first_rank[:], best[:, 0], best[:, 1], ALU.add))
            done(V.reciprocal(first_rank[:], first_rank[:]))
            for r in range(2):
                done(V.tensor_tensor(best[:, r], best[:, r], first_rank[:], ALU.mult))

            by_expert = score[:].rearrange("p a b -> p (a b)").rearrange("p (e t) -> p e t", e=NE)
            table = rank[:].rearrange("p a b -> p (a b)").rearrange("p (e t) -> p e t", e=NE)
            done(V.memset(table, 1.0))
            done(V.memset(table[:, :, 0:1], 0.0))
            dve.wait_ge(counted, 1)
            done(V.tensor_copy(by_expert, totals_ps.rearrange("p t e -> p e t")))
            done(V.tensor_tensor_scan(score[:].rearrange("p a b -> p (a b)"), rank[:].rearrange("p a b -> p (a b)"),
                                      score[:].rearrange("p a b -> p (a b)"), 0.0, ALU.mult, ALU.add))
            done(V.tensor_tensor(table, by_expert[:, :, TILES - 1:TILES].to_broadcast([P, NE, TILES]),
                                 steps[:].unsqueeze(1).to_broadcast([P, NE, TILES]), ALU.is_gt))
            done(V.tensor_reduce(used[:], table, AX, ALU.add))
            done(V.memset(used_end[:], 1.0))
            done(V.tensor_tensor_scan(used_end[:], used_end[:], used[:], 0.0, ALU.mult, ALU.add))
            done(V.tensor_tensor(used[:], used_end[:], used[:], ALU.subtract))
            done(V.tensor_scalar(used[:], used[:], float(P), None, ALU.mult))
            cand = rank[:]
            done(V.tensor_tensor(cand, score[:].rearrange("p a b -> p (a b)").rearrange("p (e t) -> p t e", e=NE), totals_ps, ALU.subtract))
            done(V.tensor_tensor(cand, cand, within_ps, ALU.add))
            done(V.tensor_tensor(cand, cand, over_tiles(used[:]), ALU.add))
            for r in range(2):
                done(V.tensor_tensor(chosen[:, r], chosen[:, r], cand, ALU.mult))
                done(V.tensor_reduce(slot_f[:, r], chosen[:, r], AX, ALU.add))
            done(V.tensor_copy(slot[:], slot_f[:]))
            assert done_steps[0] == SLOTS_AT, done_steps
            runs = rank[0:1, 0:OWNER_PART]
            for part in range(SLOT_TILES // OWNER_PART):
                at = slice(part * OWNER_PART, (part + 1) * OWNER_PART)
                done(V.tensor_tensor(runs, used_end[0:1].unsqueeze(1).to_broadcast([1, OWNER_PART, NE]),
                                     slots_seq[:, at].unsqueeze(2).to_broadcast([1, OWNER_PART, NE]), ALU.is_le))
                done(V.tensor_reduce(owner_f[:, at], runs, AX, ALU.add))
            done(V.tensor_scalar(owner_f[:], owner_f[:], float(NE - 1), None, ALU.min))
            done(V.tensor_copy(owner[:], owner_f[:]))
            assert done_steps[0] == OWNER_AT, done_steps

            def blend_shared(i):
                dve.wait_ge(down_ready, i + 1)
                dve.wait_ge(scattered[i % 4], 16 * 2 * TT * (i // 4 + 1))
                V.scalar_tensor_tensor(out=acc[:, i], in0=acc[:, i], scalar=2.0, in1=d_ps, op0=ALU.mult,
                                       op1=ALU.add).then_inc(blended, 1)

            for i in range(UNITS):
                dve.wait_ge(silu_ready, i + 1)
                dve.wait_ge(up_ready, i + 1)
                wait(dve, down_ready, i - 1)
                V.tensor_tensor(hidden[:, i % 2], silu[:, i % 2], u_ps[:, i % 2], ALU.mult).then_inc(hidden_ready, 1)
                if i > 0:
                    blend_shared(i - 1)
            blend_shared(UNITS - 1)

            def take_turned(r, c, k):
                dve.wait_ge(xt_made, tile_no(r, c) + 1)
                if k is None or k >= 4:
                    dve.wait_ge(e_up, tile_no(r, c) - 3)
                V.tensor_copy(xt[:, c % 4], xt_ps[:, c % 2, 0:DM]).then_inc(xt_ready, 1)

            def gate_hidden(r, c, k):
                dve.wait_ge(e_silu_ready, tile_no(r, c) + 1)
                if k is None or k >= 2:
                    dve.wait_ge(ht_made, tile_no(r, c) - 1)
                V.tensor_tensor(e_hidden[:, c % 2], e_silu[:, c % 2], gu_ps[:, c % 2, IF:2 * IF], ALU.mult).then_inc(e_hidden_ready, 1)

            def take_y(r, c, k):
                group = c // GROUP if c >= 0 else 1
                dve.wait_ge(y_made, tile_no(r, c) + 1)
                if c % GROUP == 0 and (k is None or k >= BODY):
                    dve.wait_ge(y_stored[group], (r if c >= 0 else r - 1) * 16)
                V.tensor_copy(y_slots[:, group, c % GROUP], y_ps[:, c % 2, 0:DM]).then_inc(y_ready, 1)

            def program(r, c, k):
                if k is None or k + 1 < SLOT_TILES:
                    if c + 1 < BODY:
                        take_turned(r, c + 1, None if k is None else k + 1)
                    else:
                        take_turned(r + 1, 0, None if k is None else k + 1)
                gate_hidden(r, c, k)
                if k is None or k >= 2:
                    take_y(r, c - 2, None if k is None else k - 2)

            take_turned(0, 0, 0)
            tiles(dve, program)
            for k in (SLOT_TILES - 2, SLOT_TILES - 1):
                take_y(BODIES - 1, k - (BODIES - 1) * BODY, k)

            def stage5(i):
                q = i % 2
                at = i * MOE_NORM
                dve.wait_ge(gathered_in[i % NG], 16 * 2 * TT * (i // NG + 1))
                for r in range(2):
                    wait(dve, mixed, i * 2 * TT + r * TT)
                    for tt in range(TT):
                        V.scalar_tensor_tensor(out=acc[:, i, tt], in0=gathered[:, i % NG, tt, r],
                                               scalar=best[:, r, i * TT + tt:i * TT + tt + 1], in1=acc[:, i, tt],
                                               op0=ALU.mult, op1=ALU.add).then_inc(mixed, 1)
                dve.wait_ge(mixed, (i + 1) * 2 * TT)
                for tt in range(TT):
                    V.bn_stats(stats[:, q, tt], acc[:, i, tt]).then_inc(norm, 1)
                dve.wait_ge(norm, at + TT)
                V.memset(spread[:, q], EPS).then_inc(norm, 1)
                for tt in range(TT):
                    V.bn_aggr(mean_var[:, q, tt], stats[:, q, tt]).then_inc(norm, 1)
                dve.wait_ge(norm, at + 2 * TT + 1)
                V.tensor_tensor(spread[:, q], spread[:, q], mean_var[:, q, :, 1], ALU.add).then_inc(norm, 1)
                dve.wait_ge(std, i + 1)
                V.reciprocal(spread[:, q], spread[:, q]).then_inc(norm, 1)
                dve.wait_ge(norm, at + 2 * TT + 3)
                for tt in range(TT):
                    row = acc[:, i, tt]
                    V.tensor_scalar(row, row, mean_var[:, q, tt, 0:1], spread[:, q, tt:tt + 1], ALU.subtract,
                                    ALU.mult).then_inc(norm, 1)

            for i in range(UNITS):
                stage5(i)


def kernel(**inputs):
    import numpy as np
    import concourse.bacc as bacc
    from concourse.bass_utils import run_bass_kernel_spmd

    g = {k: np.asarray(v) for k, v in inputs.items()}

    def chunks(v):
        v = v.reshape((v.shape[0] // P, P) + v.shape[1:])
        return v.swapaxes(0, 1)

    x = g["L0_attn_x"].reshape(NB, NW, T, DM).swapaxes(0, 1).reshape(UNITS, T, DM)
    x_proj = g["L0_attn_x_proj_w"].T
    laid = {
        "x_t": x.transpose(0, 2, 1).reshape(UNITS, KT, P, T).swapaxes(1, 2),
        "x_tok": x.reshape(UNITS, TT, P, DM).swapaxes(1, 2),
        "w_in": chunks(g["L0_attn_in_proj_w"].T),
        "b_in": chunks(g["L0_attn_in_proj_b"]),
        "taps": chunks(g["L0_attn_conv_w"]),
        "b_conv": chunks(g["L0_attn_conv_b"]),
        "a_log": chunks(g["L0_attn_A_log"].T),
        "d_skip": chunks(g["L0_attn_D"]),
        "w_x": chunks(np.concatenate([x_proj[:, :RANK]] + [x_proj[:, RANK:]] * 4, axis=1)),
        "w_dt": g["L0_attn_dt_proj_w"].T,
        "b_dt": chunks(g["L0_attn_dt_proj_b"]),
        "w_out": chunks(g["L0_attn_out_proj_w"].T),
        "b_out": g["L0_attn_out_proj_b"][None],
    }
    laid.update(moe_layout(g, chunks))
    laid = {k: np.ascontiguousarray(v) for k, v in laid.items()}

    nc = bacc.Bacc("TRN2", target_bir_lowering=False, num_devices=1)
    d = {k: nc.dram_tensor(f"in_{k}", v.shape, mybir.dt.from_np(v.dtype), kind="ExternalInput").ap()
         for k, v in laid.items()}
    d["out"] = nc.dram_tensor("out", (UNITS, P, TT, DM), F32, kind="ExternalOutput").ap()
    d["x1"] = nc.dram_tensor("x1", (UNITS, P, TT, DM), F32, kind="Internal").ap()
    for name in ("x", "y"):
        rows = nc.dram_tensor(f"{name}_rows", (SLOT_TILES * P, DM), F32, kind="Internal").ap()
        d[f"{name}_rows"] = rows
        d[f"{name}_slots"] = rows.rearrange("(s p) f -> p s f", p=P)
    mamba(nc, d)
    moe(nc, d)
    r = run_bass_kernel_spmd(nc, [{f"in_{k}": v for k, v in laid.items()}], core_ids=[0])
    out = np.asarray(r.results[0]["out"])
    return out.swapaxes(1, 2).reshape(NW, NB, T, DM).swapaxes(0, 1).reshape(NB, L, DM)
```

```python
from contextlib import ExitStack

import concourse.bass as bass
from concourse import mybir

F32 = mybir.dt.float32
BF16 = mybir.dt.bfloat16
U32 = mybir.dt.uint32
ALU = mybir.AluOpType
ACT = mybir.ActivationFunctionType

P = 128
T = 512
NB, L, DM = 4, 2048, 256
NW = L // T
UNITS = NB * NW
DI = 512
CH = DI // P
KT = DM // P
NS = 16
TAPS = 4
HALO = TAPS - 1
RANK = 64
TT = T // P
EPS = 1e-5
NE = 16
IF = 128

ROOT_SCALE = 0.5170210782894934
LOG1P = ((-1.2051646770627222, 0.11629121211354453), (0.5217478157878973, 0.2974565636862504),
         (-0.7402138145551652, 0.7266668451772348), (-0.04424682055460984, 0.8759711051528496))
FACTORS = len(LOG1P)
LOGS = 4 * FACTORS
NORM = 16
POOL_HC = (1, 3, 5, 8, 10, 12)


ITEMS = CH * NS
HS = 8
HCS = 4
LAG = 3
LEAD = 4
QUAD = 2

def count(unit, per, add):
    j, k = unit
    return per * k + add if isinstance(j, int) and j == 0 else j * (2 * per) + (per * k + add)


def number(unit):
    return count(unit, 1, 0)


def loads(unit):
    j, k = unit
    return 16 * (k // 2 + 1) if isinstance(j, int) else j * 16 + 16 * (k // 2 + 1)


def later(unit, n=1):
    return (unit[0], unit[1] + n)


def batch(unit):
    j, k = unit
    if isinstance(j, int):
        return k % NB
    half = j % 2
    return half * 2 + k if k < 2 else half * (-2) + k


def wait(eng, sem, value):
    if not isinstance(value, int) or value > 0:
        eng.wait_ge(sem, value)


def mamba(nc, d):
    with ExitStack() as ctx:
        def sb(name, shape, dt=F32):
            return ctx.enter_context(nc.sbuf_tensor(name, shape, dt))

        def psum(name, shape):
            return ctx.enter_context(nc.psum_tensor(name, shape, F32))

        def sem(name):
            return ctx.enter_context(nc.semaphore(name))

        w_in = sb("w_in", [P, KT, 2 * DI])
        w_x = sb("w_x", [P, CH, RANK + P])
        w_dt = sb("w_dt", [RANK, DI])
        w_out = sb("w_out", [P, CH, DM])
        b_out = sb("b_out", [1, DM])
        b_in = sb("b_in", [P, 2 * CH])
        taps = sb("taps", [P, CH, TAPS])
        b_conv = sb("b_conv", [P, CH])
        d_skip = sb("d_skip", [P, CH])
        b_dt = sb("b_dt", [P, CH])
        a_log = sb("a_log", [P, CH, NS])
        a_mat = sb("a_mat", [P, CH, NS])
        a_big = sb("a_big", [P, CH, NS])
        a_inv = sb("a_inv", [P, CH, NS])
        ident = sb("ident", [P, P])
        ones = sb("ones", [1, P])
        zeros = sb("zeros", [P, DM])
        shifts = sb("shifts", [P, FACTORS])
        pick = sb("pick", [P, 2 * NS], BF16)
        dg_inv = sb("dg_inv", [P, CH, len(POOL_HC), P])
        dg_tap = sb("dg_tap", [P, CH, TAPS, P])
        dg_skip = sb("dg_skip", [P, CH, P])
        carry = sb("carry", [P, NB, CH, NS])
        halo = sb("halo", [P, NB, CH, HALO])

        x_t = sb("x_t", [P, 2, KT, T])
        x_tok = sb("x_tok", [P, TT, DM])
        x_in = sb("x_in", [P, CH, HALO + T])
        x_conv = sb("x_conv", [P, 2, CH, T])
        dt = sb("dt", [P, 2, CH, T])
        gate = sb("gate", [P, CH, T])
        poly = sb("poly", [P, 2, T])
        square = sb("square", [P, 2, T])
        rest = poly[:, 0]
        dt_low = poly[0:RANK, 1]
        parts = sb("parts", [P, 2, T], BF16)
        y_gated = sb("y_gated", [P, CH, T])
        stats = sb("stats", [P, TT, 6])
        mean_var = sb("mean_var", [P, TT, 2])
        spread = sb("spread", [P, TT])

        h = sb("h", [P, HS, T])
        hc = sb("hc", [P, HCS, T])
        b_rep = sb("b_rep", [P, NS, T])
        c_rep = sb("c_rep", [P, len(POOL_HC), T])

        y_ps = psum("y_ps", [P, 2, T])
        a_ps = psum("a_ps", [P, 2, T])
        work = psum("work", [P, 2, T])
        c_ps = psum("c_ps", [P, 2, T])

        weights_in = sem("weights_in")
        x_t_in = [sem(f"x_t_in{q}") for q in range(2)]
        x_tok_in = sem("x_tok_in")
        x1_out = sem("x1_out")
        slots_zeroed = sem("slots_zeroed")
        ident_ready = sem("ident_ready")
        pick_ready = sem("pick_ready")
        zeroed = sem("zeroed")
        shifts_ready = sem("shifts_ready")
        a_exp = sem("a_exp")
        a_inv_step = sem("a_inv_step")
        diags_ready = sem("diags_ready")
        filled = [sem(f"work_filled{q}") for q in range(2)]
        emptied = [sem(f"work_emptied{q}") for q in range(2)]
        halo_moved = sem("halo_moved")
        x_conv_ready = sem("x_conv_ready")
        gate_ready = sem("gate_ready")
        abs_done = sem("abs_done")
        exp_neg_ready = sem("exp_neg_ready")
        square_ready = sem("square_ready")
        softplus_step = sem("softplus_step")
        high_ready = sem("high_ready")
        split_step = sem("split_step")
        dt_ready = sem("dt_ready")
        u_ready = sem("u_ready")
        a_ready = sem("a_ready")
        b_ready = sem("b_ready")
        scanned = sem("scanned")
        summed = sem("summed")
        c_ready = sem("c_ready")
        hc_vector = sem("hc_vector")
        hc_pool = sem("hc_pool")
        carried = sem("carried")
        gated = sem("gated")
        norm_step = sem("norm_step")
        std_ready = sem("std_ready")

        NP, NV = CH * len(POOL_HC), CH * (NS - len(POOL_HC))

        def on_pool(m):
            return m % NS in POOL_HC

        def pool_before(m):
            return sum(on_pool(k) for k in range(m))

        def vector_before(m):
            return m - pool_before(m)

        PARTS = {"x": 2, "o": 4, "c": 4, "dl": 4, "bc": 4}
        last_chunk = ITEMS - NS
        PLACE = [("x0", 0), ("x1", 2), ("x2", 4), ("x3", 6), ("o0", 8), ("o1", 12), ("c0", 16), ("c1", 20),
                 ("c2", 24), ("c3", 28), ("dl", 35), ("bc", 39), ("d0", 43), ("d1", 44), ("d2", 45), ("d3", 46)]
        PLACE += sorted([("z3", 47), ("z0", 50), ("z1", 54), ("z2", 58)] +
                        [(f"B{s}", last_chunk + s) for s in range(NS)] +
                        [(f"C{s}", last_chunk + 3 + s) for s in POOL_HC], key=lambda t: t[1])
        WHERE = dict(PLACE)

        def parts_of(t):
            return PARTS.get(t if t in ("dl", "bc") else t[0], 1)

        class Plan:

            def __init__(self, kinds, offset, per=0):
                self.tiles = [t for t, _ in PLACE if t[0] in kinds or t in kinds]
                self.offset, self.per = offset, per

            def parts_at(self, m):
                return [(t, m - WHERE[t]) for t in self.tiles if 0 <= m - WHERE[t] < parts_of(t)]

            def whole_at(self, m):
                return [t for t in self.tiles if m - WHERE[t] == parts_of(t) - 1]

            def has(self, tile):
                return tile in self.tiles

            def bank(self, tile):
                return (self.offset + self.tiles.index(tile)) % 2

            def before(self, tile, unit):
                n = (self.offset + self.tiles.index(tile)) // 2
                return count(unit, self.per // 2, n) if self.per else n

        PREP = ["x", "c", "dl", "bc", "d", "B", "C", "z0", "z1", "z2"]
        FIRST = len(Plan(PREP, 0).tiles)
        INNER = FIRST + 3
        first = Plan(PREP, 0)
        second = Plan(PREP + ["z3"], FIRST)
        inner = Plan(PREP + ["z3", "o"], FIRST - 2, INNER)
        last = Plan(["z3", "o"], FIRST - 2 + INNER * (UNITS - 1))
        final = Plan(["o"], FIRST + 1 + INNER * (UNITS - 1))
        assert INNER % 2 == 0

        def emptied_all(eng, plan, unit, tiles):
            most = {}
            for t in tiles:
                most[plan.bank(t)] = t
            for bank, t in most.items():
                eng.wait_ge(emptied[bank], plan.before(t, unit) + 1)

        def hc_wait(eng, unit, m):
            if on_pool(m):
                eng.wait_ge(hc_pool, count(unit, NP, pool_before(m) + 1))
            else:
                eng.wait_ge(hc_vector, count(unit, NV, vector_before(m) + 1))

        def before(unit, m, n):
            return (unit, m - n) if m >= n else (later(unit, -1), m - n + ITEMS)

        def after(unit, m, n):
            return (unit, m + n) if m + n < ITEMS else (later(unit), m + n - ITEMS)

        def row_ready(eng, unit, tile):
            if isinstance(unit[0], int) and unit[1] == 0:
                emptied_all(eng, first, (0, -1), [tile])
            else:
                emptied_all(eng, inner, later(unit, -1), [tile])

        def whole(eng, unit_program):
            unit_program((0, 0), second)
            with eng.Fori(0, (UNITS - 2) // 2) as j:
                unit_program((j, 1), inner)
                unit_program((j, 2), inner)
            unit_program((0, UNITS - 1), last)

        WEIGHTS = ["w_in", "w_x", "w_dt", "w_out", "b_out", "b_in", "taps", "b_conv", "d_skip", "b_dt", "a_log"]
        holders = dict(w_in=w_in, w_x=w_x, w_dt=w_dt, w_out=w_out, b_out=b_out, b_in=b_in, taps=taps,
                       b_conv=b_conv, d_skip=d_skip, b_dt=b_dt, a_log=a_log)
        ALL_WEIGHTS = 16 * len(WEIGHTS)
        ADD_RELU_AT = (54, 58, 63)
        x_arg = x_in[:, :, HALO:]

        block = ctx.enter_context(nc.Block())

        @block.sync
        def _(sp):
            sp.dma_start(x_t[:, 0], d["x_t"][0]).then_inc(x_t_in[0], 16)
            for name in WEIGHTS:
                sp.dma_start(holders[name][:], d[name]).then_inc(weights_in, 16)
            sp.dma_start(x_tok[:], d["x_tok"][0]).then_inc(x_tok_in, 16)

            ZERO = SLOT_TILES // UNITS

            def unit_program(u, plan):
                nq = (u[1] + 1) % 2
                if plan is second:
                    sp.wait_ge(zeroed, 6)
                sp.dma_start(d["x_slots"][:, bass.ds(number(u) * ZERO, ZERO)],
                             zeros[:].unsqueeze(1).to_broadcast([P, ZERO, DM])).then_inc(slots_zeroed, 16)
                if plan is not last:
                    if plan is not second:
                        prev = later(u, -1)
                        sp.wait_ge(emptied[inner.bank("z3")], inner.before("z3", prev) + 1)
                    sp.dma_start(x_t[:, nq], d["x_t"][number(later(u))]).then_inc(x_t_in[nq], 16)
                if plan is not second:
                    sp.wait_ge(norm_step, count(u, NORM, 0))
                    sp.dma_start(d["x1"][number(later(u, -1))], x_tok[:]).then_inc(x1_out, 16)
                    sp.wait_ge(x1_out, count(u, 16, 0))
                    sp.dma_start(x_tok[:], d["x_tok"][number(u)]).then_inc(x_tok_in, 16)

            whole(sp, unit_program)
            sp.wait_ge(norm_step, NORM * UNITS)
            sp.dma_start(d["x1"][UNITS - 1], x_tok[:]).then_inc(x1_out, 16)
            sp.wait_ge(x1_out, 16 * UNITS)
            sp.wait_ge(slots_zeroed, 16 * UNITS)

        @block.gpsimd
        def _(pool):
            nc.gpsimd.memset(ident[:], 0.0).then_inc(zeroed, 1)
            nc.gpsimd.memset(pick[:], 0.0).then_inc(zeroed, 1)
            nc.gpsimd.memset(ones[:], 1.0).then_inc(zeroed, 1)
            nc.gpsimd.memset(carry[:], 0.0).then_inc(zeroed, 1)
            nc.gpsimd.memset(halo[:], 0.0).then_inc(zeroed, 1)
            nc.gpsimd.memset(zeros[:], 0.0).then_inc(zeroed, 1)
            pool.wait_ge(zeroed, 6)
            for k, (shift, _) in enumerate(LOG1P):
                nc.gpsimd.memset(shifts[:, k:k + 1], shift).then_inc(shifts_ready, 1)
            nc.gpsimd.affine_select(out=ident[:], in_=ident[:], compare_op=ALU.not_equal, fill=1.0, base=0,
                                    pattern=[[-1, P]], channel_multiplier=1).then_inc(ident_ready, 1)
            for n, row in enumerate((0, 64, 96)):
                wait(pool, pick_ready, n)
                nc.gpsimd.affine_select(out=pick[:], in_=pick[:], compare_op=ALU.not_equal, fill=1.0, base=-row,
                                        pattern=[[-1, 2 * NS]], channel_multiplier=1).then_inc(pick_ready, 1)

            def make_u(u, m):
                c, s = divmod(m, NS)
                if m == 0:
                    pool.wait_ge(x_conv_ready, count(u, 2, 2))
                if c == 0:
                    row_ready(pool, u, f"B{s}")
                if u[1] > 0 or m >= HS:
                    ou, om = before(u, m, HS)
                    hc_wait(pool, ou, om)
                    pool.wait_ge(carried, count(ou, ITEMS // QUAD, om // QUAD + 1))
                nc.gpsimd.tensor_tensor(h[:, m % HS], x_conv[:, u[1] % 2, c], b_rep[:, s], ALU.mult).then_inc(u_ready, 1)

            def make_hc(u, m):
                n = POOL_HC.index(m % NS)
                pool.wait_ge(scanned, count(u, ITEMS, m + 1))
                if m < NS:
                    row_ready(pool, u, f"C{m}")
                wait(pool, summed, count(u, ITEMS, m - HCS + 1))
                nc.gpsimd.tensor_tensor(hc[:, m % HCS], h[:, m % HS], c_rep[:, n], ALU.mult).then_inc(hc_pool, 1)

            def add_relu(u, c):
                n, nq = later(u), (u[1] + 1) % 2
                pool.wait_ge(softplus_step, count(n, LOGS, (c + 1) * FACTORS))
                nc.gpsimd.tensor_tensor(dt[:, nq, c], dt[:, nq, c], poly[:, c % 2], ALU.add).then_inc(dt_ready, 1)

            def unit_program(u, plan):
                for m in range(ITEMS):
                    nu, nm = after(u, m, LEAD)
                    if not (plan is last and m + LEAD >= ITEMS):
                        make_u(nu, nm)
                    pu, pm = before(u, m, 1)
                    if on_pool(pm) and not (plan is second and m == 0):
                        make_hc(pu, pm)
                    if plan is not last and m in ADD_RELU_AT:
                        add_relu(u, ADD_RELU_AT.index(m))
                    if plan is not second and m == 3:
                        add_relu(later(u, -1), CH - 1)

            for c in range(CH):
                add_relu((0, -1), c)
            for m in range(LEAD):
                make_u((0, 0), m)
            whole(pool, unit_program)

        @block.scalar
        def _(act):
            act.wait_ge(weights_in, ALL_WEIGHTS)
            nc.scalar.activation(a_mat[:], a_log[:], ACT.Exp).then_inc(a_exp, 1)

            def make_a(u, m):
                c, s = divmod(m, NS)
                if s == 0:
                    act.wait_ge(dt_ready, count(u, CH, c + 1))
                wait(act, scanned, count(u, ITEMS, m - 1))
                nc.scalar.activation(a_ps[:, m % 2], dt[:, u[1] % 2, c], ACT.Exp,
                                     scale=a_mat[:, c, s:s + 1]).then_inc(a_ready, 1)

            def tile(u, plan, t):
                n, nq = later(u), (u[1] + 1) % 2
                bank = plan.bank(t)
                kind = t[0]
                if t in ("dl", "bc"):
                    act.wait_ge(filled[bank], plan.before(t, u) + 1)
                    if t == "dl":
                        wait(act, dt_ready, count(n, CH, 0))
                        nc.scalar.activation(dt_low, work[0:RANK, bank], ACT.Copy).then_inc(emptied[bank], 1)
                    else:
                        nc.scalar.activation(parts[:, nq], work[:, bank], ACT.Copy).then_inc(high_ready, 1)
                    return
                c = int(t[1:])
                if kind == "B":
                    act.wait_ge(filled[bank], plan.before(t, u) + 1)
                    wait(act, u_ready, count(n, ITEMS, c + 1 - NS))
                    nc.scalar.activation(b_rep[:, c], work[:, bank], ACT.Copy).then_inc(emptied[bank], 1)
                elif kind == "C":
                    k = POOL_HC.index(c)
                    act.wait_ge(filled[bank], plan.before(t, u) + 1)
                    wait(act, hc_pool, count(n, NP, k + 1 - len(POOL_HC)))
                    nc.scalar.activation(c_rep[:, k], work[:, bank], ACT.Copy).then_inc(emptied[bank], 1)
                elif kind == "x":
                    act.wait_ge(filled[bank], plan.before(t, u) + 1)
                    wait(act, softplus_step, count(n, LOGS, 0))
                    nc.scalar.activation(x_in[:, c, HALO:], work[:, bank], ACT.Identity,
                                         bias=b_in[:, c:c + 1]).then_inc(emptied[bank], 1)
                elif kind == "c":
                    act.wait_ge(filled[bank], plan.before(t, u) + 1)
                    if c == 0:
                        wait(act, u_ready, count(u, ITEMS, 0))
                    nc.scalar.activation(x_conv[:, nq, c], work[:, bank], ACT.Identity,
                                         bias=b_conv[:, c:c + 1]).then_inc(emptied[bank], 1)
                elif kind == "z":
                    act.wait_ge(filled[bank], plan.before(t, u) + 1)
                    wait(act, gated, count(u if c == CH - 1 else n, CH, c + 1 - CH))
                    nc.scalar.activation(gate[:, c], work[:, bank], ACT.Identity,
                                         bias=b_in[:, CH + c:CH + c + 1]).then_inc(emptied[bank], 1)
                elif kind == "d":
                    act.wait_ge(filled[bank], plan.before(t, u) + 1)
                    if c == 0:
                        wait(act, a_ready, count(u, ITEMS, 0))
                        act.wait_ge(halo_moved, count(n, 2, 2))
                    nc.scalar.activation(x_arg[:, c], work[:, bank], ACT.Abs, bias=b_dt[:, c:c + 1]).then_inc(abs_done, 1)
                    nc.scalar.activation(dt[:, nq, c], work[:, bank], ACT.Relu,
                                         bias=b_dt[:, c:c + 1]).then_inc(emptied[bank], 1)

            def exp_neg(u, c):
                n = later(u)
                act.wait_ge(abs_done, count(n, CH, c + 1))
                nc.scalar.activation(x_arg[:, c], x_arg[:, c], ACT.Exp, scale=-1.0).then_inc(exp_neg_ready, 1)

            def squared(u, f):
                n = later(u)
                c, k = divmod(f, FACTORS)
                act.wait_ge(exp_neg_ready, count(n, CH, c + 1))
                wait(act, softplus_step, count(n, LOGS, f - 1))
                nc.scalar.activation(square[:, f % 2], x_arg[:, c], ACT.Square, scale=ROOT_SCALE,
                                     bias=shifts[:, k:k + 1]).then_inc(square_ready, 1)

            def root(pu):
                act.wait_ge(norm_step, count(pu, NORM, 11))
                nc.scalar.activation(spread[:], spread[:], ACT.Sqrt).then_inc(std_ready, 1)

            def weave(u, plan, m):
                n, nq = later(u), (u[1] + 1) % 2
                for t in plan.whole_at(m):
                    if t[0] != "o":
                        tile(u, plan, t)
                if plan.has("c0") and m in (26, 32):
                    half = (m - 26) // 6 * 2
                    emptied_all(act, plan, u, [f"c{c}" for c in (half, half + 1)])
                    two = x_conv[:, nq, half:half + 2]
                    nc.scalar.activation(two, two, ACT.Silu).then_inc(x_conv_ready, 1)
                if m == 18 and plan.has("o0"):
                    root(later(u, -1))
                if plan.has("d0"):
                    if 44 <= m < 44 + CH:
                        exp_neg(u, m - 44)
                    if 46 <= m < 46 + LOGS:
                        squared(u, m - 46)
                if m == 56 and plan.has("z0"):
                    emptied_all(act, plan, u, ["z0", "z1"])
                    nc.scalar.activation(gate[:, 0:2], gate[:, 0:2], ACT.Silu).then_inc(gate_ready, 1)
                if m == 60:
                    news = [z for z in ("z2", "z3") if plan.has(z)]
                    emptied_all(act, plan, u, news)
                    two = gate[:, int(news[0][1]):int(news[-1][1]) + 1]
                    nc.scalar.activation(two, two, ACT.Silu).then_inc(gate_ready, 2 if plan is last else 1)

            def unit_program(u, plan):
                for m in range(ITEMS):
                    nu, nm = after(u, m, 2)
                    if not (plan is last and m + 2 >= ITEMS):
                        make_a(nu, nm)
                    weave(u, plan, m)

            for m in range(ITEMS):
                weave((0, -1), first, m)
            act.wait_ge(a_inv_step, 5)
            for m in range(2):
                make_a((0, 0), m)
            whole(act, unit_program)
            root((0, UNITS - 1))

        @block.tensor
        def _(pe):
            pe.wait_ge(weights_in, ALL_WEIGHTS)
            pe.wait_ge(diags_ready, 1)
            pe.wait_ge(pick_ready, 3)

            def replicate(dst, q, row):
                return nc.tensor.matmul(dst, pick[:, row:row + 1].to_broadcast([P, P]), parts[:, q], start=True, stop=True)

            def make_c(u, m):
                n = vector_before(m)
                if m < NS:
                    pe.wait_ge(split_step, count(u, 2, 2))
                wait(pe, hc_vector, count(u, NV, n - 1))
                replicate(c_ps[:, n % 2], u[1] % 2, NS + m % NS).then_inc(c_ready, 1)

            def add_item(u, m):
                c, s = divmod(m, NS)
                if s == 0:
                    wait(pe, gated, count(u, CH, c - 1))
                    if c == 0:
                        pe.wait_ge(x_conv_ready, count(u, 2, 2))
                    nc.tensor.matmul(y_ps[:, c % 2], dg_skip[:, c], x_conv[:, u[1] % 2, c], start=True, stop=False)
                hc_wait(pe, u, m)
                by = dg_inv[:, c, POOL_HC.index(s)] if on_pool(m) else ident[:]
                nc.tensor.matmul(y_ps[:, c % 2], by, hc[:, m % HCS], start=False,
                                 stop=(s == NS - 1)).then_inc(summed, 1)

            def tile(u, plan, t, part):
                n, q, nq = later(u), u[1] % 2, (u[1] + 1) % 2
                bank = plan.bank(t)
                if part == 0:
                    wait(pe, emptied[bank], plan.before(t, u))
                out = work[:, bank]
                if t[0] in "BC":
                    if t == "B0":
                        pe.wait_ge(split_step, count(n, 2, 2))
                    mm = replicate(out, nq, int(t[1:]) + (NS if t[0] == "C" else 0))
                elif t[0] == "x":
                    if t == "x0" and part == 0:
                        pe.wait_ge(x_t_in[nq], loads(n))
                    m, k = int(t[1]), part
                    mm = nc.tensor.matmul(out, w_in[:, k, m * P:(m + 1) * P], x_t[:, nq, k], start=(k == 0), stop=(k == KT - 1))
                elif t[0] == "z":
                    m = int(t[1]) + CH
                    src = q if t == "z3" else nq
                    for k in range(KT):
                        mm = nc.tensor.matmul(out, w_in[:, k, m * P:(m + 1) * P], x_t[:, src, k], start=(k == 0), stop=(k == KT - 1))
                elif t[0] == "c":
                    c, k = int(t[1]), part
                    if k == 0:
                        pe.wait_ge(halo_moved, count(n, 2, 1))
                        emptied_all(pe, plan, u, [f"x{c}"])
                    mm = nc.tensor.matmul(out, dg_tap[:, c, k], x_in[:, c, k:k + T], start=(k == 0), stop=(k == TAPS - 1))
                elif t == "dl":
                    c = part
                    if c == 0:
                        pe.wait_ge(x_conv_ready, count(n, 2, 2))
                    mm = nc.tensor.matmul(work[0:RANK, bank], w_x[:, c, 0:RANK], x_conv[:, nq, c], start=(c == 0), stop=(c == CH - 1))
                elif t == "bc":
                    c = part
                    mm = nc.tensor.matmul(out, w_x[:, c, RANK:], x_conv[:, nq, c], start=(c == 0), stop=(c == CH - 1))
                elif t[0] == "d":
                    c = int(t[1])
                    emptied_all(pe, plan, u, ["dl"])
                    mm = nc.tensor.matmul(out, w_dt[:, c * P:(c + 1) * P], dt_low, start=True, stop=True)
                elif t[0] == "o":
                    if part == 0:
                        pe.wait_ge(gated, count(u, CH, 0))
                    tt, rest_of_it = divmod(part, 2)
                    tok = (2 * int(t[1]) + tt) * P
                    o = work[:, bank, tt * DM:(tt + 1) * DM]
                    if not rest_of_it:
                        nc.tensor.matmul(o, ones[:], b_out[:], start=True, stop=False)
                    for c in (range(1, CH) if rest_of_it else (0,)):
                        mm = nc.tensor.matmul(o, y_gated[:, c, tok:tok + P], w_out[:, c], start=False, stop=(c == CH - 1))
                if part == parts_of(t) - 1:
                    mm.then_inc(filled[bank], 1)

            def weave(u, plan, m):
                for t, part in plan.parts_at(m):
                    tile(u, plan, t, part)

            def unit_program(u, plan):
                for m in range(ITEMS):
                    nu, nm = after(u, m, 1)
                    if not on_pool(nm) and not (plan is last and m == ITEMS - 1):
                        make_c(nu, nm)
                    pu, pm = before(u, m, LAG)
                    if not (plan is second and m < LAG):
                        add_item(pu, pm)
                    weave(u, plan, m)

            for m in range(ITEMS):
                weave((0, -1), first, m)
            make_c((0, 0), 0)
            whole(pe, unit_program)
            for m in range(ITEMS - LAG, ITEMS):
                add_item((0, UNITS - 1), m)
            for t in ("o0", "o1"):
                for part in range(parts_of(t)):
                    tile((0, UNITS), final, t, part)

        @block.vector
        def _(dve):
            dve.wait_ge(weights_in, ALL_WEIGHTS)
            dve.wait_ge(ident_ready, 1)
            for c in range(CH):
                for k in range(TAPS):
                    nc.vector.tensor_scalar(dg_tap[:, c, k], ident[:], taps[:, c, k:k + 1], None, ALU.mult)
                nc.vector.tensor_scalar(dg_skip[:, c], ident[:], d_skip[:, c:c + 1], None, ALU.mult)
            dve.wait_ge(a_exp, 1)
            nc.vector.tensor_scalar(a_big[:], a_mat[:], 1e-6, None, ALU.is_ge).then_inc(a_inv_step, 1)
            dve.wait_ge(a_inv_step, 1)
            nc.vector.scalar_tensor_tensor(out=a_inv[:], in0=a_mat[:], scalar=-1.0, in1=a_big[:], op0=ALU.mult,
                                           op1=ALU.mult).then_inc(a_inv_step, 1)
            dve.wait_ge(a_inv_step, 2)
            nc.vector.scalar_tensor_tensor(out=a_inv[:], in0=a_inv[:], scalar=1.0, in1=a_big[:], op0=ALU.add,
                                           op1=ALU.subtract).then_inc(a_inv_step, 1)
            dve.wait_ge(a_inv_step, 3)
            nc.vector.reciprocal(a_inv[:], a_inv[:]).then_inc(a_inv_step, 1)
            dve.wait_ge(a_inv_step, 4)
            nc.vector.tensor_scalar(a_mat[:], a_mat[:], -1.0, None, ALU.mult).then_inc(a_inv_step, 1)
            for c in range(CH):
                for n, s in enumerate(POOL_HC):
                    one = nc.vector.tensor_scalar(dg_inv[:, c, n], ident[:], a_inv[:, c, s:s + 1], None, ALU.mult)
            one.then_inc(diags_ready, 1)

            def make_b(u, m):
                dve.wait_ge(a_ready, count(u, ITEMS, m + 1))
                dve.wait_ge(u_ready, count(u, ITEMS, m + 1))
                nc.vector.scalar_tensor_tensor(out=h[:, m % HS], in0=a_ps[:, m % 2], scalar=1.0, in1=h[:, m % HS],
                                               op0=ALU.subtract, op1=ALU.mult).then_inc(b_ready, 1)

            def scan(u, m):
                c, s = divmod(m, NS)
                dve.wait_ge(b_ready, count(u, ITEMS, m + 1))
                nc.vector.tensor_tensor_scan(h[:, m % HS], a_ps[:, m % 2], h[:, m % HS],
                                             carry[:, batch(u), c, s:s + 1], ALU.mult, ALU.add).then_inc(scanned, 1)

            def save_carry(u, g):
                c, s = divmod(g * QUAD, NS)
                slot = g * QUAD % HS
                dve.wait_ge(scanned, count(u, ITEMS, g * QUAD + QUAD))
                nc.vector.tensor_scalar(carry[:, batch(u), c, s:s + QUAD], h[:, slot:slot + QUAD, T - 1], 1.0, None,
                                        ALU.mult).then_inc(carried, 1)

            def make_hc(u, m):
                dve.wait_ge(c_ready, count(u, NV, vector_before(m) + 1))
                dve.wait_ge(scanned, count(u, ITEMS, m + 1))
                wait(dve, summed, count(u, ITEMS, m - HCS + 1))
                c, s = divmod(m, NS)
                nc.vector.scalar_tensor_tensor(out=hc[:, m % HCS], in0=h[:, m % HS], scalar=a_inv[:, c, s:s + 1],
                                               in1=c_ps[:, vector_before(m) % 2], op0=ALU.mult,
                                               op1=ALU.mult).then_inc(hc_vector, 1)

            def make_gated(u, c):
                dve.wait_ge(summed, count(u, ITEMS, (c + 1) * NS))
                dve.wait_ge(gate_ready, count(u, 2, (1, 1, 2, 4)[c]))
                nc.vector.tensor_tensor(y_gated[:, c], y_ps[:, c % 2], gate[:, c], ALU.mult).then_inc(gated, 1)

            def halo_in(n):
                wait(dve, halo_moved, count(n, 2, 0))
                nc.vector.tensor_scalar(x_in[:, :, 0:HALO], halo[:, batch(n)], 1.0, None, ALU.mult).then_inc(halo_moved, 1)

            def halo_out(u, plan):
                emptied_all(dve, plan, u, [f"x{c}" for c in range(CH)])
                dve.wait_ge(halo_moved, count(later(u), 2, 1))
                nc.vector.tensor_scalar(halo[:, batch(later(u))], x_in[:, :, T:], 1.0, None, ALU.mult).then_inc(halo_moved, 1)

            def norm_so_far(pu, n):
                dve.wait_ge(norm_step, count(pu, NORM, n))

            def norm_sums(u, plan, t):
                k, bank, pu = int(t[1]), plan.bank(t), later(u, -1)
                if k == 0:
                    dve.wait_ge(x_tok_in, count(pu, 16, 16))
                dve.wait_ge(filled[bank], plan.before(t, u) + 1)
                two = x_tok[:, 2 * k:2 * k + 2]
                nc.vector.tensor_tensor(two, work[:, bank].rearrange("p (a b) -> p a b", a=2), two,
                                        ALU.add).then_inc(emptied[bank], 1)
                dve.wait_ge(emptied[bank], plan.before(t, u) + 1)
                for tt in (2 * k, 2 * k + 1):
                    nc.vector.bn_stats(stats[:, tt], x_tok[:, tt]).then_inc(norm_step, 1)
                norm_so_far(pu, 5 * k + 2)
                nc.vector.memset(spread[:, 2 * k:2 * k + 2], EPS).then_inc(norm_step, 1)
                for tt in (2 * k, 2 * k + 1):
                    nc.vector.bn_aggr(mean_var[:, tt], stats[:, tt]).then_inc(norm_step, 1)
                if k == 1:
                    norm_so_far(pu, 10)
                    nc.vector.tensor_tensor(spread[:], spread[:], mean_var[:, :, 1], ALU.add).then_inc(norm_step, 1)

            def normalise(pu):
                dve.wait_ge(std_ready, count(pu, 1, 1))
                nc.vector.reciprocal(spread[:], spread[:]).then_inc(norm_step, 1)
                norm_so_far(pu, 12)
                for tt in range(TT):
                    row = x_tok[:, tt]
                    nc.vector.tensor_scalar(row, row, mean_var[:, tt, 0:1], spread[:, tt:tt + 1], ALU.subtract,
                                            ALU.mult).then_inc(norm_step, 1)

            def split(u, plan):
                n, nq, bank = later(u), (u[1] + 1) % 2, plan.bank("bc")
                dve.wait_ge(high_ready, count(n, 1, 1))
                wait(dve, dt_ready, count(n, CH, 0))
                nc.vector.tensor_tensor(rest[64:], work[64:, bank], parts[64:, nq], ALU.subtract).then_inc(emptied[bank], 1)
                dve.wait_ge(emptied[bank], plan.before("bc", u) + 1)
                nc.vector.tensor_copy(parts[64:, nq], rest[64:]).then_inc(split_step, 1)
                dve.wait_ge(split_step, count(n, 2, 1))
                nc.vector.tensor_tensor(parts[96:, nq], rest[96:], parts[96:, nq], ALU.subtract).then_inc(split_step, 1)

            def softplus(u, plan, f):
                n = later(u)
                c, k = divmod(f, FACTORS)
                dve.wait_ge(square_ready, count(n, LOGS, f + 1))
                if k == 0:
                    wait(dve, dt_ready, count(n, CH, c - 1))
                    if c == 0:
                        dve.wait_ge(split_step, count(n, 2, 2))
                    if c == 1:
                        emptied_all(dve, plan, u, ["d3"])
                else:
                    dve.wait_ge(softplus_step, count(n, LOGS, f))
                nc.vector.scalar_tensor_tensor(out=poly[:, c % 2], in0=square[:, f % 2], scalar=LOG1P[k][1],
                                               in1=x_arg[:, c] if k == 0 else poly[:, c % 2], op0=ALU.add,
                                               op1=ALU.mult).then_inc(softplus_step, 1)

            GATED_AT = {20: 0, 36: 1, 52: 2}

            def weave(u, plan, m):
                if plan.has("x0"):
                    if m == 5:
                        halo_in(later(u))
                    if m == 11:
                        halo_out(u, plan)
                    if m == 44:
                        split(u, plan)
                    if m >= ITEMS - LOGS:
                        softplus(u, plan, m - (ITEMS - LOGS))
                if m == 4 and plan in (inner, last):
                    make_gated(later(u, -1), CH - 1)
                if m in GATED_AT and plan is not first:
                    make_gated(u, GATED_AT[m])
                if plan.has("o0"):
                    if m in (12, 16):
                        norm_sums(u, plan, f"o{(m - 12) // 4}")
                    if m == 22:
                        normalise(later(u, -1))

            def unit_program(u, plan):
                for m in range(ITEMS):
                    scan(u, m)
                    nu, nm = after(u, m, 1)
                    if not (plan is last and m == ITEMS - 1):
                        make_b(nu, nm)
                    pu, pm = before(u, m, 1)
                    if not on_pool(pm) and not (plan is second and m == 0):
                        make_hc(pu, pm)
                    if m % QUAD == 0 and not (plan is second and m == 0):
                        gu, gm = before(u, m, QUAD)
                        save_carry(gu, gm // QUAD)
                    weave(u, plan, m)

            dve.wait_ge(zeroed, 6)
            for m in range(ITEMS):
                weave((0, -1), first, m)
            make_b((0, 0), 0)
            whole(dve, unit_program)
            make_hc((0, UNITS - 1), ITEMS - 1)
            make_gated((0, UNITS - 1), CH - 1)
            for k in range(2):
                norm_sums((0, UNITS), final, f"o{k}")
            normalise((0, UNITS - 1))


GROUP = 4
ROWS = UNITS * T
TILES = ROWS // P
SLOT_TILES = 2 * TILES + NE
GROUPS = SLOT_TILES // GROUP
SHARED = NE


BEHIND = 2
OWNER_PART = SLOT_TILES // 3
EITHER_AT, SLOTS_AT, OWNER_AT = 12, 34, 43


def moe_layout(g, chunks):
    import numpy as np

    def stack(name):
        return np.concatenate([g[f"L0_ffn_experts_{name}"], g[f"L0_ffn_shared_{name}"][None]])

    up = np.concatenate([stack("wg"), stack("wu")], axis=2)
    return {
        "w_gate": chunks(g["L0_ffn_gate_w"]),
        "b_gate": g["L0_ffn_gate_b"][:, None],
        "w_up": up.reshape(NE + 1, KT, P, 2 * IF).transpose(2, 0, 1, 3),
        "w_down": stack("wd").transpose(1, 0, 2),
    }


def moe(nc, d):
    with ExitStack() as ctx:
        def sb(name, shape, dt=F32):
            return ctx.enter_context(nc.sbuf_tensor(name, shape, dt))

        def sem(name):
            return ctx.enter_context(nc.semaphore(name))

        w_gate = sb("w_gate", [P, KT, NE])
        b_gate = sb("b_gate", [NE, 1])
        w_up = sb("w_up", [P, NE + 1, KT, 2 * IF])
        w_down = sb("w_down", [P, NE + 1, DM])
        ident = sb("moe_ident", [P, P])
        tri = sb("tri", [P, P], BF16)
        full = sb("full", [P, P], BF16)
        precedence = sb("precedence", [P, NE])
        steps = sb("steps", [P, TILES])
        slots_seq = sb("slots_seq", [1, SLOT_TILES])

        acc = sb("acc", [P, UNITS, TT, DM])
        x1_t = sb("x1_t", [P, UNITS, KT, T])

        logits_t = sb("logits_t", [NE, 2, T])
        score = sb("score", [P, TILES, NE])
        rank = sb("rank", [P, TILES, NE])
        chosen = sb("chosen", [P, 2, TILES, NE])
        either = sb("either", [P, TILES, NE], BF16)
        best = sb("best", [P, 2, TILES])
        first_rank = sb("first_rank", [P, TILES])
        used = sb("used", [P, NE])
        used_end = sb("used_end", [P, NE])
        owner_f = sb("owner_f", [1, SLOT_TILES])
        owner = sb("owner", [1, BEHIND + SLOT_TILES], U32)
        slot_f = sb("slot_f", [P, 2, TILES])
        slot = sb("slot", [P, 2, TILES], U32)
        mean_var = sb("moe_mean_var", [P, 2, TT, 2])
        stats = sb("moe_stats", [P, 2, TT, 6])
        spread = sb("moe_spread", [P, 2, TT])
        silu = chosen[:, 0].rearrange("p a b -> p (a b)").rearrange("p (a b) -> p a b", a=2)
        hidden = chosen[:, 1].rearrange("p a b -> p (a b)").rearrange("p (a b) -> p a b", a=2)

        def room(first, units):
            return x1_t[:, first:first + units].rearrange("p u k t -> p (u k t)")

        x_slots = room(0, 2).rearrange("p (g c f) -> p g c f", g=2, c=GROUP)
        y_slots = room(2, 2).rearrange("p (g c f) -> p g c f", g=2, c=GROUP)
        xt = room(4, 1).rearrange("p (a f) -> p a f", a=4)
        e_silu = room(5, 1).rearrange("p (a f) -> p a f", a=8)[:, 0:2]
        e_hidden = room(5, 1).rearrange("p (a f) -> p a f", a=8)[:, 2:4]
        e_hidden_t = room(5, 1).rearrange("p (a f) -> p a f", a=8)[:, 4:6]
        NG = 4
        gathered = room(6, 2 * NG).rearrange("p (n t r f) -> p n t r f", n=NG, t=TT, r=2)

        banks = ctx.enter_context(nc.psum_tensor("banks", [P, 8, T], F32))
        turn_ps = banks[:, 0:4].rearrange("p (a k) t -> p a k t", a=2)
        logits_ps = banks[:, 4:6].rearrange("p a t -> p (a t)").rearrange("p (a e) -> p a e", a=TILES)
        logits_t_ps = banks[0:NE, 6:8]
        within_ps = banks[:, 0:2].rearrange("p a t -> p (a t)").rearrange("p (a e) -> p a e", a=TILES)
        totals_ps = banks[:, 2:4].rearrange("p a t -> p (a t)").rearrange("p (a e) -> p a e", a=TILES)
        g_ps, u_ps = banks[:, 0:2], banks[:, 2:4]
        d_ps = banks[:, 4:6].rearrange("p a t -> p (a t)").rearrange("p (a f) -> p a f", a=TT)
        xt_ps = banks[:, 0:2]
        gu_ps = banks[:, 2:4]
        ht_ps = banks[:, 4:5]
        y_ps = banks[:, 5:7]

        router_in = sem("router_in")
        experts_in = sem("experts_in")
        x1_in = [sem(f"x1_in{q}") for q in range(4)]
        made = sem("moe_constants_made")
        turned = sem("turned")
        x1_t_act = sem("x1_t_act")
        x1_t_dve = sem("x1_t_dve")
        logits_t_made = sem("logits_t_made")
        logits_t_ready = sem("logits_t_ready")
        logits_ready = sem("logits_ready")
        score_ready = sem("score_ready")
        step = sem("route_step")
        counted = sem("counted")
        up_ready = sem("up_ready")
        silu_ready = sem("silu_ready")
        hidden_ready = sem("hidden_ready")
        down_ready = sem("down_ready")
        blended = sem("blended")
        scattered = [sem(f"scattered{q}") for q in range(4)]
        x_slots_in = [sem(f"x_slots_in{q}") for q in range(2)]
        xt_made = sem("xt_made")
        xt_ready = sem("xt_ready")
        e_up = sem("e_up")
        e_silu_ready = sem("e_silu_ready")
        e_hidden_ready = sem("e_hidden_ready")
        ht_made = sem("ht_made")
        ht_ready = sem("ht_ready")
        y_made = sem("y_made")
        y_ready = sem("y_ready")
        y_stored = [sem(f"y_stored{q}") for q in range(2)]
        gathered_in = [sem(f"gathered_in{q}") for q in range(NG)]
        mixed = sem("mixed")
        norm = sem("moe_norm_step")
        std = sem("moe_std_ready")
        out_stored = sem("out_stored")

        MOE_NORM = 2 * TT + 3 + TT
        held = dict(w_gate=w_gate, b_gate=b_gate, w_up=w_up, w_down=w_down)

        BODY = 2 * GROUP
        BODIES = SLOT_TILES // BODY

        def tiles(eng, program):
            for c in range(BODY):
                program(0, c, c)
            with eng.Fori(1, BODIES - 1) as r:
                for c in range(BODY):
                    program(r, c, None)
            for c in range(BODY):
                program(BODIES - 1, c, (BODIES - 1) * BODY + c)

        def tile_no(r, c):
            return r * BODY + c

        block = ctx.enter_context(nc.Block())

        @block.sync
        def _(sp):
            for name in ("w_gate", "b_gate"):
                sp.dma_start(held[name][:], d[name]).then_inc(router_in, 16)
            for q in range(4):
                sp.dma_start(acc[:, q], d["x1"][q]).then_inc(x1_in[q], 16)
            for i in range(4, UNITS):
                sp.wait_ge(x1_in[i % 4], 16 * (i // 4))
                sp.dma_start(acc[:, i], d["x1"][i]).then_inc(x1_in[i % 4], 16)
            for name in ("w_up", "w_down"):
                sp.dma_start(held[name][:], d[name]).then_inc(experts_in, 16)

            for q in range(4):
                sp.wait_ge(scattered[q], UNITS // 4 * 16 * 2 * TT)
            sp.wait_ge(hidden_ready, UNITS)

            def load(r, g):
                sp.dma_start(x_slots[:, g], d["x_slots"][:, r * BODY + g * GROUP:r * BODY + (g + 1) * GROUP] if isinstance(r, int)
                             else d["x_slots"][:, bass.ds(r * BODY + g * GROUP, GROUP)]).then_inc(x_slots_in[g], 16)

            def store(r, g):
                sp.wait_ge(y_ready, r * BODY + (g + 1) * GROUP)
                sp.dma_start(d["y_slots"][:, r * BODY + g * GROUP:r * BODY + (g + 1) * GROUP] if isinstance(r, int)
                             else d["y_slots"][:, bass.ds(r * BODY + g * GROUP, GROUP)], y_slots[:, g]).then_inc(y_stored[g], 16)

            load(0, 0)
            load(0, 1)

            def body(r, more):
                for g in range(2):
                    if more:
                        sp.wait_ge(xt_made, r * BODY + (g + 1) * GROUP)
                        load(r + 1, g)
                    store(r, g)

            body(0, True)
            with sp.Fori(1, BODIES - 1) as r:
                body(r, True)
            body(BODIES - 1, False)

            for i in range(UNITS):
                sp.wait_ge(norm, (i + 1) * MOE_NORM)
                sp.dma_start(d["out"][i], acc[:, i]).then_inc(out_stored, 16)
            sp.wait_ge(out_stored, 16 * UNITS)

        @block.gpsimd
        def _(pool):
            nc.gpsimd.memset(ident[:], 0.0).then_inc(made, 1)
            nc.gpsimd.memset(tri[:], 0.0).then_inc(made, 1)
            nc.gpsimd.memset(full[:], 1.0).then_inc(made, 1)
            pool.wait_ge(made, 3)
            nc.gpsimd.affine_select(out=ident[:], in_=ident[:], compare_op=ALU.not_equal, fill=1.0, base=0,
                                    pattern=[[-1, P]], channel_multiplier=1).then_inc(made, 1)
            nc.gpsimd.affine_select(out=tri[:], in_=tri[:], compare_op=ALU.is_ge, fill=1.0, base=0,
                                    pattern=[[-1, P]], channel_multiplier=1).then_inc(made, 1)
            nc.gpsimd.iota(precedence[:], pattern=[[-1, NE]], base=NE, channel_multiplier=0,
                           allow_small_or_imprecise_dtypes=True).then_inc(made, 1)
            nc.gpsimd.iota(steps[:], pattern=[[P, TILES]], base=0, channel_multiplier=0,
                           allow_small_or_imprecise_dtypes=True).then_inc(made, 1)
            nc.gpsimd.iota(slots_seq[:], pattern=[[1, SLOT_TILES]], base=0, channel_multiplier=0,
                           allow_small_or_imprecise_dtypes=True).then_inc(made, 1)

            pool.wait_ge(step, SLOTS_AT)
            for t in range(TILES):
                i, tt = divmod(t, TT)
                if tt == 0:
                    wait(pool, scattered[i % 4], 16 * 2 * TT * (i // 4))
                for r in range(2):
                    nc.gpsimd.indirect_dma_start(
                        d["x_rows"], bass.IndirectOffsetOnAxis(slot[:, r, t:t + 1], 0),
                        acc[:, i, tt], None).then_inc(scattered[i % 4], 16)

            for q in range(2):
                pool.wait_ge(y_stored[q], 16 * BODIES)
            for t in range(TILES):
                i, tt = divmod(t, TT)
                if tt == 0 and i >= NG:
                    pool.wait_ge(mixed, (i - NG + 1) * 2 * TT)
                for r in range(2):
                    nc.gpsimd.indirect_dma_start(
                        gathered[:, i % NG, tt, r], None, d["y_rows"],
                        bass.IndirectOffsetOnAxis(slot[:, r, t:t + 1], 0)).then_inc(gathered_in[i % NG], 16)

        MADE = 8

        @block.scalar
        def _(act):
            def add_bias(i):
                act.wait_ge(logits_t_made, i + 1)
                wait(act, logits_ready, i - 1)
                nc.scalar.activation(logits_t[:, i % 2], logits_t_ps[:, i % 2], ACT.Identity, bias=b_gate[:, 0:1]).then_inc(logits_t_ready, 1)

            act.wait_ge(router_in, 32)
            for i in range(UNITS):
                act.wait_ge(turned, i + 1)
                nc.scalar.copy(x1_t[:, i, 0], turn_ps[:, i % 2, 0]).then_inc(x1_t_act, 1)
                if i > 0:
                    add_bias(i - 1)
            add_bias(UNITS - 1)
            act.wait_ge(logits_ready, UNITS)
            nc.scalar.activation(score[:], logits_ps, ACT.Sigmoid).then_inc(score_ready, 1)
            for i in range(UNITS):
                act.wait_ge(up_ready, i + 1)
                act.wait_ge(step, SLOTS_AT)
                wait(act, hidden_ready, i - 1)
                nc.scalar.activation(silu[:, i % 2], g_ps[:, i % 2], ACT.Silu).then_inc(silu_ready, 1)

            def hidden_t(r, c, k):
                act.wait_ge(ht_made, tile_no(r, c) + 1)
                if k is None or k >= 2:
                    act.wait_ge(y_made, tile_no(r, c) - 1)
                nc.scalar.copy(e_hidden_t[:, c % 2], ht_ps[:, 0, 0:P]).then_inc(ht_ready, 1)

            def program(r, c, k):
                if k is None or k >= 2:
                    hidden_t(r, c - 2, None if k is None else k - 2)
                act.wait_ge(e_up, tile_no(r, c) + 1)
                if k is None or k >= 2:
                    act.wait_ge(e_hidden_ready, tile_no(r, c) - 1)
                nc.scalar.activation(e_silu[:, c % 2], gu_ps[:, c % 2, 0:IF], ACT.Silu).then_inc(e_silu_ready, 1)

            tiles(act, program)
            for k in (SLOT_TILES - 2, SLOT_TILES - 1):
                hidden_t(BODIES - 1, k - (BODIES - 1) * BODY, k)

            for i in range(UNITS):
                act.wait_ge(norm, i * MOE_NORM + 2 * TT + 2)
                nc.scalar.activation(spread[:, i % 2], spread[:, i % 2], ACT.Sqrt).then_inc(std, 1)

        @block.tensor
        def _(pe):
            pe.wait_ge(made, MADE)
            pe.wait_ge(router_in, 32)

            def turn(i):
                pe.wait_ge(x1_in[i % 4], 16 * (i // 4 + 1))
                wait(pe, x1_t_act, i - 1)
                wait(pe, x1_t_dve, i - 1)
                for k in range(KT):
                    for tt in range(TT):
                        one = nc.tensor.transpose(turn_ps[:, i % 2, k, tt * P:(tt + 1) * P],
                                                  acc[:, i, tt, k * P:(k + 1) * P], ident[:])
                one.then_inc(turned, 1)

            def logits(i):
                pe.wait_ge(x1_t_act, i + 1)
                pe.wait_ge(x1_t_dve, i + 1)
                wait(pe, logits_t_ready, i - 1)
                for k in range(KT):
                    one = nc.tensor.matmul(logits_t_ps[:, i % 2], w_gate[:, k], x1_t[:, i, k], start=(k == 0), stop=(k == KT - 1))
                one.then_inc(logits_t_made, 1)

            def turn_logits(i):
                pe.wait_ge(logits_t_ready, i + 1)
                for tt in range(TT):
                    one = nc.tensor.transpose(logits_ps[:, i * TT + tt], logits_t[:, i % 2, tt * P:(tt + 1) * P], ident[0:NE, 0:NE])
                one.then_inc(logits_ready, 1)

            for i in range(UNITS + 2):
                if i < UNITS:
                    turn(i)
                if 1 <= i <= UNITS:
                    logits(i - 1)
                if i >= 2:
                    turn_logits(i - 2)

            pe.wait_ge(step, EITHER_AT)
            half = TILES // 2
            for a in range(2):
                nc.tensor.matmul(within_ps[:, a * half:(a + 1) * half], tri[:], either[:, a * half:(a + 1) * half], start=True, stop=True)
            for a in range(2):
                one = nc.tensor.matmul(totals_ps[:, a * half:(a + 1) * half], full[:], either[:, a * half:(a + 1) * half], start=True, stop=True)
            one.then_inc(counted, 1)

            pe.wait_ge(step, SLOTS_AT)
            pe.wait_ge(experts_in, 32)

            def down(i):
                pe.wait_ge(hidden_ready, i + 1)
                wait(pe, blended, i)
                for tt in range(TT):
                    one = nc.tensor.matmul(d_ps[:, tt], hidden[:, i % 2, tt * P:(tt + 1) * P], w_down[:, SHARED], start=True, stop=True)
                one.then_inc(down_ready, 1)

            for i in range(UNITS):
                wait(pe, hidden_ready, i - 1)
                for o, at in ((g_ps, 0), (u_ps, IF)):
                    for k in range(KT):
                        one = nc.tensor.matmul(o[:, i % 2], w_up[:, SHARED, k, at:at + IF], x1_t[:, i, k], start=(k == 0), stop=(k == KT - 1))
                one.then_inc(up_ready, 1)
                if i > 0:
                    down(i - 1)
            down(UNITS - 1)

            pe.wait_ge(step, OWNER_AT)
            pe.wait_ge(hidden_ready, UNITS)
            pe.wait_ge(blended, UNITS)

            def turn_slots(r, c, k):
                group = c // GROUP
                if c % GROUP == 0:
                    pe.wait_ge(x_slots_in[group], (r + 1) * 16)
                if k is None or k >= 2:
                    pe.wait_ge(xt_ready, tile_no(r, c) - 1)
                for h in range(KT):
                    one = nc.tensor.transpose(xt_ps[:, c % 2, h * P:(h + 1) * P],
                                              x_slots[:, group, c % GROUP, h * P:(h + 1) * P], ident[:])
                one.then_inc(xt_made, 1)

            def up_slots(r, c, k, e):
                pe.wait_ge(xt_ready, tile_no(r, c) + 1)
                if k is None or k >= 2:
                    pe.wait_ge(e_hidden_ready, tile_no(r, c) - 1)
                for h in range(KT):
                    one = nc.tensor.matmul(gu_ps[:, c % 2, 0:2 * IF], xt[:, c % 4, h * P:(h + 1) * P], w_up[:, e, h], start=(h == 0), stop=(h == KT - 1))
                one.then_inc(e_up, 1)

            def turn_hidden(r, c, k):
                pe.wait_ge(e_hidden_ready, tile_no(r, c) + 1)
                if k is None or k >= 1:
                    pe.wait_ge(ht_ready, tile_no(r, c))
                nc.tensor.transpose(ht_ps[:, 0, 0:P], e_hidden[:, c % 2], ident[:]).then_inc(ht_made, 1)

            def down_slots(r, c, k, e):
                pe.wait_ge(ht_ready, tile_no(r, c) + 1)
                if k is None or k >= 2:
                    pe.wait_ge(y_ready, tile_no(r, c) - 1)
                nc.tensor.matmul(y_ps[:, c % 2, 0:DM], e_hidden_t[:, c % 2], w_down[:, e], start=True, stop=True).then_inc(y_made, 1)

            owner_regs = [pe.alloc_register(f"owner{c}") for c in range(BEHIND + BODY)]

            def load_owners(r):
                pe.load(owner_regs, owner[0:1, bass.ds(r * BODY, BEHIND + BODY)])
                return {c - BEHIND: pe.snap(reg, min_val=0, max_val=NE - 1) for c, reg in enumerate(owner_regs)}

            def body(r, k0):
                owners = load_owners(r)
                for c in range(BODY):
                    k = None if k0 is None else k0 + c
                    old = None if k0 is None else k - 2
                    if old is None or old >= 0:
                        turn_hidden(r, c - 2, old)
                    if k is None or k + 1 < SLOT_TILES:
                        if c + 1 < BODY:
                            turn_slots(r, c + 1, None if k is None else k + 1)
                        else:
                            turn_slots(r + 1, 0, None if k is None else k + 1)
                    up_slots(r, c, k, owners[c])
                    if old is None or old >= 0:
                        down_slots(r, c - 2, old, owners[c - 2])
                return owners

            turn_slots(0, 0, 0)
            body(0, 0)
            with pe.Fori(1, BODIES - 1) as r:
                body(r, None)
            owners = body(BODIES - 1, (BODIES - 1) * BODY)
            for k in (SLOT_TILES - 2, SLOT_TILES - 1):
                c = k - (BODIES - 1) * BODY
                turn_hidden(BODIES - 1, c, k)
                down_slots(BODIES - 1, c, k, owners[c])

        @block.vector
        def _(dve):
            AX = mybir.AxisListType.X
            V = nc.vector
            dve.wait_ge(made, MADE)
            for i in range(UNITS):
                dve.wait_ge(turned, i + 1)
                V.tensor_copy(x1_t[:, i, 1], turn_ps[:, i % 2, 1]).then_inc(x1_t_dve, 1)

            done_steps = [0]

            def done(one):
                one.then_inc(step, 1)
                done_steps[0] += 1
                dve.wait_ge(step, done_steps[0])

            def over_experts(v):
                return v.unsqueeze(2).to_broadcast([P, TILES, NE])

            def over_tiles(v):
                return v.unsqueeze(1).to_broadcast([P, TILES, NE])

            dve.wait_ge(score_ready, 1)
            for r in range(2):
                done(V.tensor_reduce(best[:, r], score[:], AX, ALU.max))
                done(V.tensor_tensor(rank[:], score[:], over_experts(best[:, r]), ALU.is_equal))
                done(V.tensor_tensor(rank[:], rank[:], over_tiles(precedence[:]), ALU.mult))
                done(V.tensor_reduce(first_rank[:], rank[:], AX, ALU.max))
                done(V.tensor_tensor(chosen[:, r], rank[:], over_experts(first_rank[:]), ALU.is_equal))
                if r == 0:
                    done(V.scalar_tensor_tensor(out=score[:], in0=chosen[:, 0], scalar=-2.0, in1=score[:],
                                                op0=ALU.mult, op1=ALU.add))
            done(V.tensor_tensor(either[:], chosen[:, 0], chosen[:, 1], ALU.add))
            assert done_steps[0] == EITHER_AT
            done(V.tensor_tensor(first_rank[:], best[:, 0], best[:, 1], ALU.add))
            done(V.reciprocal(first_rank[:], first_rank[:]))
            for r in range(2):
                done(V.tensor_tensor(best[:, r], best[:, r], first_rank[:], ALU.mult))

            by_expert = score[:].rearrange("p a b -> p (a b)").rearrange("p (e t) -> p e t", e=NE)
            table = rank[:].rearrange("p a b -> p (a b)").rearrange("p (e t) -> p e t", e=NE)
            done(V.memset(table, 1.0))
            done(V.memset(table[:, :, 0:1], 0.0))
            dve.wait_ge(counted, 1)
            done(V.tensor_copy(by_expert, totals_ps.rearrange("p t e -> p e t")))
            done(V.tensor_tensor_scan(score[:].rearrange("p a b -> p (a b)"), rank[:].rearrange("p a b -> p (a b)"),
                                      score[:].rearrange("p a b -> p (a b)"), 0.0, ALU.mult, ALU.add))
            done(V.tensor_tensor(table, by_expert[:, :, TILES - 1:TILES].to_broadcast([P, NE, TILES]),
                                 steps[:].unsqueeze(1).to_broadcast([P, NE, TILES]), ALU.is_gt))
            done(V.tensor_reduce(used[:], table, AX, ALU.add))
            done(V.memset(used_end[:], 1.0))
            done(V.tensor_tensor_scan(used_end[:], used_end[:], used[:], 0.0, ALU.mult, ALU.add))
            done(V.tensor_tensor(used[:], used_end[:], used[:], ALU.subtract))
            done(V.tensor_scalar(used[:], used[:], float(P), None, ALU.mult))
            cand = rank[:]
            done(V.tensor_tensor(cand, score[:].rearrange("p a b -> p (a b)").rearrange("p (e t) -> p t e", e=NE), totals_ps, ALU.subtract))
            done(V.tensor_tensor(cand, cand, within_ps, ALU.add))
            done(V.tensor_tensor(cand, cand, over_tiles(used[:]), ALU.add))
            for r in range(2):
                done(V.tensor_tensor(chosen[:, r], chosen[:, r], cand, ALU.mult))
                done(V.tensor_reduce(slot_f[:, r], chosen[:, r], AX, ALU.add))
            done(V.tensor_copy(slot[:], slot_f[:]))
            assert done_steps[0] == SLOTS_AT, done_steps
            runs = rank[0:1, 0:OWNER_PART]
            for part in range(SLOT_TILES // OWNER_PART):
                at = slice(part * OWNER_PART, (part + 1) * OWNER_PART)
                done(V.tensor_tensor(runs, used_end[0:1].unsqueeze(1).to_broadcast([1, OWNER_PART, NE]),
                                     slots_seq[:, at].unsqueeze(2).to_broadcast([1, OWNER_PART, NE]), ALU.is_le))
                done(V.tensor_reduce(owner_f[:, at], runs, AX, ALU.add))
            done(V.tensor_scalar(owner_f[:], owner_f[:], float(NE - 1), None, ALU.min))
            done(V.tensor_copy(owner[:, BEHIND:], owner_f[:]))
            done(V.memset(owner[:, 0:BEHIND], 0))
            assert done_steps[0] == OWNER_AT, done_steps

            def blend_shared(i):
                dve.wait_ge(down_ready, i + 1)
                dve.wait_ge(scattered[i % 4], 16 * 2 * TT * (i // 4 + 1))
                V.scalar_tensor_tensor(out=acc[:, i], in0=acc[:, i], scalar=2.0, in1=d_ps, op0=ALU.mult,
                                       op1=ALU.add).then_inc(blended, 1)

            for i in range(UNITS):
                dve.wait_ge(silu_ready, i + 1)
                dve.wait_ge(up_ready, i + 1)
                wait(dve, down_ready, i - 1)
                V.tensor_tensor(hidden[:, i % 2], silu[:, i % 2], u_ps[:, i % 2], ALU.mult).then_inc(hidden_ready, 1)
                if i > 0:
                    blend_shared(i - 1)
            blend_shared(UNITS - 1)

            def take_turned(r, c, k):
                dve.wait_ge(xt_made, tile_no(r, c) + 1)
                if k is None or k >= 4:
                    dve.wait_ge(e_up, tile_no(r, c) - 3)
                V.tensor_copy(xt[:, c % 4], xt_ps[:, c % 2, 0:DM]).then_inc(xt_ready, 1)

            def gate_hidden(r, c, k):
                dve.wait_ge(e_silu_ready, tile_no(r, c) + 1)
                if k is None or k >= 2:
                    dve.wait_ge(ht_made, tile_no(r, c) - 1)
                V.tensor_tensor(e_hidden[:, c % 2], e_silu[:, c % 2], gu_ps[:, c % 2, IF:2 * IF], ALU.mult).then_inc(e_hidden_ready, 1)

            def take_y(r, c, k):
                group = c // GROUP if c >= 0 else 1
                dve.wait_ge(y_made, tile_no(r, c) + 1)
                if c % GROUP == 0 and (k is None or k >= BODY):
                    dve.wait_ge(y_stored[group], (r if c >= 0 else r - 1) * 16)
                V.tensor_copy(y_slots[:, group, c % GROUP], y_ps[:, c % 2, 0:DM]).then_inc(y_ready, 1)

            def program(r, c, k):
                if k is None or k + 1 < SLOT_TILES:
                    if c + 1 < BODY:
                        take_turned(r, c + 1, None if k is None else k + 1)
                    else:
                        take_turned(r + 1, 0, None if k is None else k + 1)
                gate_hidden(r, c, k)
                if k is None or k >= 2:
                    take_y(r, c - 2, None if k is None else k - 2)

            take_turned(0, 0, 0)
            tiles(dve, program)
            for k in (SLOT_TILES - 2, SLOT_TILES - 1):
                take_y(BODIES - 1, k - (BODIES - 1) * BODY, k)

            def stage5(i):
                q = i % 2
                at = i * MOE_NORM
                dve.wait_ge(gathered_in[i % NG], 16 * 2 * TT * (i // NG + 1))
                for r in range(2):
                    wait(dve, mixed, i * 2 * TT + r * TT)
                    for tt in range(TT):
                        V.scalar_tensor_tensor(out=acc[:, i, tt], in0=gathered[:, i % NG, tt, r],
                                               scalar=best[:, r, i * TT + tt:i * TT + tt + 1], in1=acc[:, i, tt],
                                               op0=ALU.mult, op1=ALU.add).then_inc(mixed, 1)
                dve.wait_ge(mixed, (i + 1) * 2 * TT)
                for tt in range(TT):
                    V.bn_stats(stats[:, q, tt], acc[:, i, tt]).then_inc(norm, 1)
                dve.wait_ge(norm, at + TT)
                V.memset(spread[:, q], EPS).then_inc(norm, 1)
                for tt in range(TT):
                    V.bn_aggr(mean_var[:, q, tt], stats[:, q, tt]).then_inc(norm, 1)
                dve.wait_ge(norm, at + 2 * TT + 1)
                V.tensor_tensor(spread[:, q], spread[:, q], mean_var[:, q, :, 1], ALU.add).then_inc(norm, 1)
                dve.wait_ge(std, i + 1)
                V.reciprocal(spread[:, q], spread[:, q]).then_inc(norm, 1)
                dve.wait_ge(norm, at + 2 * TT + 3)
                for tt in range(TT):
                    row = acc[:, i, tt]
                    V.tensor_scalar(row, row, mean_var[:, q, tt, 0:1], spread[:, q, tt:tt + 1], ALU.subtract,
                                    ALU.mult).then_inc(norm, 1)

            for i in range(UNITS):
                stage5(i)


def kernel(**inputs):
    import numpy as np
    import concourse.bacc as bacc
    from concourse.bass_utils import run_bass_kernel_spmd

    g = {k: np.asarray(v) for k, v in inputs.items()}

    def chunks(v):
        v = v.reshape((v.shape[0] // P, P) + v.shape[1:])
        return v.swapaxes(0, 1)

    x = g["L0_attn_x"].reshape(NB, NW, T, DM).swapaxes(0, 1).reshape(UNITS, T, DM)
    x_proj = g["L0_attn_x_proj_w"].T
    laid = {
        "x_t": x.transpose(0, 2, 1).reshape(UNITS, KT, P, T).swapaxes(1, 2),
        "x_tok": x.reshape(UNITS, TT, P, DM).swapaxes(1, 2),
        "w_in": chunks(g["L0_attn_in_proj_w"].T),
        "b_in": chunks(g["L0_attn_in_proj_b"]),
        "taps": chunks(g["L0_attn_conv_w"]),
        "b_conv": chunks(g["L0_attn_conv_b"]),
        "a_log": chunks(g["L0_attn_A_log"].T),
        "d_skip": chunks(g["L0_attn_D"]),
        "w_x": chunks(np.concatenate([x_proj[:, :RANK]] + [x_proj[:, RANK:]] * 4, axis=1)),
        "w_dt": g["L0_attn_dt_proj_w"].T,
        "b_dt": chunks(g["L0_attn_dt_proj_b"]),
        "w_out": chunks(g["L0_attn_out_proj_w"].T),
        "b_out": g["L0_attn_out_proj_b"][None],
    }
    laid.update(moe_layout(g, chunks))
    laid = {k: np.ascontiguousarray(v) for k, v in laid.items()}

    nc = bacc.Bacc("TRN2", target_bir_lowering=False, num_devices=1)
    d = {k: nc.dram_tensor(f"in_{k}", v.shape, mybir.dt.from_np(v.dtype), kind="ExternalInput").ap()
         for k, v in laid.items()}
    d["out"] = nc.dram_tensor("out", (UNITS, P, TT, DM), F32, kind="ExternalOutput").ap()
    d["x1"] = nc.dram_tensor("x1", (UNITS, P, TT, DM), F32, kind="Internal").ap()
    for name in ("x", "y"):
        rows = nc.dram_tensor(f"{name}_rows", (SLOT_TILES * P, DM), F32, kind="Internal").ap()
        d[f"{name}_rows"] = rows
        d[f"{name}_slots"] = rows.rearrange("(s p) f -> p s f", p=P)
    mamba(nc, d)
    moe(nc, d)
    r = run_bass_kernel_spmd(nc, [{f"in_{k}": v for k, v in laid.items()}], core_ids=[0])
    out = np.asarray(r.results[0]["out"])
    return out.swapaxes(1, 2).reshape(NW, NB, T, DM).swapaxes(0, 1).reshape(NB, L, DM)
```

```python
from contextlib import ExitStack

import concourse.bass as bass
from concourse import mybir

F32 = mybir.dt.float32
BF16 = mybir.dt.bfloat16
U32 = mybir.dt.uint32
ALU = mybir.AluOpType
ACT = mybir.ActivationFunctionType

P = 128
T = 512
NB, L, DM = 4, 2048, 256
NW = L // T
UNITS = NB * NW
DI = 512
CH = DI // P
KT = DM // P
NS = 16
TAPS = 4
HALO = TAPS - 1
RANK = 64
TT = T // P
EPS = 1e-5
NE = 16
IF = 128

ROOT_SCALE = 0.5170210782894934
LOG1P = ((-1.2051646770627222, 0.11629121211354453), (0.5217478157878973, 0.2974565636862504),
         (-0.7402138145551652, 0.7266668451772348), (-0.04424682055460984, 0.8759711051528496))
FACTORS = len(LOG1P)
LOGS = 4 * FACTORS
NORM = 16
POOL_HC = (1, 3, 5, 7, 9, 11, 13, 15)


ITEMS = CH * NS
HS = 8
HCS = 4
LAG = 2
LEAD = 4
LATE_FROM = 13
A_AHEAD = 3

def count(unit, per, add):
    j, k = unit
    return per * k + add if isinstance(j, int) and j == 0 else j * (2 * per) + (per * k + add)


def number(unit):
    return count(unit, 1, 0)


def loads(unit):
    j, k = unit
    return 16 * (k // 2 + 1) if isinstance(j, int) else j * 16 + 16 * (k // 2 + 1)


def later(unit, n=1):
    return (unit[0], unit[1] + n)


def batch(unit):
    j, k = unit
    if isinstance(j, int):
        return k % NB
    half = j % 2
    return half * 2 + k if k < 2 else half * (-2) + k


def wait(eng, sem, value):
    if not isinstance(value, int) or value > 0:
        eng.wait_ge(sem, value)


def mamba(nc, d):
    with ExitStack() as ctx:
        def sb(name, shape, dt=F32):
            return ctx.enter_context(nc.sbuf_tensor(name, shape, dt))

        def psum(name, shape):
            return ctx.enter_context(nc.psum_tensor(name, shape, F32))

        def sem(name):
            return ctx.enter_context(nc.semaphore(name))

        w_in = sb("w_in", [P, KT, 2 * DI])
        w_x = sb("w_x", [P, CH, RANK + P])
        dt_out = sb("dt_out", [RANK + 1, DI])
        w_dt = dt_out[0:RANK]
        b_out = dt_out[RANK:, 0:DM]
        ones = dt_out[RANK:, DM:DM + P]
        w_out = sb("w_out", [P, CH, DM])
        b_in = sb("b_in", [P, 2 * CH])
        taps = sb("taps", [P, CH, TAPS])
        b_conv = sb("b_conv", [P, CH])
        d_skip = sb("d_skip", [P, CH])
        b_dt = sb("b_dt", [P, CH])
        a_log = sb("a_log", [P, CH, NS])
        a_mat = sb("a_mat", [P, CH, NS])
        a_big = a_log
        a_inv = sb("a_inv", [P, CH, NS])
        ident = sb("ident", [P, P])
        shifts = sb("shifts", [P, FACTORS])
        pick = sb("pick", [P, 2 * NS], BF16)
        dg_inv = sb("dg_inv", [P, CH, len(POOL_HC), P])
        dg_tap = sb("dg_tap", [P, CH, TAPS, P])
        dg_skip = sb("dg_skip", [P, CH, P])
        carry = sb("carry", [P, NB, CH, NS])
        halo = sb("halo", [P, NB, CH, HALO])

        x_t = sb("x_t", [P, 2, KT, T])
        x_tok = sb("x_tok", [P, TT, DM])
        x_in = sb("x_in", [P, CH, HALO + T])
        x_conv = sb("x_conv", [P, 2, CH, T])
        dt = sb("dt", [P, CH + 1, T])
        gate = sb("gate", [P, CH, T])
        poly = sb("poly", [P, 2, T])
        square = sb("square", [P, 2, T])
        rest = poly[:, 0]
        dt_low = poly[0:RANK, 1]
        parts = sb("parts", [P, T], BF16)
        y_gated = sb("y_gated", [P, CH, T])
        room = a_log[:].rearrange("p c s -> p (c s)")
        stats = room[:, 0:TT * 6].rearrange("p (t k) -> p t k", t=TT)
        mean_var = room[:, TT * 6:TT * 8].rearrange("p (t k) -> p t k", t=TT)
        spread = room[:, TT * 8:TT * 9]

        h = sb("h", [P, HS, T])
        hc = sb("hc", [P, HCS, T])
        b_rep = sb("b_rep", [P, NS, T])
        c_rep = sb("c_rep", [P, NS, T])

        y_ps = psum("y_ps", [P, 2, T])
        a_ps = psum("a_ps", [P, 3, T])
        work = psum("work", [P, 2, T])
        h_ps = psum("h_ps", [P, T])

        early_in = sem("early_in")
        small_in = sem("small_in")
        later_in = sem("later_in")
        x_t_in = [sem(f"x_t_in{q}") for q in range(2)]
        x_tok_in = sem("x_tok_in")
        x1_out = sem("x1_out")
        ident_ready = sem("ident_ready")
        pick_ready = sem("pick_ready")
        zeroed = sem("zeroed")
        shifts_ready = sem("shifts_ready")
        a_exp = sem("a_exp")
        a_inv_step = sem("a_inv_step")
        diags_ready = sem("diags_ready")
        filled = [sem(f"work_filled{q}") for q in range(2)]
        emptied = [sem(f"work_emptied{q}") for q in range(2)]
        halo_moved = sem("halo_moved")
        x_conv_ready = sem("x_conv_ready")
        gate_ready = sem("gate_ready")
        abs_done = sem("abs_done")
        exp_neg_ready = sem("exp_neg_ready")
        square_ready = sem("square_ready")
        softplus_step = sem("softplus_step")
        high_ready = sem("high_ready")
        split_step = sem("split_step")
        dt_ready = sem("dt_ready")
        u_ready = sem("u_ready")
        a_ready = sem("a_ready")
        b_ready = sem("b_ready")
        scanned = sem("scanned")
        summed = sem("summed")
        hc_vector = sem("hc_vector")
        hc_pool = sem("hc_pool")
        carried = sem("carried")
        gated = sem("gated")
        norm_step = sem("norm_step")
        std_ready = sem("std_ready")

        NP, NV = CH * len(POOL_HC), CH * (NS - len(POOL_HC))

        def on_pool(m):
            return m % NS in POOL_HC

        def pool_before(m):
            return sum(on_pool(k) for k in range(m))

        def vector_before(m):
            return m - pool_before(m)

        PARTS = {"x": 2, "o": 4, "c": 4, "dl": 4, "bc": 4}
        last_chunk = ITEMS - NS
        PLACE = [("x0", 0), ("x1", 2), ("x2", 4), ("x3", 6), ("o0", 8), ("o1", 12), ("c0", 16), ("c1", 20),
                 ("c2", 24), ("c3", 28), ("z3", 33), ("dl", 35), ("bc", 39), ("d0", 43), ("d1", 44), ("d2", 45), ("d3", 46)]
        LATE_C = [f"C{s}" for s in range(LATE_FROM, NS)]
        PLACE = sorted(PLACE + [(t, 1 + 2 * k) for k, t in enumerate(LATE_C)], key=lambda t: t[1])
        PLACE += sorted([("z0", 47), ("z1", 51), ("z2", 55)] +
                        [(f"B{s}", last_chunk + s) for s in range(NS)] +
                        [(f"C{s}", last_chunk + 3 + s) for s in range(LATE_FROM)], key=lambda t: t[1])
        WHERE = dict(PLACE)

        def parts_of(t):
            return PARTS.get(t if t in ("dl", "bc") else t[0], 1)

        class Plan:

            def __init__(self, kinds, offset, per=0):
                self.tiles = [t for t, _ in PLACE if t[0] in kinds or t in kinds]
                self.offset, self.per = offset, per

            def parts_at(self, m):
                return [(t, m - WHERE[t]) for t in self.tiles if 0 <= m - WHERE[t] < parts_of(t)]

            def whole_at(self, m):
                return [t for t in self.tiles if m - WHERE[t] == parts_of(t) - 1]

            def has(self, tile):
                return tile in self.tiles

            def bank(self, tile):
                return (self.offset + self.tiles.index(tile)) % 2

            def before(self, tile, unit):
                n = (self.offset + self.tiles.index(tile)) // 2
                return count(unit, self.per // 2, n) if self.per else n

        PREP = ["x", "c", "dl", "bc", "d", "B", "z0", "z1", "z2"] + [f"C{s}" for s in range(LATE_FROM)]
        OWN = ["z3", "o"] + LATE_C
        FIRST = len(Plan(PREP + LATE_C, 0).tiles)
        INNER = len(Plan(PREP + OWN, 0).tiles)
        AHEAD = FIRST - len(LATE_C) - 2
        first = Plan(PREP, 0)
        extra = Plan(LATE_C, len(first.tiles))
        second = Plan(PREP + ["z3"], FIRST)
        inner = Plan(PREP + OWN, AHEAD, INNER)
        last = Plan(OWN, AHEAD + INNER * (UNITS - 1))
        final = Plan(["o"], last.offset + len(last.tiles))
        assert INNER % 2 == 0

        def emptied_all(eng, plan, unit, tiles):
            most = {}
            for t in tiles:
                most[plan.bank(t)] = t
            for bank, t in most.items():
                eng.wait_ge(emptied[bank], plan.before(t, unit) + 1)

        def hc_wait(eng, unit, m):
            if on_pool(m):
                eng.wait_ge(hc_pool, count(unit, NP, pool_before(m) + 1))
            else:
                eng.wait_ge(hc_vector, count(unit, NV, vector_before(m) + 1))

        def carried_by(m):
            if on_pool(m):
                m += (-m) % 4
            return m + 1 if m % 4 == 0 else m

        def a_bank(m):
            return m % 3 if m < ITEMS - 1 else (m - 2) % 3

        def a_since(m):
            return next(n for n in range(1, 6) if a_bank((m - n) % ITEMS) == a_bank(m))

        def before(unit, m, n):
            return (unit, m - n) if m >= n else (later(unit, -1), m - n + ITEMS)

        def after(unit, m, n):
            return (unit, m + n) if m + n < ITEMS else (later(unit), m + n - ITEMS)

        def made_before(eng, unit, tile):
            if isinstance(unit[0], int) and unit[1] == 0:
                emptied_all(eng, extra if tile in LATE_C else first, (0, -1), [tile])
            elif tile not in LATE_C:
                emptied_all(eng, inner, later(unit, -1), [tile])
            else:
                emptied_all(eng, last if isinstance(unit[0], int) else inner, unit, [tile])

        def whole(eng, unit_program):
            unit_program((0, 0), second)
            with eng.Fori(0, (UNITS - 2) // 2) as j:
                unit_program((j, 1), inner)
                unit_program((j, 2), inner)
            unit_program((0, UNITS - 1), last)

        EARLY = ["w_in", "b_in"]
        SMALL = ["taps", "d_skip", "a_log", "b_conv", "b_dt"]
        LATER = ["w_x", "w_dt", "w_out", "b_out"]
        holders = dict(w_in=w_in, w_x=w_x, w_dt=w_dt, w_out=w_out, b_out=b_out, b_in=b_in, taps=taps,
                       b_conv=b_conv, d_skip=d_skip, b_dt=b_dt, a_log=a_log)
        ADD_RELU_AT = (54, 58, 63)
        def dt_of(parity, c):
            return dt[:, c if c < CH - 1 else c + parity]

        x_arg = x_in[:, :, HALO:]

        block = ctx.enter_context(nc.Block())

        @block.sync
        def _(sp):
            sp.dma_start(x_t[:, 0], d["x_t"][0]).then_inc(x_t_in[0], 16)
            for group, loaded in ((EARLY, early_in), (SMALL, small_in), (LATER, later_in)):
                for name in group:
                    sp.dma_start(holders[name][:], d[name]).then_inc(loaded, 16)
            sp.dma_start(x_tok[:], d["x_tok"][0]).then_inc(x_tok_in, 16)

            def unit_program(u, plan):
                nq = (u[1] + 1) % 2
                if plan is not last:
                    if plan is not second:
                        prev = later(u, -1)
                        sp.wait_ge(emptied[inner.bank("z3")], inner.before("z3", prev) + 1)
                    sp.dma_start(x_t[:, nq], d["x_t"][number(later(u))]).then_inc(x_t_in[nq], 16)
                if plan is not second:
                    sp.wait_ge(norm_step, count(u, NORM, 0))
                    sp.dma_start(d["x1"][number(later(u, -1))], x_tok[:]).then_inc(x1_out, 16)
                    sp.wait_ge(x1_out, count(u, 16, 0))
                    sp.dma_start(x_tok[:], d["x_tok"][number(u)]).then_inc(x_tok_in, 16)

            whole(sp, unit_program)
            sp.wait_ge(norm_step, NORM * UNITS)
            sp.dma_start(d["x1"][UNITS - 1], x_tok[:]).then_inc(x1_out, 16)
            sp.wait_ge(x1_out, 16 * UNITS)

        @block.gpsimd
        def _(pool):
            nc.gpsimd.memset(ident[:], 0.0).then_inc(zeroed, 1)
            nc.gpsimd.memset(pick[:], 0.0).then_inc(zeroed, 1)
            nc.gpsimd.memset(carry[:], 0.0).then_inc(zeroed, 1)
            nc.gpsimd.memset(halo[:], 0.0).then_inc(zeroed, 1)
            pool.wait_ge(zeroed, 4)
            nc.gpsimd.memset(ones, 1.0).then_inc(zeroed, 1)
            pool.wait_ge(zeroed, 5)
            for k, (shift, _) in enumerate(LOG1P):
                nc.gpsimd.memset(shifts[:, k:k + 1], shift).then_inc(shifts_ready, 1)
            nc.gpsimd.affine_select(out=ident[:], in_=ident[:], compare_op=ALU.not_equal, fill=1.0, base=0,
                                    pattern=[[-1, P]], channel_multiplier=1).then_inc(ident_ready, 1)
            for n, row in enumerate((0, 64, 96)):
                wait(pool, pick_ready, n)
                nc.gpsimd.affine_select(out=pick[:], in_=pick[:], compare_op=ALU.not_equal, fill=1.0, base=-row,
                                        pattern=[[-1, 2 * NS]], channel_multiplier=1).then_inc(pick_ready, 1)

            def make_u(u, m):
                c, s = divmod(m, NS)
                if m == 0:
                    pool.wait_ge(x_conv_ready, count(u, 2, 2))
                if c == 0:
                    made_before(pool, u, f"B{s}")
                if u[1] > 0 or m >= HS:
                    ou, om = before(u, m, HS)
                    if on_pool(om):
                        hc_wait(pool, ou, om)
                    else:
                        pool.wait_ge(scanned, count(ou, ITEMS, om + 1))
                    if on_pool(om):
                        pool.wait_ge(carried, count(ou, ITEMS, carried_by(om)))
                nc.gpsimd.tensor_tensor(h[:, m % HS], x_conv[:, u[1] % 2, c], b_rep[:, s], ALU.mult).then_inc(u_ready, 1)

            def make_hc(u, m):
                pool.wait_ge(scanned, count(u, ITEMS, m + 1))
                if m < NS:
                    made_before(pool, u, f"C{m}")
                wait(pool, summed, count(u, ITEMS, m - HCS + 1))
                nc.gpsimd.tensor_tensor(hc[:, m % HCS], h[:, m % HS], c_rep[:, m % NS], ALU.mult).then_inc(hc_pool, 1)

            def add_relu(u, c):
                n, nq = later(u), (u[1] + 1) % 2
                pool.wait_ge(softplus_step, count(n, LOGS, (c + 1) * FACTORS))
                nc.gpsimd.tensor_tensor(dt_of(nq, c), dt_of(nq, c), poly[:, c % 2], ALU.add).then_inc(dt_ready, 1)

            def unit_program(u, plan):
                for m in range(ITEMS):
                    nu, nm = after(u, m, LEAD)
                    if not (plan is last and m + LEAD >= ITEMS):
                        make_u(nu, nm)
                    pu, pm = before(u, m, 1)
                    if on_pool(pm) and not (plan is second and m == 0):
                        make_hc(pu, pm)
                    if plan is not last and m in ADD_RELU_AT:
                        add_relu(u, ADD_RELU_AT.index(m))
                    if plan is not second and m == 3:
                        add_relu(later(u, -1), CH - 1)

            for c in range(CH):
                add_relu((0, -1), c)
            for m in range(LEAD):
                make_u((0, 0), m)
            whole(pool, unit_program)
            if on_pool(ITEMS - 1):
                make_hc((0, UNITS - 1), ITEMS - 1)

        @block.scalar
        def _(act):
            act.wait_ge(early_in, 16 * len(EARLY))
            act.wait_ge(small_in, 16 * len(SMALL))
            nc.scalar.activation(a_mat[:], a_log[:], ACT.Exp).then_inc(a_exp, 1)

            def make_a(u, m):
                c, s = divmod(m, NS)
                if s == 0:
                    act.wait_ge(dt_ready, count(u, CH, c + 1))
                if u[1] > 0 or a_since(m) <= m:
                    ou, om = before(u, m, a_since(m))
                    act.wait_ge(scanned, count(ou, ITEMS, om + 1))
                nc.scalar.activation(a_ps[:, a_bank(m)], dt_of(u[1] % 2, c), ACT.Exp,
                                     scale=a_mat[:, c, s:s + 1]).then_inc(a_ready, 1)

            def tile(u, plan, t):
                n, nq = later(u), (u[1] + 1) % 2
                bank = plan.bank(t)
                kind = t[0]
                if t in ("dl", "bc"):
                    act.wait_ge(filled[bank], plan.before(t, u) + 1)
                    if t == "dl":
                        wait(act, dt_ready, count(n, CH, 0))
                        nc.scalar.activation(dt_low, work[0:RANK, bank], ACT.Copy).then_inc(emptied[bank], 1)
                    else:
                        nc.scalar.activation(parts[:], work[:, bank], ACT.Copy).then_inc(high_ready, 1)
                    return
                c = int(t[1:])
                if kind == "B":
                    act.wait_ge(filled[bank], plan.before(t, u) + 1)
                    wait(act, u_ready, count(n, ITEMS, c + 1 - NS))
                    nc.scalar.activation(b_rep[:, c], work[:, bank], ACT.Copy).then_inc(emptied[bank], 1)
                elif kind == "C":
                    act.wait_ge(filled[bank], plan.before(t, u) + 1)
                    if plan not in (first, extra):
                        hc_wait(act, later(u, -1) if t in LATE_C else u, last_chunk + c)
                    nc.scalar.activation(c_rep[:, c], work[:, bank], ACT.Copy).then_inc(emptied[bank], 1)
                elif kind == "x":
                    act.wait_ge(filled[bank], plan.before(t, u) + 1)
                    wait(act, softplus_step, count(n, LOGS, 0))
                    nc.scalar.activation(x_in[:, c, HALO:], work[:, bank], ACT.Identity,
                                         bias=b_in[:, c:c + 1]).then_inc(emptied[bank], 1)
                elif kind == "c":
                    act.wait_ge(filled[bank], plan.before(t, u) + 1)
                    if c == 0:
                        wait(act, u_ready, count(u, ITEMS, 0))
                    nc.scalar.activation(x_conv[:, nq, c], work[:, bank], ACT.Identity,
                                         bias=b_conv[:, c:c + 1]).then_inc(emptied[bank], 1)
                elif kind == "z":
                    act.wait_ge(filled[bank], plan.before(t, u) + 1)
                    wait(act, gated, count(u if c == CH - 1 else n, CH, c + 1 - CH))
                    nc.scalar.activation(gate[:, c], work[:, bank], ACT.Identity,
                                         bias=b_in[:, CH + c:CH + c + 1]).then_inc(emptied[bank], 1)
                elif kind == "d":
                    act.wait_ge(filled[bank], plan.before(t, u) + 1)
                    wait(act, a_ready, count(u, ITEMS, (c + 1) * NS if c < CH - 1 else 0))
                    if c == 0:
                        act.wait_ge(halo_moved, count(n, 2, 2))
                    nc.scalar.activation(x_arg[:, c], work[:, bank], ACT.Abs, bias=b_dt[:, c:c + 1]).then_inc(abs_done, 1)
                    nc.scalar.activation(dt_of(nq, c), work[:, bank], ACT.Relu,
                                         bias=b_dt[:, c:c + 1]).then_inc(emptied[bank], 1)

            def exp_neg(u, c):
                n = later(u)
                act.wait_ge(abs_done, count(n, CH, c + 1))
                nc.scalar.activation(x_arg[:, c], x_arg[:, c], ACT.Exp, scale=-1.0).then_inc(exp_neg_ready, 1)

            def squared(u, f):
                n = later(u)
                c, k = divmod(f, FACTORS)
                act.wait_ge(exp_neg_ready, count(n, CH, c + 1))
                wait(act, softplus_step, count(n, LOGS, f - 1))
                nc.scalar.activation(square[:, f % 2], x_arg[:, c], ACT.Square, scale=ROOT_SCALE,
                                     bias=shifts[:, k:k + 1]).then_inc(square_ready, 1)

            def root(pu):
                act.wait_ge(norm_step, count(pu, NORM, 11))
                nc.scalar.activation(spread, spread, ACT.Sqrt).then_inc(std_ready, 1)

            def weave(u, plan, m):
                n, nq = later(u), (u[1] + 1) % 2
                for t in plan.whole_at(m):
                    if t[0] != "o":
                        tile(u, plan, t)
                if plan.has("c0") and m in (26, 32):
                    half = (m - 26) // 6 * 2
                    emptied_all(act, plan, u, [f"c{c}" for c in (half, half + 1)])
                    two = x_conv[:, nq, half:half + 2]
                    nc.scalar.activation(two, two, ACT.Silu).then_inc(x_conv_ready, 1)
                if m == 18 and plan.has("o0"):
                    root(later(u, -1))
                if plan.has("d0"):
                    if 44 <= m < 44 + CH:
                        exp_neg(u, m - 44)
                    if 46 <= m < 46 + LOGS:
                        squared(u, m - 46)
                if m in (10, 40) and plan not in (first, extra):
                    two = 0 if m == 10 else 2
                    for c in (two, two + 1):
                        if c < CH - 1:
                            made_before(act, u, f"z{c}")
                        else:
                            emptied_all(act, plan, u, ["z3"])
                    nc.scalar.activation(gate[:, two:two + 2], gate[:, two:two + 2], ACT.Silu).then_inc(gate_ready, 1)

            def unit_program(u, plan):
                for m in range(ITEMS):
                    nu, nm = after(u, m, A_AHEAD)
                    if not (plan is last and m + A_AHEAD >= ITEMS):
                        make_a(nu, nm)
                    weave(u, plan, m)

            for m in range(ITEMS):
                weave((0, -1), first, m)
            for m in range(2 * len(LATE_C)):
                weave((0, -1), extra, m)
            act.wait_ge(a_inv_step, 5)
            for m in range(A_AHEAD):
                make_a((0, 0), m)
            whole(act, unit_program)
            root((0, UNITS - 1))

        @block.tensor
        def _(pe):
            pe.wait_ge(early_in, 16 * len(EARLY))

            def replicate(dst, row):
                return nc.tensor.matmul(dst, pick[:, row:row + 1].to_broadcast([P, P]), parts[:], start=True, stop=True)

            def add_item(u, m):
                c, s = divmod(m, NS)
                if s == 0:
                    wait(pe, gated, count(u, CH, c - 1))
                    if c == 0:
                        pe.wait_ge(x_conv_ready, count(u, 2, 2))
                    nc.tensor.matmul(y_ps[:, c % 2], dg_skip[:, c], x_conv[:, u[1] % 2, c], start=True, stop=False)
                hc_wait(pe, u, m)
                by = dg_inv[:, c, POOL_HC.index(s)] if on_pool(m) else ident[:]
                nc.tensor.matmul(y_ps[:, c % 2], by, hc[:, m % HCS], start=False,
                                 stop=(s == NS - 1)).then_inc(summed, 1)

            def tile(u, plan, t, part):
                n, q, nq = later(u), u[1] % 2, (u[1] + 1) % 2
                bank = plan.bank(t)
                if part == 0:
                    wait(pe, emptied[bank], plan.before(t, u))
                out = work[:, bank]
                if t[0] in "BC":
                    if t == "B0":
                        pe.wait_ge(split_step, count(n, 2, 2))
                    mm = replicate(out, int(t[1:]) + (NS if t[0] == "C" else 0))
                elif t[0] == "x":
                    if t == "x0" and part == 0:
                        pe.wait_ge(x_t_in[nq], loads(n))
                    m, k = int(t[1]), part
                    mm = nc.tensor.matmul(out, w_in[:, k, m * P:(m + 1) * P], x_t[:, nq, k], start=(k == 0), stop=(k == KT - 1))
                elif t[0] == "z":
                    m = int(t[1]) + CH
                    src = q if t == "z3" else nq
                    for k in range(KT):
                        mm = nc.tensor.matmul(out, w_in[:, k, m * P:(m + 1) * P], x_t[:, src, k], start=(k == 0), stop=(k == KT - 1))
                elif t[0] == "c":
                    c, k = int(t[1]), part
                    if plan is first and c == 0 and k == 0:
                        pe.wait_ge(diags_ready, 1)
                        pe.wait_ge(pick_ready, 3)
                        pe.wait_ge(later_in, 16 * len(LATER))
                    if k == 0:
                        pe.wait_ge(halo_moved, count(n, 2, 1))
                        emptied_all(pe, plan, u, [f"x{c}"])
                    mm = nc.tensor.matmul(out, dg_tap[:, c, k], x_in[:, c, k:k + T], start=(k == 0), stop=(k == TAPS - 1))
                elif t == "dl":
                    c = part
                    if c == 0:
                        pe.wait_ge(x_conv_ready, count(n, 2, 2))
                    mm = nc.tensor.matmul(work[0:RANK, bank], w_x[:, c, 0:RANK], x_conv[:, nq, c], start=(c == 0), stop=(c == CH - 1))
                elif t == "bc":
                    c = part
                    mm = nc.tensor.matmul(out, w_x[:, c, RANK:], x_conv[:, nq, c], start=(c == 0), stop=(c == CH - 1))
                elif t[0] == "d":
                    c = int(t[1])
                    emptied_all(pe, plan, u, ["dl"])
                    mm = nc.tensor.matmul(out, w_dt[:, c * P:(c + 1) * P], dt_low, start=True, stop=True)
                elif t[0] == "o":
                    if part == 0:
                        pe.wait_ge(gated, count(u, CH, 0))
                    tt, rest_of_it = divmod(part, 2)
                    tok = (2 * int(t[1]) + tt) * P
                    o = work[:, bank, tt * DM:(tt + 1) * DM]
                    if not rest_of_it:
                        nc.tensor.matmul(o, ones[:], b_out[:], start=True, stop=False)
                    for c in (range(1, CH) if rest_of_it else (0,)):
                        mm = nc.tensor.matmul(o, y_gated[:, c, tok:tok + P], w_out[:, c], start=False, stop=(c == CH - 1))
                if part == parts_of(t) - 1:
                    mm.then_inc(filled[bank], 1)

            def weave(u, plan, m):
                for t, part in plan.parts_at(m):
                    tile(u, plan, t, part)

            def unit_program(u, plan):
                for m in range(ITEMS):
                    pu, pm = before(u, m, LAG)
                    if not (plan is second and m < LAG):
                        add_item(pu, pm)
                    weave(u, plan, m)

            for m in range(ITEMS):
                weave((0, -1), first, m)
            for m in range(2 * len(LATE_C)):
                weave((0, -1), extra, m)
            pe.wait_ge(diags_ready, 2)
            whole(pe, unit_program)
            for m in range(ITEMS - LAG, ITEMS):
                add_item((0, UNITS - 1), m)
            for t in ("o0", "o1"):
                for part in range(parts_of(t)):
                    tile((0, UNITS), final, t, part)

        @block.vector
        def _(dve):
            dve.wait_ge(small_in, 16 * len(SMALL))
            dve.wait_ge(ident_ready, 1)
            for c in range(CH):
                for k in range(TAPS):
                    nc.vector.tensor_scalar(dg_tap[:, c, k], ident[:], taps[:, c, k:k + 1], None, ALU.mult)
                one = nc.vector.tensor_scalar(dg_skip[:, c], ident[:], d_skip[:, c:c + 1], None, ALU.mult)
            one.then_inc(diags_ready, 1)

            def invert_a():
                V = nc.vector
                dve.wait_ge(a_exp, 1)
                V.tensor_scalar(a_big[:], a_mat[:], 1e-6, None, ALU.is_ge).then_inc(a_inv_step, 1)
                dve.wait_ge(a_inv_step, 1)
                V.scalar_tensor_tensor(out=a_inv[:], in0=a_mat[:], scalar=-1.0, in1=a_big[:], op0=ALU.mult,
                                       op1=ALU.mult).then_inc(a_inv_step, 1)
                dve.wait_ge(a_inv_step, 2)
                V.scalar_tensor_tensor(out=a_inv[:], in0=a_inv[:], scalar=1.0, in1=a_big[:], op0=ALU.add,
                                       op1=ALU.subtract).then_inc(a_inv_step, 1)
                dve.wait_ge(a_inv_step, 3)
                V.reciprocal(a_inv[:], a_inv[:]).then_inc(a_inv_step, 1)
                dve.wait_ge(a_inv_step, 4)
                V.tensor_scalar(a_mat[:], a_mat[:], -1.0, None, ALU.mult).then_inc(a_inv_step, 1)
                for c in range(CH):
                    for n, s in enumerate(POOL_HC):
                        one = V.tensor_scalar(dg_inv[:, c, n], ident[:], a_inv[:, c, s:s + 1], None, ALU.mult)
                one.then_inc(diags_ready, 1)

            def h_of(m):
                return h[:, m % HS] if on_pool(m) else h_ps[:]

            def vector_item_before(u, m):
                n = next(n for n in range(1, NS) if not on_pool((m - n) % ITEMS))
                return before(u, m, n)

            def make_b(u, m):
                dve.wait_ge(a_ready, count(u, ITEMS, m + 1))
                dve.wait_ge(u_ready, count(u, ITEMS, m + 1))
                nc.vector.scalar_tensor_tensor(out=h[:, m % HS], in0=a_ps[:, a_bank(m)], scalar=1.0, in1=h[:, m % HS],
                                               op0=ALU.subtract, op1=ALU.mult).then_inc(b_ready, 1)

            def scan(u, m):
                c, s = divmod(m, NS)
                dve.wait_ge(b_ready, count(u, ITEMS, m + 1))
                if not on_pool(m) and (u[1] > 0 or m > 0):
                    pu, pm = vector_item_before(u, m)
                    dve.wait_ge(hc_vector, count(pu, NV, vector_before(pm) + 1))
                    dve.wait_ge(carried, count(pu, ITEMS, carried_by(pm)))
                nc.vector.tensor_tensor_scan(h_of(m), a_ps[:, a_bank(m)], h[:, m % HS],
                                             carry[:, batch(u), c, s:s + 1], ALU.mult, ALU.add).then_inc(scanned, 1)

            def save_carry(u, m):
                c, s = divmod(m, NS)
                dve.wait_ge(scanned, count(u, ITEMS, m + 1))
                nc.vector.tensor_scalar(carry[:, batch(u), c, s:s + 1], h_ps[:, T - 1:T], 1.0, None,
                                        ALU.mult).then_inc(carried, 1)

            def save_two(u, m):
                c, s = divmod(m - 2, NS)
                slot = (m - 2) % HS
                dve.wait_ge(scanned, count(u, ITEMS, m + 1))
                nc.vector.tensor_scalar(carry[:, batch(u), c, s:s + 3:2], h[:, slot:slot + 3:2, T - 1], 1.0, None,
                                        ALU.mult).then_inc(carried, 2)

            def make_hc(u, m):
                if m < NS:
                    made_before(dve, u, f"C{m}")
                dve.wait_ge(scanned, count(u, ITEMS, m + 1))
                wait(dve, summed, count(u, ITEMS, m - HCS + 1))
                c, s = divmod(m, NS)
                nc.vector.scalar_tensor_tensor(out=hc[:, m % HCS], in0=h_ps[:], scalar=a_inv[:, c, s:s + 1],
                                               in1=c_rep[:, s], op0=ALU.mult,
                                               op1=ALU.mult).then_inc(hc_vector, 1)

            def make_gated(u, c):
                dve.wait_ge(summed, count(u, ITEMS, (c + 1) * NS))
                dve.wait_ge(gate_ready, count(u, 2, c // 2 + 1))
                nc.vector.tensor_tensor(y_gated[:, c], y_ps[:, c % 2], gate[:, c], ALU.mult).then_inc(gated, 1)

            def halo_in(n):
                wait(dve, halo_moved, count(n, 2, 0))
                nc.vector.tensor_scalar(x_in[:, :, 0:HALO], halo[:, batch(n)], 1.0, None, ALU.mult).then_inc(halo_moved, 1)

            def halo_out(u, plan):
                emptied_all(dve, plan, u, [f"x{c}" for c in range(CH)])
                dve.wait_ge(halo_moved, count(later(u), 2, 1))
                nc.vector.tensor_scalar(halo[:, batch(later(u))], x_in[:, :, T:], 1.0, None, ALU.mult).then_inc(halo_moved, 1)

            def norm_so_far(pu, n):
                dve.wait_ge(norm_step, count(pu, NORM, n))

            def norm_sums(u, plan, t):
                k, bank, pu = int(t[1]), plan.bank(t), later(u, -1)
                if k == 0:
                    dve.wait_ge(x_tok_in, count(pu, 16, 16))
                dve.wait_ge(filled[bank], plan.before(t, u) + 1)
                two = x_tok[:, 2 * k:2 * k + 2]
                nc.vector.tensor_tensor(two, work[:, bank].rearrange("p (a b) -> p a b", a=2), two,
                                        ALU.add).then_inc(emptied[bank], 1)
                dve.wait_ge(emptied[bank], plan.before(t, u) + 1)
                for tt in (2 * k, 2 * k + 1):
                    nc.vector.bn_stats(stats[:, tt], x_tok[:, tt]).then_inc(norm_step, 1)
                norm_so_far(pu, 5 * k + 2)
                nc.vector.memset(spread[:, 2 * k:2 * k + 2], EPS).then_inc(norm_step, 1)
                for tt in (2 * k, 2 * k + 1):
                    nc.vector.bn_aggr(mean_var[:, tt], stats[:, tt]).then_inc(norm_step, 1)
                if k == 1:
                    norm_so_far(pu, 10)
                    nc.vector.tensor_tensor(spread, spread, mean_var[:, :, 1], ALU.add).then_inc(norm_step, 1)

            def normalise(pu):
                dve.wait_ge(std_ready, count(pu, 1, 1))
                nc.vector.reciprocal(spread, spread).then_inc(norm_step, 1)
                norm_so_far(pu, 12)
                for tt in range(TT):
                    row = x_tok[:, tt]
                    nc.vector.tensor_scalar(row, row, mean_var[:, tt, 0:1], spread[:, tt:tt + 1], ALU.subtract,
                                            ALU.mult).then_inc(norm_step, 1)

            def split(u, plan):
                n, nq, bank = later(u), (u[1] + 1) % 2, plan.bank("bc")
                dve.wait_ge(high_ready, count(n, 1, 1))
                wait(dve, dt_ready, count(n, CH, 0))
                nc.vector.tensor_tensor(rest[64:], work[64:, bank], parts[64:], ALU.subtract).then_inc(emptied[bank], 1)
                dve.wait_ge(emptied[bank], plan.before("bc", u) + 1)
                nc.vector.tensor_copy(parts[64:], rest[64:]).then_inc(split_step, 1)
                dve.wait_ge(split_step, count(n, 2, 1))
                nc.vector.tensor_tensor(parts[96:], rest[96:], parts[96:], ALU.subtract).then_inc(split_step, 1)

            def softplus(u, plan, f):
                n = later(u)
                c, k = divmod(f, FACTORS)
                dve.wait_ge(square_ready, count(n, LOGS, f + 1))
                if k == 0:
                    wait(dve, dt_ready, count(n, CH, c - 1))
                    if c == 0:
                        dve.wait_ge(split_step, count(n, 2, 2))
                    if c == 1:
                        emptied_all(dve, plan, u, ["d3"])
                else:
                    dve.wait_ge(softplus_step, count(n, LOGS, f))
                nc.vector.scalar_tensor_tensor(out=poly[:, c % 2], in0=square[:, f % 2], scalar=LOG1P[k][1],
                                               in1=x_arg[:, c] if k == 0 else poly[:, c % 2], op0=ALU.add,
                                               op1=ALU.mult).then_inc(softplus_step, 1)

            GATED_AT = {20: 0, 36: 1, 52: 2}

            def weave(u, plan, m):
                if plan.has("x0"):
                    if m == 5:
                        halo_in(later(u))
                    if m == 11:
                        halo_out(u, plan)
                    if m == 44:
                        split(u, plan)
                    if m >= ITEMS - LOGS:
                        softplus(u, plan, m - (ITEMS - LOGS))
                if m == 4 and plan in (inner, last):
                    make_gated(later(u, -1), CH - 1)
                if m in GATED_AT and plan is not first:
                    make_gated(u, GATED_AT[m])
                if plan.has("o0"):
                    if m in (12, 16):
                        norm_sums(u, plan, f"o{(m - 12) // 4}")
                    if m == 22:
                        normalise(later(u, -1))

            def unit_program(u, plan):
                for m in range(ITEMS):
                    scan(u, m)
                    if not on_pool(m):
                        if not (plan is last and m + 1 >= ITEMS):
                            make_b(*after(u, m, 1))
                        if m % 4 == 0 and not (plan is second and m == 0):
                            save_two(*before(u, m, 1))
                        save_carry(u, m)
                        make_hc(u, m)
                        if not (plan is last and m + 2 >= ITEMS):
                            make_b(*after(u, m, 2))
                    weave(u, plan, m)

            dve.wait_ge(zeroed, 5)
            for m in range(ITEMS):
                weave((0, -1), first, m)
                if m == 12:
                    invert_a()
            make_b((0, 0), 0)
            whole(dve, unit_program)
            save_two((0, UNITS - 1), ITEMS - 1)
            make_gated((0, UNITS - 1), CH - 1)
            for k in range(2):
                norm_sums((0, UNITS), final, f"o{k}")
            normalise((0, UNITS - 1))


GROUP = 4
ROWS = UNITS * T
TILES = ROWS // P
SLOT_TILES = 2 * TILES + NE
REGION = ROWS + P
SPARE = NE * REGION
SLOT_ROWS = SPARE + NE * P
BATCH = 4
BT = BATCH * TT
BATCHES = UNITS // BATCH
SHARED = NE


BEHIND = 2
OWNER_PART = SLOT_TILES // 3
BATCH_STEPS, CHOICE_STEPS = 23, 12
SLOTS_AT = BATCHES * BATCH_STEPS
PADS_AT, OWNER_AT, RESULTS_AT = SLOTS_AT + 2, SLOTS_AT + 26, SLOTS_AT + 36


def moe_layout(g, chunks):
    import numpy as np

    def stack(name):
        return np.concatenate([g[f"L0_ffn_experts_{name}"], g[f"L0_ffn_shared_{name}"][None]])

    up = np.concatenate([stack("wg"), stack("wu")], axis=2)
    return {
        "w_gate": chunks(g["L0_ffn_gate_w"]),
        "b_gate": g["L0_ffn_gate_b"][:, None],
        "w_up": up.reshape(NE + 1, KT, P, 2 * IF).transpose(2, 0, 1, 3),
        "w_down": stack("wd").transpose(1, 0, 2),
    }


def moe(nc, d):
    with ExitStack() as ctx:
        def sb(name, shape, dt=F32):
            return ctx.enter_context(nc.sbuf_tensor(name, shape, dt))

        def sem(name):
            return ctx.enter_context(nc.semaphore(name))

        w_gate = sb("w_gate", [P, KT, NE])
        b_gate = sb("b_gate", [NE, 1])
        w_up = sb("w_up", [P, NE + 1, KT, 2 * IF])
        w_down = sb("w_down", [P, NE + 1, DM])
        ident = sb("moe_ident", [P, P])
        tri = sb("tri", [P, P], BF16)
        full = sb("full", [P, P], BF16)
        precedence = sb("precedence", [P, NE])
        region = sb("region", [P, NE])
        lane = sb("lane", [P, 1])
        mask = sb("mask", [P, NE, BT])
        zeros = sb("zeros", [P, DM])
        steps = sb("steps", [P, TILES])
        slots_seq = sb("slots_seq", [1, SLOT_TILES])

        acc = sb("acc", [P, UNITS, TT, DM])
        x1_t = sb("x1_t", [P, UNITS, KT, T])

        logits_t = sb("logits_t", [NE, T])
        score = sb("score", [P, TILES, NE])
        rank = sb("rank", [P, TILES, NE])
        chosen = sb("chosen", [P, 2, TILES, NE])
        either = sb("either", [P, TILES, NE], BF16)
        best = sb("best", [P, 2, TILES])
        first_rank = sb("first_rank", [P, TILES])
        following = sb("following", [P, NE])
        pad_f = sb("pad_f", [P, NE])
        pad = sb("pad", [P, NE], U32)
        jump = sb("jump", [P, NE])
        used = sb("used", [P, NE])
        used_end = sb("used_end", [P, NE])
        owner = sb("owner", [1, BEHIND + SLOT_TILES], U32)
        owner_f = logits_t[0:1, 0:SLOT_TILES]
        row_f = logits_t[0:1, SLOT_TILES:2 * SLOT_TILES]
        row = sb("row", [1, SLOT_TILES + 2 * GROUP], U32)
        slot_f = sb("slot_f", [P, 2, TILES])
        slot = sb("slot", [P, 2, TILES], U32)
        result = sb("result", [P, 2, TILES], U32)
        mean_var = sb("moe_mean_var", [P, 2, TT, 2])
        stats = sb("moe_stats", [P, 2, TT, 6])
        spread = sb("moe_spread", [P, 2, TT])
        silu = chosen[:, 0].rearrange("p a b -> p (a b)").rearrange("p (a b) -> p a b", a=2)
        hidden = chosen[:, 1].rearrange("p a b -> p (a b)").rearrange("p (a b) -> p a b", a=2)

        def room(first, units):
            return x1_t[:, first:first + units].rearrange("p u k t -> p (u k t)")

        x_slots = room(0, 2).rearrange("p (g c f) -> p g c f", g=2, c=GROUP)
        y_slots = room(2, 2).rearrange("p (g c f) -> p g c f", g=2, c=GROUP)
        xt = room(4, 1).rearrange("p (a f) -> p a f", a=4)
        e_silu = room(5, 1).rearrange("p (a f) -> p a f", a=8)[:, 0:2]
        e_hidden = room(5, 1).rearrange("p (a f) -> p a f", a=8)[:, 2:4]
        e_hidden_t = room(5, 1).rearrange("p (a f) -> p a f", a=8)[:, 4:6]
        NG = 4
        gathered = room(6, 2 * NG).rearrange("p (n t r f) -> p n t r f", n=NG, t=TT, r=2)

        banks = ctx.enter_context(nc.psum_tensor("banks", [P, 8, T], F32))
        turn_ps = banks[:, 0:4].rearrange("p (a k) t -> p a k t", a=2)
        logits_ps = [banks[:, 4 + q, 0:BT * NE].rearrange("p (a e) -> p a e", a=BT) for q in range(2)]
        logits_t_ps = banks[0:NE, 6]
        within_ps = banks[:, 7, 0:BT * NE].rearrange("p (a e) -> p a e", a=BT)
        totals_ps = banks[:, 7, BT * NE:2 * BT * NE].rearrange("p (a e) -> p a e", a=BT)
        g_ps, u_ps = banks[:, 0:2], banks[:, 2:4]
        d_ps = banks[:, 4:6].rearrange("p a t -> p (a t)").rearrange("p (a f) -> p a f", a=TT)
        xt_ps = banks[:, 0:2]
        gu_ps = banks[:, 2:4]
        ht_ps = banks[:, 4:5]
        y_ps = banks[:, 5:7]

        router_in = sem("router_in")
        experts_in = sem("experts_in")
        x1_in = [sem(f"x1_in{q}") for q in range(4)]
        made = sem("moe_constants_made")
        turned = sem("turned")
        x1_t_act = sem("x1_t_act")
        x1_t_dve = sem("x1_t_dve")
        logits_t_made = sem("logits_t_made")
        logits_t_ready = sem("logits_t_ready")
        logits_ready = sem("logits_ready")
        score_ready = sem("score_ready")
        step = sem("route_step")
        following_ready = sem("following_ready")
        counted = sem("counted")
        up_ready = sem("up_ready")
        silu_ready = sem("silu_ready")
        hidden_ready = sem("hidden_ready")
        down_ready = sem("down_ready")
        blended = sem("blended")
        scattered = [sem(f"scattered{q}") for q in range(4)]
        padded = sem("padded")
        spare_zeroed = sem("spare_zeroed")
        x_slots_in = [sem(f"x_slots_in{q}") for q in range(2)]
        xt_made = sem("xt_made")
        xt_ready = sem("xt_ready")
        e_up = sem("e_up")
        e_silu_ready = sem("e_silu_ready")
        e_hidden_ready = sem("e_hidden_ready")
        ht_made = sem("ht_made")
        ht_ready = sem("ht_ready")
        y_made = sem("y_made")
        y_ready = sem("y_ready")
        y_stored = [sem(f"y_stored{q}") for q in range(2)]
        gathered_in = [sem(f"gathered_in{q}") for q in range(NG)]
        mixed = sem("mixed")
        norm = sem("moe_norm_step")
        std = sem("moe_std_ready")
        out_stored = sem("out_stored")

        MOE_NORM = 2 * TT + 3 + TT
        held = dict(w_gate=w_gate, b_gate=b_gate, w_up=w_up, w_down=w_down)

        BODY = 2 * GROUP
        BODIES = SLOT_TILES // BODY
        MADE = 13

        def tiles(eng, program):
            for c in range(BODY):
                program(0, c, c)
            with eng.Fori(1, BODIES - 1) as r:
                for c in range(BODY):
                    program(r, c, None)
            for c in range(BODY):
                program(BODIES - 1, c, (BODIES - 1) * BODY + c)

        def tile_no(r, c):
            return r * BODY + c

        block = ctx.enter_context(nc.Block())

        @block.sync
        def _(sp):
            for name in ("w_gate", "b_gate"):
                sp.dma_start(held[name][:], d[name]).then_inc(router_in, 16)
            for q in range(4):
                sp.dma_start(acc[:, q], d["x1"][q]).then_inc(x1_in[q], 16)
            for i in range(4, UNITS):
                sp.wait_ge(x1_in[i % 4], 16 * (i // 4))
                sp.dma_start(acc[:, i], d["x1"][i]).then_inc(x1_in[i % 4], 16)
            for name in ("w_up", "w_down"):
                sp.dma_start(held[name][:], d[name]).then_inc(experts_in, 16)

            sp.wait_ge(made, MADE)
            sp.dma_start(d["x_rows"][SPARE:].rearrange("(s p) f -> p s f", p=P),
                         zeros[:].unsqueeze(1).to_broadcast([P, NE, DM])).then_inc(spare_zeroed, 16)

            for q in range(4):
                sp.wait_ge(scattered[q], UNITS // 4 * 16 * 2 * TT)
            sp.wait_ge(hidden_ready, UNITS)

            sp.wait_ge(padded, 16 * NE)
            sp.wait_ge(spare_zeroed, 16)
            sp.wait_ge(step, OWNER_AT)
            row_regs = [sp.alloc_register(f"row{c}") for c in range(2 * BODY)]

            def rows_of(r):
                sp.load(row_regs, row[0:1, bass.ds(r * BODY, 2 * BODY)])
                return [sp.snap(reg, min_val=0, max_val=SLOT_ROWS - P) for reg in row_regs]

            def load(rows, g):
                for c in range(GROUP):
                    sp.dma_start(x_slots[:, g, c], d["x_rows"][bass.ds(rows[g * GROUP + c], P)]).then_inc(x_slots_in[g], 16)

            def store(r, g):
                sp.wait_ge(y_ready, r * BODY + (g + 1) * GROUP)
                sp.dma_start(d["y_slots"][:, bass.ds(r * BODY + g * GROUP, GROUP)], y_slots[:, g]).then_inc(y_stored[g], 16)

            def body(r, more, begin=False):
                rows = rows_of(r)
                if begin:
                    load(rows, 0)
                    load(rows, 1)
                for g in range(2):
                    if more:
                        sp.wait_ge(xt_made, r * BODY + (g + 1) * GROUP)
                        load(rows[BODY:], g)
                    store(r, g)

            body(0, True, True)
            with sp.Fori(1, BODIES - 1) as r:
                body(r, True)
            body(BODIES - 1, False)

            for i in range(UNITS):
                sp.wait_ge(norm, (i + 1) * MOE_NORM)
                sp.dma_start(d["out"][i], acc[:, i]).then_inc(out_stored, 16)
            sp.wait_ge(out_stored, 16 * UNITS)

        @block.gpsimd
        def _(pool):
            nc.gpsimd.memset(ident[:], 0.0).then_inc(made, 1)
            nc.gpsimd.memset(zeros[:], 0.0).then_inc(made, 1)
            nc.gpsimd.memset(mask[:], 1.0).then_inc(made, 1)
            nc.gpsimd.memset(tri[:], 0.0).then_inc(made, 1)
            nc.gpsimd.memset(full[:], 1.0).then_inc(made, 1)
            pool.wait_ge(made, 5)
            nc.gpsimd.memset(mask[:, :, 0:1], 0.0).then_inc(made, 1)
            nc.gpsimd.affine_select(out=ident[:], in_=ident[:], compare_op=ALU.not_equal, fill=1.0, base=0,
                                    pattern=[[-1, P]], channel_multiplier=1).then_inc(made, 1)
            nc.gpsimd.affine_select(out=tri[:], in_=tri[:], compare_op=ALU.is_ge, fill=1.0, base=0,
                                    pattern=[[-1, P]], channel_multiplier=1).then_inc(made, 1)
            nc.gpsimd.iota(precedence[:], pattern=[[-1, NE]], base=NE, channel_multiplier=0,
                           allow_small_or_imprecise_dtypes=True).then_inc(made, 1)
            nc.gpsimd.iota(region[:], pattern=[[REGION, NE]], base=0, channel_multiplier=0,
                           allow_small_or_imprecise_dtypes=True).then_inc(made, 1)
            nc.gpsimd.iota(lane[:], pattern=[[0, 1]], base=0, channel_multiplier=1,
                           allow_small_or_imprecise_dtypes=True).then_inc(made, 1)
            nc.gpsimd.iota(steps[:], pattern=[[P, TILES]], base=0, channel_multiplier=0,
                           allow_small_or_imprecise_dtypes=True).then_inc(made, 1)
            nc.gpsimd.iota(slots_seq[:], pattern=[[1, SLOT_TILES]], base=0, channel_multiplier=0,
                           allow_small_or_imprecise_dtypes=True).then_inc(made, 1)

            for t in range(TILES):
                i, tt = divmod(t, TT)
                if t % BT == 0:
                    pool.wait_ge(step, (t // BT + 1) * BATCH_STEPS)
                if tt == 0:
                    wait(pool, scattered[i % 4], 16 * 2 * TT * (i // 4))
                for r in range(2):
                    nc.gpsimd.indirect_dma_start(
                        d["x_rows"], bass.IndirectOffsetOnAxis(slot[:, r, t:t + 1], 0),
                        acc[:, i, tt], None).then_inc(scattered[i % 4], 16)

            pool.wait_ge(step, PADS_AT)
            for e in range(NE):
                nc.gpsimd.indirect_dma_start(d["x_rows"], bass.IndirectOffsetOnAxis(pad[:, e:e + 1], 0), zeros[:],
                                             None).then_inc(padded, 16)

            pool.wait_ge(step, RESULTS_AT)
            for q in range(2):
                pool.wait_ge(y_stored[q], 16 * BODIES)
            for t in range(TILES):
                i, tt = divmod(t, TT)
                if tt == 0 and i >= NG:
                    pool.wait_ge(mixed, (i - NG + 1) * 2 * TT)
                for r in range(2):
                    nc.gpsimd.indirect_dma_start(
                        gathered[:, i % NG, tt, r], None, d["y_rows"],
                        bass.IndirectOffsetOnAxis(result[:, r, t:t + 1], 0)).then_inc(gathered_in[i % NG], 16)

        @block.scalar
        def _(act):
            def add_bias(i):
                act.wait_ge(logits_t_made, i + 1)
                wait(act, logits_ready, i)
                nc.scalar.activation(logits_t[:], logits_t_ps, ACT.Identity, bias=b_gate[:, 0:1]).then_inc(logits_t_ready, 1)

            act.wait_ge(router_in, 32)
            for i in range(UNITS + 2):
                if i < UNITS:
                    act.wait_ge(turned, i + 1)
                    nc.scalar.copy(x1_t[:, i, 0], turn_ps[:, i % 2, 0]).then_inc(x1_t_act, 1)
                if 1 <= i <= UNITS:
                    add_bias(i - 1)
                if i >= 5 and (i - 5) % BATCH == 0:
                    b = (i - 5) // BATCH
                    act.wait_ge(logits_ready, (b + 1) * BATCH)
                    nc.scalar.activation(score[:, b * BT:(b + 1) * BT], logits_ps[b % 2], ACT.Sigmoid).then_inc(score_ready, 1)
            for i in range(UNITS):
                act.wait_ge(up_ready, i + 1)
                act.wait_ge(step, SLOTS_AT)
                wait(act, hidden_ready, i - 1)
                nc.scalar.activation(silu[:, i % 2], g_ps[:, i % 2], ACT.Silu).then_inc(silu_ready, 1)

            def hidden_t(r, c, k):
                act.wait_ge(ht_made, tile_no(r, c) + 1)
                if k is None or k >= 2:
                    act.wait_ge(y_made, tile_no(r, c) - 1)
                nc.scalar.copy(e_hidden_t[:, c % 2], ht_ps[:, 0, 0:P]).then_inc(ht_ready, 1)

            def program(r, c, k):
                if k is None or k >= 2:
                    hidden_t(r, c - 2, None if k is None else k - 2)
                act.wait_ge(e_up, tile_no(r, c) + 1)
                if k is None or k >= 2:
                    act.wait_ge(e_hidden_ready, tile_no(r, c) - 1)
                nc.scalar.activation(e_silu[:, c % 2], gu_ps[:, c % 2, 0:IF], ACT.Silu).then_inc(e_silu_ready, 1)

            tiles(act, program)
            for k in (SLOT_TILES - 2, SLOT_TILES - 1):
                hidden_t(BODIES - 1, k - (BODIES - 1) * BODY, k)

            for i in range(UNITS):
                act.wait_ge(norm, i * MOE_NORM + 2 * TT + 2)
                nc.scalar.activation(spread[:, i % 2], spread[:, i % 2], ACT.Sqrt).then_inc(std, 1)

        @block.tensor
        def _(pe):
            pe.wait_ge(made, MADE)
            pe.wait_ge(router_in, 32)

            def turn(i):
                pe.wait_ge(x1_in[i % 4], 16 * (i // 4 + 1))
                wait(pe, x1_t_act, i - 1)
                wait(pe, x1_t_dve, i - 1)
                for k in range(KT):
                    for tt in range(TT):
                        one = nc.tensor.transpose(turn_ps[:, i % 2, k, tt * P:(tt + 1) * P],
                                                  acc[:, i, tt, k * P:(k + 1) * P], ident[:])
                one.then_inc(turned, 1)

            def logits(i):
                pe.wait_ge(x1_t_act, i + 1)
                pe.wait_ge(x1_t_dve, i + 1)
                wait(pe, logits_t_ready, i)
                for k in range(KT):
                    one = nc.tensor.matmul(logits_t_ps, w_gate[:, k], x1_t[:, i, k], start=(k == 0), stop=(k == KT - 1))
                one.then_inc(logits_t_made, 1)

            def turn_logits(i):
                pe.wait_ge(logits_t_ready, i + 1)
                b, at = divmod(i, BATCH)
                if at == 0:
                    wait(pe, score_ready, b - 1)
                for tt in range(TT):
                    one = nc.tensor.transpose(logits_ps[b % 2][:, at * TT + tt], logits_t[:, tt * P:(tt + 1) * P], ident[0:NE, 0:NE])
                one.then_inc(logits_ready, 1)

            def prefix(b):
                pe.wait_ge(step, b * BATCH_STEPS + CHOICE_STEPS)
                these = either[:, b * BT:(b + 1) * BT]
                nc.tensor.matmul(within_ps, tri[:], these, start=True, stop=True)
                nc.tensor.matmul(totals_ps, full[:], these, start=True, stop=True).then_inc(counted, 1)

            for i in range(UNITS + 3):
                if i < UNITS:
                    turn(i)
                if 1 <= i <= UNITS:
                    logits(i - 1)
                if 2 <= i < UNITS + 2:
                    turn_logits(i - 2)
                if i >= 6 and (i - 6) % BATCH == 0:
                    prefix((i - 6) // BATCH)

            pe.wait_ge(step, SLOTS_AT)
            pe.wait_ge(experts_in, 32)

            def down(i):
                pe.wait_ge(hidden_ready, i + 1)
                wait(pe, blended, i)
                for tt in range(TT):
                    one = nc.tensor.matmul(d_ps[:, tt], hidden[:, i % 2, tt * P:(tt + 1) * P], w_down[:, SHARED], start=True, stop=True)
                one.then_inc(down_ready, 1)

            for i in range(UNITS):
                wait(pe, hidden_ready, i - 1)
                for o, at in ((g_ps, 0), (u_ps, IF)):
                    for k in range(KT):
                        one = nc.tensor.matmul(o[:, i % 2], w_up[:, SHARED, k, at:at + IF], x1_t[:, i, k], start=(k == 0), stop=(k == KT - 1))
                one.then_inc(up_ready, 1)
                if i > 0:
                    down(i - 1)
            down(UNITS - 1)

            pe.wait_ge(step, OWNER_AT)
            pe.wait_ge(hidden_ready, UNITS)
            pe.wait_ge(blended, UNITS)

            def turn_slots(r, c, k):
                group = c // GROUP
                if c % GROUP == 0:
                    pe.wait_ge(x_slots_in[group], (r + 1) * (16 * GROUP))
                if k is None or k >= 2:
                    pe.wait_ge(xt_ready, tile_no(r, c) - 1)
                for h in range(KT):
                    one = nc.tensor.transpose(xt_ps[:, c % 2, h * P:(h + 1) * P],
                                              x_slots[:, group, c % GROUP, h * P:(h + 1) * P], ident[:])
                one.then_inc(xt_made, 1)

            def up_slots(r, c, k, e):
                pe.wait_ge(xt_ready, tile_no(r, c) + 1)
                if k is None or k >= 2:
                    pe.wait_ge(e_hidden_ready, tile_no(r, c) - 1)
                for h in range(KT):
                    one = nc.tensor.matmul(gu_ps[:, c % 2, 0:2 * IF], xt[:, c % 4, h * P:(h + 1) * P], w_up[:, e, h], start=(h == 0), stop=(h == KT - 1))
                one.then_inc(e_up, 1)

            def turn_hidden(r, c, k):
                pe.wait_ge(e_hidden_ready, tile_no(r, c) + 1)
                if k is None or k >= 1:
                    pe.wait_ge(ht_ready, tile_no(r, c))
                nc.tensor.transpose(ht_ps[:, 0, 0:P], e_hidden[:, c % 2], ident[:]).then_inc(ht_made, 1)

            def down_slots(r, c, k, e):
                pe.wait_ge(ht_ready, tile_no(r, c) + 1)
                if k is None or k >= 2:
                    pe.wait_ge(y_ready, tile_no(r, c) - 1)
                nc.tensor.matmul(y_ps[:, c % 2, 0:DM], e_hidden_t[:, c % 2], w_down[:, e], start=True, stop=True).then_inc(y_made, 1)

            owner_regs = [pe.alloc_register(f"owner{c}") for c in range(BEHIND + BODY)]

            def load_owners(r):
                pe.load(owner_regs, owner[0:1, bass.ds(r * BODY, BEHIND + BODY)])
                return {c - BEHIND: pe.snap(reg, min_val=0, max_val=NE - 1) for c, reg in enumerate(owner_regs)}

            def body(r, k0):
                owners = load_owners(r)
                for c in range(BODY):
                    k = None if k0 is None else k0 + c
                    old = None if k0 is None else k - 2
                    if old is None or old >= 0:
                        turn_hidden(r, c - 2, old)
                    if k is None or k + 1 < SLOT_TILES:
                        if c + 1 < BODY:
                            turn_slots(r, c + 1, None if k is None else k + 1)
                        else:
                            turn_slots(r + 1, 0, None if k is None else k + 1)
                    up_slots(r, c, k, owners[c])
                    if old is None or old >= 0:
                        down_slots(r, c - 2, old, owners[c - 2])
                return owners

            turn_slots(0, 0, 0)
            body(0, 0)
            with pe.Fori(1, BODIES - 1) as r:
                body(r, None)
            owners = body(BODIES - 1, (BODIES - 1) * BODY)
            for k in (SLOT_TILES - 2, SLOT_TILES - 1):
                c = k - (BODIES - 1) * BODY
                turn_hidden(BODIES - 1, c, k)
                down_slots(BODIES - 1, c, k, owners[c])

        @block.vector
        def _(dve):
            AX = mybir.AxisListType.X
            V = nc.vector
            dve.wait_ge(made, MADE)
            done_steps = [0]

            def done(one):
                one.then_inc(step, 1)
                done_steps[0] += 1
                dve.wait_ge(step, done_steps[0])

            def over_experts(v, n):
                return v.unsqueeze(2).to_broadcast([P, n, NE])

            def over_tiles(v, n):
                return v.unsqueeze(1).to_broadcast([P, n, NE])

            def choose(b):
                at = slice(b * BT, (b + 1) * BT)
                dve.wait_ge(score_ready, b + 1)
                for r in range(2):
                    done(V.tensor_reduce(best[:, r, at], score[:, at], AX, ALU.max))
                    done(V.tensor_tensor(rank[:, at], score[:, at], over_experts(best[:, r, at], BT), ALU.is_equal))
                    done(V.tensor_tensor(rank[:, at], rank[:, at], over_tiles(precedence[:], BT), ALU.mult))
                    done(V.tensor_reduce(first_rank[:, at], rank[:, at], AX, ALU.max))
                    done(V.tensor_tensor(chosen[:, r, at], rank[:, at], over_experts(first_rank[:, at], BT), ALU.is_equal))
                    if r == 0:
                        done(V.scalar_tensor_tensor(out=score[:, at], in0=chosen[:, 0, at], scalar=-2.0,
                                                    in1=score[:, at], op0=ALU.mult, op1=ALU.add))
                done(V.tensor_tensor(either[:, at], chosen[:, 0, at], chosen[:, 1, at], ALU.add))
                assert done_steps[0] == b * BATCH_STEPS + CHOICE_STEPS

            def find_slots(b):
                at = slice(b * BT, (b + 1) * BT)
                flat = score[:, at].rearrange("p a b -> p (a b)")
                cand = rank[:, at]
                dve.wait_ge(counted, b + 1)
                done(V.tensor_copy(flat.rearrange("p (e t) -> p e t", e=NE), totals_ps.rearrange("p t e -> p e t")))
                done(V.tensor_tensor_scan(flat, mask[:].rearrange("p a b -> p (a b)"), flat, 0.0, ALU.mult, ALU.add))
                done(V.tensor_tensor(cand, flat.rearrange("p (e t) -> p t e", e=NE), totals_ps, ALU.subtract))
                done(V.tensor_tensor(cand, cand, within_ps, ALU.add))
                done(V.tensor_tensor(cand, cand, over_tiles(following[:], BT), ALU.add))
                for r in range(2):
                    done(V.tensor_tensor(chosen[:, r, at], chosen[:, r, at], cand, ALU.mult))
                    done(V.tensor_reduce(slot_f[:, r, at], chosen[:, r, at], AX, ALU.add))
                done(V.tensor_tensor(following[:], following[:], flat.rearrange("p (e t) -> p e t", e=NE)[:, :, BT - 1], ALU.add))
                done(V.tensor_copy(slot[:, :, at], slot_f[:, :, at]))
                assert done_steps[0] == (b + 1) * BATCH_STEPS

            V.tensor_copy(following[:], region[:]).then_inc(following_ready, 1)
            dve.wait_ge(following_ready, 1)
            for i in range(UNITS + 3):
                if i < UNITS:
                    dve.wait_ge(turned, i + 1)
                    V.tensor_copy(x1_t[:, i, 1], turn_ps[:, i % 2, 1]).then_inc(x1_t_dve, 1)
                if i >= 5 and (i - 5) % BATCH == 0:
                    choose((i - 5) // BATCH)
                if i >= 6 and (i - 6) % BATCH == 0:
                    find_slots((i - 6) // BATCH)
            assert done_steps[0] == SLOTS_AT

            room_f = rank[:].rearrange("p a b -> p (a b)")
            table = room_f.rearrange("p (e t) -> p e t", e=NE)
            runs = rank[0:1, 0:OWNER_PART]

            def count_tiles():
                done(V.tensor_scalar(pad_f[:], following[:], lane[:], None, ALU.add))
                done(V.tensor_copy(pad[:], pad_f[:]))
                assert done_steps[0] == PADS_AT
                done(V.tensor_tensor(used[:], following[:], region[:], ALU.subtract))
                done(V.tensor_tensor(table, used[:].unsqueeze(2).to_broadcast([P, NE, TILES]),
                                     steps[:].unsqueeze(1).to_broadcast([P, NE, TILES]), ALU.is_gt))
                done(V.tensor_reduce(used[:], table, AX, ALU.add))
                done(V.memset(used_end[:], 1.0))
                done(V.tensor_tensor_scan(used_end[:], used_end[:], used[:], 0.0, ALU.mult, ALU.add))
                done(V.tensor_scalar(jump[:], used[:], -float(P), float(REGION), ALU.mult, ALU.add))

            def find_owners(part):
                at = slice(part * OWNER_PART, (part + 1) * OWNER_PART)
                done(V.tensor_tensor(runs, used_end[0:1].unsqueeze(1).to_broadcast([1, OWNER_PART, NE]),
                                     slots_seq[:, at].unsqueeze(2).to_broadcast([1, OWNER_PART, NE]), ALU.is_le))
                done(V.tensor_reduce(owner_f[:, at], runs, AX, ALU.add))
                done(V.tensor_tensor(runs, runs, jump[0:1].unsqueeze(1).to_broadcast([1, OWNER_PART, NE]), ALU.mult))
                done(V.tensor_reduce(row_f[:, at], runs, AX, ALU.add))

            def list_tiles():
                done(V.tensor_scalar(owner_f, owner_f, float(NE - 1), None, ALU.min))
                done(V.tensor_copy(owner[:, BEHIND:], owner_f))
                done(V.memset(owner[:, 0:BEHIND], 0))
                done(V.scalar_tensor_tensor(out=row_f, in0=slots_seq[:], scalar=float(P), in1=row_f,
                                            op0=ALU.mult, op1=ALU.add))
                done(V.tensor_copy(row[:, 0:SLOT_TILES], row_f))
                assert done_steps[0] + 1 == OWNER_AT, done_steps
                done(V.memset(row[:, SLOT_TILES:], 0))

            def find_results(r):
                done(V.scalar_tensor_tensor(out=rank[:], in0=over_experts(slot_f[:, r], TILES), scalar=float(REGION),
                                            in1=over_tiles(region[:], TILES), op0=ALU.subtract, op1=ALU.is_ge))
                done(V.tensor_tensor(rank[:], rank[:], over_tiles(jump[:], TILES), ALU.mult))
                done(V.tensor_reduce(first_rank[:], rank[:], AX, ALU.add))
                done(V.tensor_tensor(slot_f[:, r], slot_f[:, r], first_rank[:], ALU.subtract))
                done(V.tensor_copy(result[:, r], slot_f[:, r]))

            def find_shares():
                assert done_steps[0] == RESULTS_AT
                done(V.tensor_tensor(first_rank[:], best[:, 0], best[:, 1], ALU.add))
                done(V.reciprocal(first_rank[:], first_rank[:]))
                for r in range(2):
                    done(V.tensor_tensor(best[:, r], best[:, r], first_rank[:], ALU.mult))

            def blend_shared(i):
                dve.wait_ge(down_ready, i + 1)
                dve.wait_ge(scattered[i % 4], 16 * 2 * TT * (i // 4 + 1))
                V.scalar_tensor_tensor(out=acc[:, i], in0=acc[:, i], scalar=2.0, in1=d_ps, op0=ALU.mult,
                                       op1=ALU.add).then_inc(blended, 1)

            for i in range(UNITS):
                dve.wait_ge(silu_ready, i + 1)
                dve.wait_ge(up_ready, i + 1)
                wait(dve, down_ready, i - 1)
                V.tensor_tensor(hidden[:, i % 2], silu[:, i % 2], u_ps[:, i % 2], ALU.mult).then_inc(hidden_ready, 1)
                if i == 0:
                    count_tiles()
                elif i <= 3:
                    find_owners(i - 1)
                elif i == 4:
                    list_tiles()
                elif i <= 6:
                    find_results(i - 5)
                elif i == 7:
                    find_shares()
                if i > 0:
                    blend_shared(i - 1)
            blend_shared(UNITS - 1)

            def take_turned(r, c, k):
                dve.wait_ge(xt_made, tile_no(r, c) + 1)
                if k is None or k >= 4:
                    dve.wait_ge(e_up, tile_no(r, c) - 3)
                V.tensor_copy(xt[:, c % 4], xt_ps[:, c % 2, 0:DM]).then_inc(xt_ready, 1)

            def gate_hidden(r, c, k):
                dve.wait_ge(e_silu_ready, tile_no(r, c) + 1)
                if k is None or k >= 2:
                    dve.wait_ge(ht_made, tile_no(r, c) - 1)
                V.tensor_tensor(e_hidden[:, c % 2], e_silu[:, c % 2], gu_ps[:, c % 2, IF:2 * IF], ALU.mult).then_inc(e_hidden_ready, 1)

            def take_y(r, c, k):
                group = c // GROUP if c >= 0 else 1
                dve.wait_ge(y_made, tile_no(r, c) + 1)
                if c % GROUP == 0 and (k is None or k >= BODY):
                    dve.wait_ge(y_stored[group], (r if c >= 0 else r - 1) * 16)
                V.tensor_copy(y_slots[:, group, c % GROUP], y_ps[:, c % 2, 0:DM]).then_inc(y_ready, 1)

            def program(r, c, k):
                if k is None or k + 1 < SLOT_TILES:
                    if c + 1 < BODY:
                        take_turned(r, c + 1, None if k is None else k + 1)
                    else:
                        take_turned(r + 1, 0, None if k is None else k + 1)
                gate_hidden(r, c, k)
                if k is None or k >= 2:
                    take_y(r, c - 2, None if k is None else k - 2)

            take_turned(0, 0, 0)
            tiles(dve, program)
            for k in (SLOT_TILES - 2, SLOT_TILES - 1):
                take_y(BODIES - 1, k - (BODIES - 1) * BODY, k)

            def stage5(i):
                q = i % 2
                at = i * MOE_NORM
                dve.wait_ge(gathered_in[i % NG], 16 * 2 * TT * (i // NG + 1))
                for r in range(2):
                    wait(dve, mixed, i * 2 * TT + r * TT)
                    for tt in range(TT):
                        V.scalar_tensor_tensor(out=acc[:, i, tt], in0=gathered[:, i % NG, tt, r],
                                               scalar=best[:, r, i * TT + tt:i * TT + tt + 1], in1=acc[:, i, tt],
                                               op0=ALU.mult, op1=ALU.add).then_inc(mixed, 1)
                dve.wait_ge(mixed, (i + 1) * 2 * TT)
                for tt in range(TT):
                    V.bn_stats(stats[:, q, tt], acc[:, i, tt]).then_inc(norm, 1)
                dve.wait_ge(norm, at + TT)
                V.memset(spread[:, q], EPS).then_inc(norm, 1)
                for tt in range(TT):
                    V.bn_aggr(mean_var[:, q, tt], stats[:, q, tt]).then_inc(norm, 1)
                dve.wait_ge(norm, at + 2 * TT + 1)
                V.tensor_tensor(spread[:, q], spread[:, q], mean_var[:, q, :, 1], ALU.add).then_inc(norm, 1)
                dve.wait_ge(std, i + 1)
                V.reciprocal(spread[:, q], spread[:, q]).then_inc(norm, 1)
                dve.wait_ge(norm, at + 2 * TT + 3)
                for tt in range(TT):
                    row = acc[:, i, tt]
                    V.tensor_scalar(row, row, mean_var[:, q, tt, 0:1], spread[:, q, tt:tt + 1], ALU.subtract,
                                    ALU.mult).then_inc(norm, 1)

            for i in range(UNITS):
                stage5(i)


def kernel(**inputs):
    import numpy as np
    import concourse.bacc as bacc
    from concourse.bass_utils import run_bass_kernel_spmd

    g = {k: np.asarray(v) for k, v in inputs.items()}

    def chunks(v):
        v = v.reshape((v.shape[0] // P, P) + v.shape[1:])
        return v.swapaxes(0, 1)

    x = g["L0_attn_x"].reshape(NB, NW, T, DM).swapaxes(0, 1).reshape(UNITS, T, DM)
    x_proj = g["L0_attn_x_proj_w"].T
    laid = {
        "x_t": x.transpose(0, 2, 1).reshape(UNITS, KT, P, T).swapaxes(1, 2),
        "x_tok": x.reshape(UNITS, TT, P, DM).swapaxes(1, 2),
        "w_in": chunks(g["L0_attn_in_proj_w"].T),
        "b_in": chunks(g["L0_attn_in_proj_b"]),
        "taps": chunks(g["L0_attn_conv_w"]),
        "b_conv": chunks(g["L0_attn_conv_b"]),
        "a_log": chunks(g["L0_attn_A_log"].T),
        "d_skip": chunks(g["L0_attn_D"]),
        "w_x": chunks(np.concatenate([x_proj[:, :RANK]] + [x_proj[:, RANK:]] * 4, axis=1)),
        "w_dt": g["L0_attn_dt_proj_w"].T,
        "b_dt": chunks(g["L0_attn_dt_proj_b"]),
        "w_out": chunks(g["L0_attn_out_proj_w"].T),
        "b_out": g["L0_attn_out_proj_b"][None],
    }
    laid.update(moe_layout(g, chunks))
    laid = {k: np.ascontiguousarray(v) for k, v in laid.items()}

    nc = bacc.Bacc("TRN2", target_bir_lowering=False, num_devices=1)
    d = {k: nc.dram_tensor(f"in_{k}", v.shape, mybir.dt.from_np(v.dtype), kind="ExternalInput").ap()
         for k, v in laid.items()}
    d["out"] = nc.dram_tensor("out", (UNITS, P, TT, DM), F32, kind="ExternalOutput").ap()
    d["x1"] = nc.dram_tensor("x1", (UNITS, P, TT, DM), F32, kind="Internal").ap()
    d["x_rows"] = nc.dram_tensor("x_rows", (SLOT_ROWS, DM), F32, kind="Internal").ap()
    d["y_rows"] = nc.dram_tensor("y_rows", (SLOT_TILES * P, DM), F32, kind="Internal").ap()
    d["y_slots"] = d["y_rows"].rearrange("(s p) f -> p s f", p=P)
    mamba(nc, d)
    moe(nc, d)
    r = run_bass_kernel_spmd(nc, [{f"in_{k}": v for k, v in laid.items()}], core_ids=[0])
    out = np.asarray(r.results[0]["out"])
    return out.swapaxes(1, 2).reshape(NW, NB, T, DM).swapaxes(0, 1).reshape(NB, L, DM)
```
